# Optimizing a Trainium2 kernel written in Bass

```python
import numpy as np
import jax
import jax.numpy as jnp

def _softmax(x, axis=-1):
    return jax.nn.softmax(x, axis=axis)

def _gelu(x):
    return jax.nn.gelu(x, approximate=True)

def _silu(x):
    return jax.nn.silu(x)

def _sigmoid(x):
    return jax.nn.sigmoid(x)

def _layernorm(x, axis=-1, eps=1e-05):
    m = jnp.mean(x, axis=axis, keepdims=True)
    v = jnp.var(x, axis=axis, keepdims=True)
    return (x - m) / jnp.sqrt(v + eps)

def _scatter_add(tgt, idx, src, axis=0):
    return tgt.at[idx].add(src)

def _segment_sum(src, seg, n):
    return jax.ops.segment_sum(src, seg, n)
kernel_name = 'mk_xattn_ffn_d2_seqx_r4_572acf'

def setup_inputs(seed: int=0):
    np.random.seed(seed)
    _w = jnp.asarray

    def _rec_inputs():
        import jax
        import jax.numpy as jnp
        _rk = jax.random.key(seed)
        x = -0.0002928 + 1 * jax.random.normal(jax.random.fold_in(_rk, 1), (4, 512, 256), jnp.float32)
        _lenS = 512 - jax.random.randint(jax.random.fold_in(_rk, 7), (4,), 0, max(1, 512 // 4) + 1, jnp.int32)
        _lenS2 = 512 - jax.random.randint(jax.random.fold_in(_rk, 8), (4,), 0, max(1, 512 // 4) + 1, jnp.int32)
        _ctx_1024P = jax.random.normal(jax.random.fold_in(_rk, 11), (4, 16, 256), jnp.float32)
        _ctx_1024c = jax.random.dirichlet(jax.random.fold_in(_rk, 511), 0.3 * jnp.ones((16,), jnp.float32), (4, 512))
        _ctx_1024t = jnp.einsum('bsk,bkd->bsd', _ctx_1024c, _ctx_1024P)
        _ctx_1024t = _ctx_1024t * jax.lax.rsqrt(jnp.mean(jnp.square(_ctx_1024t)) + 1e-12) * 0.953939
        ctx_1024 = -1.39393e-06 + 0.999914 * (_ctx_1024t + 0.3 * jax.random.normal(jax.random.fold_in(_rk, 611), (4, 512, 256), jnp.float32))
        _validS = jnp.arange(512)[None, :] < _lenS[:, None]
        _validS2 = jnp.arange(512)[None, :] < _lenS2[:, None]
        _causal = jnp.tril(jnp.ones((512, 512), dtype=bool))
        mask_1x1xSxS2_ik0 = jnp.where(jnp.broadcast_to(_validS2[0:1, None, None, :], (1, 1, 512, 512)), 0, 1).astype(jnp.int32)
        return (x, ctx_1024, mask_1x1xSxS2_ik0)
    x, ctx_1024, mask_1x1xSxS2_ik0 = _rec_inputs()

    def _L0_xattn_setup():
        import jax, jax.numpy as jnp
        import numpy as np
        import math
        D_MODEL = 256
        NUM_HEADS = 16
        MAX_LEN = 512
        D_HEAD = D_MODEL // NUM_HEADS
        BATCH = 2
        SEQ = 512

        def _skew(QEr):
            B, H, R, C = QEr.shape
            padded = jnp.pad(QEr, ((0, 0), (0, 0), (0, 0), (1, 0)))
            reshaped = padded.reshape(B, H, C + 1, R)
            return reshaped[:, :, 1:, :]
        root = jax.random.key(seed)
        ks = jax.random.split(root, 10)
        s = 1.0 / math.sqrt(D_MODEL)
        return {'query': jax.random.normal(ks[0], (BATCH, SEQ, D_MODEL), jnp.float32), 'key': jax.random.normal(ks[1], (BATCH, SEQ, D_MODEL), jnp.float32), 'value': jax.random.normal(ks[2], (BATCH, SEQ, D_MODEL), jnp.float32), 'Wq': jax.random.normal(ks[3], (D_MODEL, D_MODEL), jnp.float32) * s, 'bq': jax.random.normal(ks[4], (D_MODEL,), jnp.float32) * s, 'Wk': jax.random.normal(ks[5], (D_MODEL, D_MODEL), jnp.float32) * s, 'bk': jax.random.normal(ks[6], (D_MODEL,), jnp.float32) * s, 'Wv': jax.random.normal(ks[7], (D_MODEL, D_MODEL), jnp.float32) * s, 'bv': jax.random.normal(ks[8], (D_MODEL,), jnp.float32) * s, 'Er': jax.random.normal(ks[9], (MAX_LEN, D_HEAD), jnp.float32)}
    _L0_xattn_all = _L0_xattn_setup()
    _L0_xattn_in = {k: v for k, v in _L0_xattn_all.items() if k in ('Wq', 'bq', 'Wk', 'bk', 'Wv', 'bv', 'Er')}
    del _L0_xattn_all

    def _L0_ffn_setup():
        import jax, jax.numpy as jnp
        import numpy as np
        TOP_K = 2
        key = jax.random.key(seed)
        ks = jax.random.split(key, 6)
        B, T, H, E, F = (2, 512, 256, 8, 1024)
        s = 0.02
        return {'hidden_states': jax.random.normal(ks[0], (B, T, H), dtype=jnp.float32), 'router_w': jax.random.normal(ks[1], (E, H), dtype=jnp.float32) * s, 'w1': jax.random.normal(ks[2], (E, F, H), dtype=jnp.float32) * s, 'b1': jax.random.normal(ks[3], (E, F), dtype=jnp.float32) * s, 'w2': jax.random.normal(ks[4], (E, H, F), dtype=jnp.float32) * s, 'b2': jax.random.normal(ks[5], (E, H), dtype=jnp.float32) * s}
    _L0_ffn_all = _L0_ffn_setup()
    _L0_ffn_in = {k: v for k, v in _L0_ffn_all.items() if k in ('router_w', 'w1', 'b1', 'w2', 'b2')}
    del _L0_ffn_all

    def _L1_xattn_setup():
        import jax, jax.numpy as jnp
        import numpy as np
        NUM_HEAD = 16
        DIM_MODEL = 256
        D_K = DIM_MODEL // NUM_HEAD
        NEG = -1000000000.0
        key = jax.random.key(seed)
        ks = jax.random.split(key, 8)
        B, S, D = (2, 512, DIM_MODEL)
        q = jax.random.normal(ks[0], (B, S, D), dtype=jnp.float32)
        k = jax.random.normal(ks[1], (B, S, D), dtype=jnp.float32)
        v = jax.random.normal(ks[2], (B, S, D), dtype=jnp.float32)
        mask = jnp.tril(jnp.ones((S, S), dtype=jnp.int32))[None, None]
        scale = 1.0 / np.sqrt(D)
        w_q = jax.random.normal(ks[3], (D, D), dtype=jnp.float32) * scale
        w_k = jax.random.normal(ks[4], (D, D), dtype=jnp.float32) * scale
        w_v = jax.random.normal(ks[5], (D, D), dtype=jnp.float32) * scale
        w_o = jax.random.normal(ks[6], (D, D), dtype=jnp.float32) * scale
        return {'q': q, 'k': k, 'v': v, 'mask': mask, 'w_q': w_q, 'w_k': w_k, 'w_v': w_v, 'w_o': w_o}
    _L1_xattn_all = _L1_xattn_setup()
    _L1_xattn_in = {k: v for k, v in _L1_xattn_all.items() if k in ('w_q', 'w_k', 'w_v', 'w_o')}
    del _L1_xattn_all

    def _L1_ffn_setup():
        import jax, jax.numpy as jnp
        import numpy as np
        HIDDEN = 256
        INNER = 1024

        def _weight_quant(w):
            scale = 1.0 / jnp.clip(jnp.mean(jnp.abs(w)), 1e-05)
            wq = jnp.clip(jnp.round(w * scale), -1.0, 1.0) / scale
            return w + jax.lax.stop_gradient(wq - w)

        def _act_quant(x):
            scale = 127.0 / jnp.clip(jnp.max(jnp.abs(x), axis=-1, keepdims=True), 1e-05)
            xq = jnp.clip(jnp.round(x * scale), -128.0, 127.0) / scale
            return x + jax.lax.stop_gradient(xq - x)

        def _bitlinear(x, w):
            return jnp.einsum('bsi,oi->bso', _act_quant(x), _weight_quant(w))
        key = jax.random.key(seed)
        k0, k1, k2, k3 = jax.random.split(key, 4)
        x = jax.random.normal(k0, (4, 512, HIDDEN), dtype=jnp.float32)
        w_gate = jax.random.normal(k1, (INNER, HIDDEN), dtype=jnp.float32) / np.sqrt(HIDDEN)
        w_up = jax.random.normal(k2, (INNER, HIDDEN), dtype=jnp.float32) / np.sqrt(HIDDEN)
        w_down = jax.random.normal(k3, (HIDDEN, INNER), dtype=jnp.float32) / np.sqrt(INNER)
        return {'x': x, 'w_gate': w_gate, 'w_up': w_up, 'w_down': w_down}
    _L1_ffn_all = _L1_ffn_setup()
    _L1_ffn_in = {k: v for k, v in _L1_ffn_all.items() if k in ('w_gate', 'w_up', 'w_down')}
    del _L1_ffn_all
    return {'x': x, 'ctx_1024': ctx_1024, 'mask_1x1xSxS2_ik0': mask_1x1xSxS2_ik0, 'L0_xattn_Wq': _L0_xattn_in['Wq'], 'L0_xattn_bq': _L0_xattn_in['bq'], 'L0_xattn_Wk': _L0_xattn_in['Wk'], 'L0_xattn_bk': _L0_xattn_in['bk'], 'L0_xattn_Wv': _L0_xattn_in['Wv'], 'L0_xattn_bv': _L0_xattn_in['bv'], 'L0_xattn_Er': _L0_xattn_in['Er'], 'L0_ffn_router_w': _L0_ffn_in['router_w'], 'L0_ffn_w1': _L0_ffn_in['w1'], 'L0_ffn_b1': _L0_ffn_in['b1'], 'L0_ffn_w2': _L0_ffn_in['w2'], 'L0_ffn_b2': _L0_ffn_in['b2'], 'L1_xattn_w_q': _L1_xattn_in['w_q'], 'L1_xattn_w_k': _L1_xattn_in['w_k'], 'L1_xattn_w_v': _L1_xattn_in['w_v'], 'L1_xattn_w_o': _L1_xattn_in['w_o'], 'L1_ffn_w_gate': _L1_ffn_in['w_gate'], 'L1_ffn_w_up': _L1_ffn_in['w_up'], 'L1_ffn_w_down': _L1_ffn_in['w_down']}

def reference(x, ctx_1024, mask_1x1xSxS2_ik0, L0_xattn_Wq, L0_xattn_bq, L0_xattn_Wk, L0_xattn_bk, L0_xattn_Wv, L0_xattn_bv, L0_xattn_Er, L0_ffn_router_w, L0_ffn_w1, L0_ffn_b1, L0_ffn_w2, L0_ffn_b2, L1_xattn_w_q, L1_xattn_w_k, L1_xattn_w_v, L1_xattn_w_o, L1_ffn_w_gate, L1_ffn_w_up, L1_ffn_w_down):
    import jax
    import jax.numpy as jnp

    def _L0_xattn_ref(query, key, value, Wq, bq, Wk, bk, Wv, bv, Er):
        import jax, jax.numpy as jnp
        import numpy as np
        import math
        D_MODEL = 256
        NUM_HEADS = 16
        MAX_LEN = 512
        D_HEAD = D_MODEL // NUM_HEADS
        BATCH = 2
        SEQ = 512

        def _skew(QEr):
            B, H, R, C = QEr.shape
            padded = jnp.pad(QEr, ((0, 0), (0, 0), (0, 0), (1, 0)))
            reshaped = padded.reshape(B, H, C + 1, R)
            return reshaped[:, :, 1:, :]
        B, S, D = query.shape
        H, dh = (NUM_HEADS, D_HEAD)
        q = (jnp.einsum('bsd,ed->bse', query, Wq) + bq).reshape(B, S, H, dh).transpose(0, 2, 1, 3)
        k = (jnp.einsum('bsd,ed->bse', key, Wk) + bk).reshape(B, S, H, dh).transpose(0, 2, 1, 3)
        v = (jnp.einsum('bsd,ed->bse', value, Wv) + bv).reshape(B, S, H, dh).transpose(0, 2, 1, 3)
        start = MAX_LEN - S
        Er_s = Er[start:, :]
        QEr = jnp.einsum('bhsd,ld->bhsl', q, Er_s)
        Srel = _skew(QEr)
        QK = jnp.einsum('bhsd,bhtd->bhst', q, k)
        attn = (QK + Srel) / math.sqrt(dh)
        causal = jnp.tril(jnp.ones((S, S), dtype=bool))
        attn = jnp.where(causal[None, None], attn, -jnp.inf)
        attn = jax.nn.softmax(attn, axis=-1)
        out = jnp.einsum('bhst,bhtd->bhsd', attn, v)
        out = out.transpose(0, 2, 1, 3).reshape(B, S, D)
        return out

    def _L0_ffn_ref(hidden_states, router_w, w1, b1, w2, b2):
        import jax, jax.numpy as jnp
        import numpy as np
        TOP_K = 2
        x = hidden_states
        router_logits = jnp.einsum('bth,eh->bte', x, router_w)
        topk_values, topk_indices = jax.lax.top_k(router_logits, TOP_K)
        topk_weights = jax.nn.softmax(topk_values.astype(jnp.float32), axis=-1).astype(x.dtype)
        h1 = jnp.einsum('bth,efh->btef', x, w1) + b1
        h1 = jax.nn.gelu(h1, approximate=False)
        expert_outputs = jnp.einsum('btef,ehf->bteh', h1, w2) + b2
        gather_idx = topk_indices[..., None]
        topk_expert_outputs = jnp.take_along_axis(expert_outputs, gather_idx, axis=2)
        mixed_output = jnp.sum(topk_expert_outputs * topk_weights[..., None], axis=2)
        return mixed_output

    def _L1_xattn_ref(q, k, v, mask, w_q, w_k, w_v, w_o):
        import jax, jax.numpy as jnp
        import numpy as np
        NUM_HEAD = 16
        DIM_MODEL = 256
        D_K = DIM_MODEL // NUM_HEAD
        NEG = -1000000000.0
        B, S, D = q.shape
        H, dk = (NUM_HEAD, D_K)

        def proj(x, w):
            return (x @ w.T).reshape(B, -1, H, dk).transpose(0, 2, 1, 3)
        Q, K, V = (proj(q, w_q), proj(k, w_k), proj(v, w_v))
        scores = jnp.einsum('bhqd,bhkd->bhqk', Q, K) / jnp.sqrt(jnp.float32(dk))
        scores = jnp.where(mask == 0, NEG, scores)
        attn = jax.nn.softmax(scores, axis=-1)
        out = jnp.einsum('bhqk,bhkd->bhqd', attn, V)
        out = out.transpose(0, 2, 1, 3).reshape(B, S, D)
        return out @ w_o.T

    def _L1_ffn_ref(x, w_gate, w_up, w_down):
        import jax, jax.numpy as jnp
        import numpy as np
        HIDDEN = 256
        INNER = 1024

        def _weight_quant(w):
            scale = 1.0 / jnp.clip(jnp.mean(jnp.abs(w)), 1e-05)
            wq = jnp.clip(jnp.round(w * scale), -1.0, 1.0) / scale
            return w + jax.lax.stop_gradient(wq - w)

        def _act_quant(x):
            scale = 127.0 / jnp.clip(jnp.max(jnp.abs(x), axis=-1, keepdims=True), 1e-05)
            xq = jnp.clip(jnp.round(x * scale), -128.0, 127.0) / scale
            return x + jax.lax.stop_gradient(xq - x)

        def _bitlinear(x, w):
            return jnp.einsum('bsi,oi->bso', _act_quant(x), _weight_quant(w))
        gate = jax.nn.silu(_bitlinear(x, w_gate))
        up = _bitlinear(x, w_up)
        return _bitlinear(gate * up, w_down)
    x = x + _L0_xattn_ref(_layernorm(x, axis=-1), ctx_1024, ctx_1024, L0_xattn_Wq, L0_xattn_bq, L0_xattn_Wk, L0_xattn_bk, L0_xattn_Wv, L0_xattn_bv, L0_xattn_Er)
    x = x + _L0_ffn_ref(_layernorm(x, axis=-1), L0_ffn_router_w, L0_ffn_w1, L0_ffn_b1, L0_ffn_w2, L0_ffn_b2)
    x = x + _L1_xattn_ref(_layernorm(x, axis=-1), ctx_1024, ctx_1024, mask_1x1xSxS2_ik0, L1_xattn_w_q, L1_xattn_w_k, L1_xattn_w_v, L1_xattn_w_o)
    x = x + _L1_ffn_ref(_layernorm(x, axis=-1), L1_ffn_w_gate, L1_ffn_w_up, L1_ffn_w_down)
    return x

_drawn_inputs = setup_inputs


def setup_inputs(seed=0):
    import zlib

    import numpy as np

    out = dict(_drawn_inputs(seed))
    spreads = {}
    factors = {'L0_xattn_bq': 3.402, 'L0_xattn_bk': 8.0, 'L0_ffn_b1': 8.0, 'L0_ffn_b2': 4.711}
    for name, (base, spread) in spreads.items():
        noise = np.random.default_rng([zlib.crc32(name.encode()), seed]).standard_normal(out[name].shape)
        drawn = base * np.exp(spread * noise) if base else spread * noise
        out[name] = jnp.asarray(drawn.astype(out[name].dtype))
    for name, factor in factors.items():
        out[name] = (out[name] * factor).astype(out[name].dtype)
    return out
```

```python
from contextlib import ExitStack

import concourse.bass as bass
from concourse import mybir

ALU = mybir.AluOpType
ACT = mybir.ActivationFunctionType
AX = mybir.AxisListType
F32 = mybir.dt.float32
BF16 = mybir.dt.bfloat16
I32 = mybir.dt.int32
U32 = mybir.dt.uint32

P = 128
B, S, D = 4, 512, 256
TOK = B * S
TT = TOK // P
DK = D // P
HEADS, DH = 16, 16
NBH = B * HEADS
NI = S // P
E, F, TOPK = 8, 1024, 2
FB = F // P
NEG = -1.0e30
LN_EPS = 1e-5
MAGIC = 1.5 * 2.0 ** 23
PIECES = 6
KP = PIECES * DH
RING = 4
PADW = P

CAUSAL_UNITS = [[(3, 0, 512)], [(2, 0, 384), (0, 384, 128)], [(1, 0, 256)]]
FULL_UNITS = [[(i, 0, S)] for i in range(NI)]


def wait(eng, sem, value):
    if isinstance(value, int) and value <= 0:
        return
    eng.wait_ge(sem, value)


def build(nc, a, out):
    top = ExitStack()

    def dram(name, shape, dt):
        return nc.dram_tensor(name, shape, dt)

    q_pieces = dram("q_pieces", (3, B, D, S), BF16)
    k_pieces = dram("k_pieces", (4, B, D, S), BF16)
    rel = [[dram(f"rel_{r}_{i}", (P, P * (i + 1) + PADW), F32) for i in range(NI)] for r in range(RING)]

    with top:
        def sem(name):
            return top.enter_context(nc.semaphore(name))

        def sb(ctx, name, shape, dt=F32):
            return ctx.enter_context(nc.sbuf_tensor(name, shape, dt))

        def banks(ctx, name, n, dt=F32):
            return [ctx.enter_context(nc.psum_tensor(f"{name}{i}", [P, 512], dt)) for i in range(n)]

        x = sb(top, "x", [P, TT, D])
        xn = sb(top, "xn", [P, TT, D])
        xnT = sb(top, "xnT", [P, DK, TOK])
        ident = sb(top, "ident", [P, P])
        s_const = sem("s_const")
        s_ctx = sem("s_ctx")

        def layer_norm(tag, load_x=False):
            with ExitStack() as ctx:
                stats = sb(ctx, f"stats{tag}", [P, TT, 6])
                mv = sb(ctx, f"mv{tag}", [P, TT, 2])
                ve = sb(ctx, f"ve{tag}", [P, TT])
                sd = sb(ctx, f"sd{tag}", [P, TT])
                rs = sb(ctx, f"rs{tag}", [P, TT])
                t1 = sb(ctx, f"t1{tag}", [P, TT])
                t2 = sb(ctx, f"t2{tag}", [P, TT])
                ps = banks(ctx, f"lnps{tag}", 4)
                s_stat, s_var, s_sd, s_rs = (sem(f"s_{n}{tag}") for n in ("stat", "var", "sd", "rs"))
                s_xn, s_tr, s_ev = (sem(f"s_{n}{tag}") for n in ("xn", "tr", "ev"))
                block = ctx.enter_context(nc.Block())

                @block.vector
                def _(dve):
                    if load_x:
                        dve.wait_ge(s_const, 32)
                    for t in range(TT):
                        nc.vector.bn_stats(stats[:, t, :], x[:, t, :]).then_inc(s_stat, 1)
                    for t in range(TT):
                        dve.wait_ge(s_stat, t + 1)
                        agg = nc.vector.bn_aggr(mv[:, t, :], stats[:, t, :])
                    agg.then_inc(s_var, 1)
                    dve.wait_ge(s_var, 1)
                    nc.vector.tensor_scalar(ve[:, :], mv[:, :, 1], LN_EPS, None, ALU.add).then_inc(s_var, 1)
                    dve.wait_ge(s_sd, 1)
                    nc.vector.reciprocal(rs[:, :], sd[:, :]).then_inc(s_rs, 1)
                    dve.wait_ge(s_rs, 1)
                    nc.vector.tensor_tensor(t1[:, :], rs[:, :], rs[:, :], ALU.mult).then_inc(s_rs, 1)
                    dve.wait_ge(s_rs, 2)
                    nc.vector.tensor_tensor(t2[:, :], t1[:, :], ve[:, :], ALU.mult).then_inc(s_rs, 1)
                    dve.wait_ge(s_rs, 3)
                    nc.vector.tensor_scalar(t1[:, :], t2[:, :], -0.5, 1.5, ALU.mult, ALU.add).then_inc(s_rs, 1)
                    dve.wait_ge(s_rs, 4)
                    nc.vector.tensor_tensor(sd[:, :], t1[:, :], rs[:, :], ALU.mult).then_inc(s_rs, 1)
                    dve.wait_ge(s_rs, 5)
                    for t in range(TT):
                        nc.vector.tensor_scalar(xn[:, t, :], x[:, t, :], mv[:, t, 0:1], sd[:, t:t + 1],
                                                ALU.subtract, ALU.mult).then_inc(s_xn, 1)

                @block.scalar
                def _(act):
                    act.wait_ge(s_var, 2)
                    nc.scalar.activation(sd[:, :], ve[:, :], ACT.Sqrt).then_inc(s_sd, 1)
                    for u in range(B * DK):
                        c, dk = divmod(u, DK)
                        act.wait_ge(s_tr, u + 1)
                        nc.scalar.copy(xnT[:, dk, c * S:(c + 1) * S], ps[u % 4][:, :]).then_inc(s_ev, 1)

                @block.tensor
                def _(pe):
                    if load_x:
                        pe.wait_ge(s_const, 32)
                    for u in range(B * DK):
                        c, dk = divmod(u, DK)
                        pe.wait_ge(s_xn, NI * (c + 1))
                        wait(pe, s_ev, u - 3)
                        for j in range(NI):
                            tr = nc.tensor.transpose(ps[u % 4][:, j * P:(j + 1) * P],
                                                     xn[:, c * NI + j, dk * P:(dk + 1) * P], ident[:, :])
                        tr.then_inc(s_tr, 1)

        def project(tag, w_q, w_k, w_v, b_q, b_k, b_v, V, ctxT):
            with ExitStack() as ctx:
                w = sb(ctx, f"wqkv{tag}", [P, 3, DK, D])
                bqk = sb(ctx, f"bqk{tag}", [P, 2, DK])
                bvb = sb(ctx, f"bvb{tag}", [P, D])
                full = sb(ctx, f"full{tag}", [P, 2, S])
                rest = sb(ctx, f"rest{tag}", [P, 2, S])
                pieces = sb(ctx, f"pieces{tag}", [P, 2, 3, S], BF16)
                ps = banks(ctx, f"prps{tag}", 4)
                pv = banks(ctx, f"pvps{tag}", 4)
                s_w, s_mm, s_full, s_r1, s_p2, s_p3 = (sem(f"s_{n}{tag}") for n in ("w", "mm", "full", "r1", "p2", "p3"))
                s_vmm, s_vev = sem(f"s_vmm{tag}"), sem(f"s_vev{tag}")
                s_out = [sem(f"s_pout{tag}{i}") for i in range(2)]
                units = [(1, c, eh) for c in range(B) for eh in range(DK)] + [(0, c, eh) for c in range(B) for eh in range(DK)]
                per_use = [0, 0]
                done_after = []
                for g, (qk, c, eh) in enumerate(units):
                    per_use[g % 2] += 16 * (1 + qk)
                    done_after.append(per_use[g % 2])
                loads = 3 + (b_q is not None) * 3
                block = ctx.enter_context(nc.Block())

                @block.sync
                def _(sp):
                    for n, src in enumerate((w_q, w_k, w_v)):
                        sp.dma_start(w[:, n, :, :], src.rearrange("(k p) e -> p k e", p=P)).then_inc(s_w, 16)
                    if b_q is not None:
                        sp.dma_start(bqk[:, 0, :], b_q).then_inc(s_w, 16)
                        sp.dma_start(bqk[:, 1, :], b_k).then_inc(s_w, 16)
                        sp.dma_start(bvb[:, :], bass.AP(b_v.tensor, 0, [[0, P], [1, D]])).then_inc(s_w, 16)
                    for g, (qk, c, eh) in enumerate(units):
                        dst = (q_pieces, k_pieces)[qk]
                        sp.wait_ge(s_p3, g + 1)
                        to = dst[0:3, c, eh * P:(eh + 1) * P, :].rearrange("a e s -> e a s")
                        sp.dma_start(to, pieces[:, g % 2, :, :]).then_inc(s_out[g % 2], 16)
                        if qk:
                            sp.dma_start(dst[3, c, eh * P:(eh + 1) * P, :], pieces[:, g % 2, 0, :]).then_inc(s_out[g % 2], 16)
                    for i in range(2):
                        sp.wait_ge(s_out[i], per_use[i])

                @block.tensor
                def _(pe):
                    pe.wait_ge(s_w, 16 * loads)
                    pe.wait_ge(s_ctx, 16)

                    def v_tile(t):
                        wait(pe, s_vev, t - 3)
                        for dk in range(DK):
                            mm = nc.tensor.matmul(pv[t % 4][:, 0:D], ctxT[:, dk, t * P:(t + 1) * P], w[:, 2, dk, :],
                                                  start=(dk == 0), stop=(dk == DK - 1))
                        mm.then_inc(s_vmm, 1)

                    for g, (qk, c, eh) in enumerate(units):
                        src = ctxT if qk else xnT
                        wait(pe, s_full, g - 3)
                        for dk in range(DK):
                            mm = nc.tensor.matmul(ps[g % 4][:, :], w[:, qk, dk, eh * P:(eh + 1) * P],
                                                  src[:, dk, c * S:(c + 1) * S], start=(dk == 0), stop=(dk == DK - 1))
                        mm.then_inc(s_mm, 1)
                        v_tile(g)

                @block.scalar
                def _(act):
                    act.wait_ge(s_w, 16 * loads)
                    for g, (qk, c, eh) in enumerate(units):
                        act.wait_ge(s_mm, g + 1)
                        wait(act, s_p3, g - 1)
                        if g >= 2:
                            act.wait_ge(s_out[g % 2], done_after[g - 2])
                        if b_q is not None:
                            bias = bqk[:, qk, eh:eh + 1]
                            nc.scalar.activation(full[:, g % 2, :], ps[g % 4][:, :], ACT.Identity, bias=bias)
                            nc.scalar.activation(pieces[:, g % 2, 0, :], ps[g % 4][:, :], ACT.Identity,
                                                 bias=bias).then_inc(s_full, 1)
                        else:
                            nc.scalar.copy(full[:, g % 2, :], ps[g % 4][:, :])
                            nc.scalar.copy(pieces[:, g % 2, 0, :], ps[g % 4][:, :]).then_inc(s_full, 1)

                @block.vector
                def _(dve):
                    dve.wait_ge(s_w, 16 * loads)
                    for g in range(len(units)):
                        k = g % 2
                        dve.wait_ge(s_full, g + 1)
                        nc.vector.tensor_tensor(rest[:, k, :], full[:, k, :], pieces[:, k, 0, :], ALU.subtract).then_inc(s_r1, 1)
                        dve.wait_ge(s_vmm, g + 1)
                        b, j = divmod(g, NI)
                        to = V[:, b * HEADS:(b + 1) * HEADS, j, :]
                        src = pv[g % 4][:, 0:D].rearrange("p (h d) -> p h d", d=DH)
                        if b_v is not None:
                            nc.vector.tensor_tensor(to, src, bvb[:, :].rearrange("p (h d) -> p h d", d=DH), ALU.add).then_inc(s_vev, 1)
                        else:
                            nc.vector.tensor_copy(to, src).then_inc(s_vev, 1)
                        dve.wait_ge(s_r1, g + 1)
                        nc.vector.tensor_copy(pieces[:, k, 1, :], rest[:, k, :]).then_inc(s_p2, 1)
                        dve.wait_ge(s_p2, g + 1)
                        nc.vector.tensor_tensor(pieces[:, k, 2, :], rest[:, k, :], pieces[:, k, 1, :], ALU.subtract).then_inc(s_p3, 1)

        def attention(tag, causal, V, attn, bias_sb, ErP):
            units = CAUSAL_UNITS if causal else FULL_UNITS
            NU = len(units)
            WU = [u[-1][1] + u[-1][2] for u in units]
            place = {i: (512 * u + off, w) for u, unit in enumerate(units) for i, off, w in unit}
            act_units = () if causal else (2, 3)
            dve_units = tuple(u for u in range(NU) if u not in act_units)
            LOAD, REL, READ, SCORE, SOFT = 5, 4, 3, 2, 2
            with ExitStack() as ctx:
                q = [sb(ctx, f"q{tag}{r}", [KP, S], BF16) for r in range(RING)]
                k = [sb(ctx, f"k{tag}{r}", [KP, S], BF16) for r in range(RING)]
                if causal:
                    stage = [sb(ctx, f"stage{r}", [P, 512 * NU]) for r in range(RING)]
                    bias = [sb(ctx, f"bias{r}", [P, 512 * NU]) for r in range(RING)]
                else:
                    bias = [bias_sb] * RING
                scores = [sb(ctx, f"scores{tag}{r}", [P, 512 * NU]) for r in range(RING)]
                PT = [sb(ctx, f"PT{tag}{r}", [P, 512 * NU]) for r in range(2)]
                mx = sb(ctx, f"mx{tag}", [P, RING, NI])
                nm = sb(ctx, f"nm{tag}", [P, RING, NI])
                sums = sb(ctx, f"sums{tag}", [P, RING, NI])
                rinv = sb(ctx, f"rinv{tag}", [P, RING, NI])
                psE = banks(ctx, f"psE{tag}", 2) if causal else None
                psS = banks(ctx, f"psS{tag}", 2)
                psT = banks(ctx, f"psT{tag}", 2)
                psO = banks(ctx, f"psO{tag}", 2)
                s_qk = [sem(f"s_qk{tag}{r}") for r in range(RING)]
                s_wr = [sem(f"s_wr{tag}{r}") for r in range(RING)] if causal else None
                s_rd = [sem(f"s_rd{tag}{r}") for r in range(RING)] if causal else None
                names = ("emm", "eev", "smm", "soft", "nm", "exp", "tmm", "tdve", "tact", "pv", "rinv", "o")
                s_emm, s_eev, s_smm, s_soft, s_nm, s_exp, s_tmm, s_tdve, s_tact, s_pv, s_rinv, s_o = (
                    sem(f"s_{n}{tag}") for n in names)
                s_seen, s_seen_sp = sem(f"s_seen{tag}"), sem(f"s_seen_sp{tag}")

                def run(eng, step):
                    for n in range(-LOAD, RING):
                        step(n, n % RING, n // RING)
                    last = NBH // RING - 2
                    with eng.Fori(1, last) as it:
                        for r in range(RING):
                            step(it * RING + r, r, it)
                    for n in range(last * RING, NBH + 1):
                        step(n, n % RING, n // RING)

                def stage_of(n, r, it, ahead):
                    if isinstance(n, int) and not 0 <= n + ahead < NBH:
                        return None
                    return n + ahead, (r + ahead) % RING, it + (r + ahead) // RING

                block = ctx.enter_context(nc.Block())

                @block.sync
                def _(sp):
                    def step(n, r, it):
                        if h := stage_of(n, r, it, LOAD):
                            m, slot, turn = h
                            at = m * (DH * S)
                            wait(sp, s_smm, NU * (m - RING + 1))
                            for half, (dst, src) in enumerate(((q[slot], q_pieces), (k[slot], k_pieces))):
                                PS = B * D * S
                                a4 = [[PS, 2], [0, 2]] if half == 0 else [[0, 2], [PS, 2]]
                                a2 = [2 * PS, 2] if half == 0 else [PS, 2]
                                base = src.ap().tensor
                                for i in range(2):
                                    first = (a4[0][0] * i)
                                    sp.dma_start(dst[32 * i:32 * i + 32, :],
                                                 bass.AP(base, at + first, [a4[1], [S, DH], [1, S]])).then_inc(s_qk[slot], 8 * 2)
                                sp.dma_start(dst[64:96, :],
                                             bass.AP(base, at + (0 if half == 0 else 2 * PS), [a2, [S, DH], [1, S]])).then_inc(s_qk[slot], 16)
                        if causal and (h := stage_of(n, r, it, REL)):
                            m, slot, turn = h
                            sp.wait_ge(s_eev, NU * (m + 1))
                            wait(sp, s_rd[slot], 64 * turn)
                            for i in range(NI):
                                at, w = place[i]
                                sp.dma_start(rel[slot][i][:, 0:w], stage[slot][:, at:at + w]).then_inc(s_wr[slot], 16)
                        if causal and (h := stage_of(n, r, it, READ)):
                            m, slot, turn = h
                            sp.wait_ge(s_wr[slot], 64 * (turn + 1))
                            sp.sem_inc(s_seen_sp, 1)
                            wait(sp, s_soft, NU * (m - RING + 1))
                            for i in range(NI):
                                at, w = place[i]
                                skewed = bass.AP(rel[slot][i].ap().tensor, P - 1, [[w + PADW - 1, P], [1, w]])
                                sp.dma_start(bias[slot][:, at:at + w], skewed).then_inc(s_rd[slot], 16)
                    run(sp, step)

                @block.tensor
                def _(pe):
                    def step(n, r, it):
                        if causal and (h := stage_of(n, r, it, REL)):
                            m, slot, turn = h
                            pe.wait_ge(s_qk[slot], 96 * (turn + 1))
                            for u, unit in enumerate(units):
                                g = NU * m + u
                                bank = (NU * slot + u) % 2
                                wait(pe, s_eev, g - 1)
                                for i, off, w in unit:
                                    mm = nc.tensor.matmul(psE[bank][:, off:off + w], q[slot][:, i * P:(i + 1) * P],
                                                          ErP[:, S - w:S], start=True, stop=True)
                                mm.then_inc(s_emm, 1)
                        if h := stage_of(n, r, it, 0):
                            m, slot, turn = h
                            pe.wait_ge(s_exp, m + 1)
                            for u, unit in enumerate(units):
                                bank = (NU * slot + u) % 2
                                before = (u - 2) % NU
                                owner, back = (s_tact, act_units) if before in act_units else (s_tdve, dve_units)
                                wait(pe, owner, len(back) * (m - (u < 2)) + back.index(before) + 1)
                                for i, off, w in unit:
                                    at = 512 * u + off
                                    for j in range(w // P):
                                        tr = nc.tensor.transpose(psT[bank][:, off + j * P:off + (j + 1) * P],
                                                                 scores[slot][:, at + j * P:at + (j + 1) * P], ident[:, :])
                                tr.then_inc(s_tmm, 1)
                        if h := stage_of(n, r, it, SCORE):
                            m, slot, turn = h
                            pe.wait_ge(s_qk[slot], 96 * (turn + 1))
                            for u, unit in enumerate(units):
                                g = NU * m + u
                                bank = (NU * slot + u) % 2
                                wait(pe, s_soft, g - 1)
                                for i, off, w in unit:
                                    mm = nc.tensor.matmul(psS[bank][:, off:off + w], q[slot][:, i * P:(i + 1) * P],
                                                          k[slot][:, 0:w], start=True, stop=True)
                                mm.then_inc(s_smm, 1)
                        if h := stage_of(n, r, it, 0):
                            m, slot, turn = h
                            pe.wait_ge(s_tdve, len(dve_units) * (m + 1))
                            if act_units:
                                pe.wait_ge(s_tact, len(act_units) * (m + 1))
                            wait(pe, s_o, m - 1)
                            for i in range(NI):
                                at, w = place[i]
                                nj = w // P
                                for j in range(nj):
                                    mm = nc.tensor.matmul(psO[slot % 2][:, i * DH:(i + 1) * DH],
                                                          PT[slot % 2][:, at + j * P:at + (j + 1) * P],
                                                          V[:, bass.ds(m, 1), j, :].rearrange("p a d -> p (a d)"),
                                                          start=(j == 0), stop=(j == nj - 1))
                            mm.then_inc(s_pv, 1)
                    run(pe, step)

                @block.vector
                def _(dve):
                    def step(n, r, it):
                        if h := stage_of(n, r, it, -1):
                            m, slot, turn = h
                            dve.wait_ge(s_exp, m + 1)
                            nc.vector.reciprocal(rinv[:, slot, :], sums[:, slot, :]).then_inc(s_rinv, 1)
                            dve.wait_ge(s_rinv, m + 1)
                            dve.wait_ge(s_pv, m + 1)
                            nc.vector.tensor_tensor(attn[:, bass.ds(m, 1), :, :].rearrange("p a i d -> p (a i) d"),
                                                    psO[slot % 2][:, 0:NI * DH].rearrange("p (i d) -> p i d", d=DH),
                                                    rinv[:, slot, :].unsqueeze(2).broadcast_to([P, NI, DH]), ALU.mult).then_inc(s_o, 1)
                        if h := stage_of(n, r, it, 0):
                            m, slot, turn = h
                            wait(dve, s_pv, m - 1)
                            for u in dve_units:
                                dve.wait_ge(s_tmm, NU * m + u + 1)
                                nc.vector.tensor_copy(PT[slot % 2][:, 512 * u:512 * u + WU[u]],
                                                      psT[(NU * slot + u) % 2][:, 0:WU[u]]).then_inc(s_tdve, 1)
                        if h := stage_of(n, r, it, SOFT):
                            m, slot, turn = h
                            if causal:
                                dve.wait_ge(s_rd[slot], 64 * (turn + 1))
                            wait(dve, s_tmm, NU * (m - RING + 1))
                            for u, unit in enumerate(units):
                                dve.wait_ge(s_smm, NU * m + u + 1)
                                dve.sem_inc(s_seen, 1)
                                for i, off, w in unit:
                                    at = 512 * u + off
                                    ttr = nc.vector.tensor_tensor_reduce(
                                        out=scores[slot][:, at:at + w], in0=psS[(NU * slot + u) % 2][:, off:off + w],
                                        in1=bias[slot][:, at:at + w], scale=1.0, scalar=-3.0e38, op0=ALU.add, op1=ALU.max,
                                        accum_out=mx[:, slot, i:i + 1])
                                ttr.then_inc(s_soft, 1)
                            dve.wait_ge(s_soft, NU * (m + 1))
                            nc.vector.tensor_scalar(nm[:, slot, :], mx[:, slot, :], -1.0 / 4, None, ALU.mult).then_inc(s_nm, 1)
                    run(dve, step)

                @block.scalar
                def _(act):
                    def step(n, r, it):
                        if causal and (h := stage_of(n, r, it, REL)):
                            m, slot, turn = h
                            wait(act, s_wr[slot], 64 * turn)
                            for u in range(NU):
                                act.wait_ge(s_emm, NU * m + u + 1)
                                nc.scalar.copy(stage[slot][:, 512 * u:512 * u + WU[u]],
                                               psE[(NU * slot + u) % 2][:, 0:WU[u]]).then_inc(s_eev, 1)
                        if act_units and (h := stage_of(n, r, it, 0)):
                            m, slot, turn = h
                            wait(act, s_pv, m - 1)
                            for u in act_units:
                                act.wait_ge(s_tmm, NU * m + u + 1)
                                nc.scalar.copy(PT[slot % 2][:, 512 * u:512 * u + WU[u]],
                                               psT[(NU * slot + u) % 2][:, 0:WU[u]]).then_inc(s_tact, 1)
                        if h := stage_of(n, r, it, SOFT):
                            m, slot, turn = h
                            act.wait_ge(s_nm, m + 1)
                            wait(act, s_rinv, m - RING + 1)
                            for i in range(NI):
                                at, w = place[i]
                                ex = nc.scalar.activation(scores[slot][:, at:at + w], scores[slot][:, at:at + w], ACT.Exp,
                                                          bias=nm[:, slot, i:i + 1], scale=1.0 / 4,
                                                          accum_out=sums[:, slot, i:i + 1])
                            ex.then_inc(s_exp, 1)
                    run(act, step)

        with ExitStack() as ctx:
            ctxT = sb(ctx, "ctxT", [P, DK, TOK])
            V = sb(ctx, "V", [P, NBH, NI, DH])
            attn = sb(ctx, "attn", [P, NBH, NI, DH])

            with ExitStack() as c0:
                ErP = sb(c0, "ErP", [KP, S], BF16)
                with ExitStack() as c1:
                    er = sb(c1, "er", [KP, S])
                    ep = sb(c1, "ep", [KP, 2, S])
                    eb = sb(c1, "eb", [KP, 3, S], BF16)
                    neg = sb(c1, "neg", [P, PADW])
                    s_er, s_neg, s_pad, s_es, s_pick = (sem(f"s_{n}") for n in ("er", "neg", "pad", "es", "pick"))
                    block = c1.enter_context(nc.Block())

                    @block.sync
                    def _(sp):
                        sp.dma_start(x[:, :, :], a["x"].rearrange("b (i p) d -> p (b i) d", p=P)).then_inc(s_const, 16)
                        sp.dma_start(ident[:, :], a["ident"]).then_inc(s_const, 16)
                        sp.dma_start(ctxT[:, :, :], a["ctxT"].rearrange("(k p) t -> p k t", p=P)).then_inc(s_ctx, 16)
                        er_t = a["ErT"].tensor
                        sp.dma_start(er[:, :], bass.AP(er_t, 0, [[0, PIECES], [S, DH], [1, S]])).then_inc(s_er, 16)
                        sp.wait_ge(s_neg, 1)
                        for r in range(RING):
                            for i in range(NI):
                                w = P * (i + 1)
                                sp.dma_start(rel[r][i][:, w:w + PADW], neg[:, :]).then_inc(s_pad, 16)
                        sp.wait_ge(s_es, 5)
                        for g, piece in enumerate((0, 1, 0, 1, 2, 0)):
                            rows = slice(g * DH, (g + 1) * DH)
                            sp.dma_start(ErP[rows, :], eb[rows, piece, :]).then_inc(s_pick, 16)
                        sp.wait_ge(s_pick, 16 * PIECES)
                        sp.wait_ge(s_pad, 16 * RING * NI)

                    @block.vector
                    def _(dve):
                        nc.vector.memset(neg[:, :], NEG).then_inc(s_neg, 1)
                        dve.wait_ge(s_er, 16)
                        nc.vector.tensor_copy(eb[:, 0, :], er[:, :]).then_inc(s_es, 1)
                        dve.wait_ge(s_es, 1)
                        nc.vector.tensor_tensor(ep[:, 0, :], er[:, :], eb[:, 0, :], ALU.subtract).then_inc(s_es, 1)
                        dve.wait_ge(s_es, 2)
                        nc.vector.tensor_copy(eb[:, 1, :], ep[:, 0, :]).then_inc(s_es, 1)
                        dve.wait_ge(s_es, 3)
                        nc.vector.tensor_tensor(ep[:, 1, :], ep[:, 0, :], eb[:, 1, :], ALU.subtract).then_inc(s_es, 1)
                        dve.wait_ge(s_es, 4)
                        nc.vector.tensor_copy(eb[:, 2, :], ep[:, 1, :]).then_inc(s_es, 1)

                layer_norm("a", load_x=True)
                project("a", a["L0_WqT"], a["L0_WkT"], a["L0_WvT"], a["L0_bq"], a["L0_bk"], a["L0_bv"], V, ctxT)
                attention("a", True, V, attn, None, ErP)

            def add_attention():
                s_res = sem("s_res")
                with nc.Block() as block:
                    @block.vector
                    def _(dve):
                        for b in range(B):
                            to = x[:, b * NI:(b + 1) * NI, :].rearrange("p i (h d) -> p i h d", d=DH)
                            src = attn[:, b * HEADS:(b + 1) * HEADS, :, :].rearrange("p h i d -> p i h d")
                            for i in range(NI):
                                nc.vector.tensor_tensor(to[:, i], to[:, i], src[:, i], ALU.add).then_inc(s_res, 1)

            add_attention()
            layer_norm("b")

            moe(nc, a, sem, sb, banks, x, xnT, ident)

            layer_norm("c")
            project("c", a["L1_WqT"], a["L1_WkT"], a["L1_WvT"], None, None, None, V, ctxT)
            with ExitStack() as c2:
                mask_bias = sb(c2, "mask_bias", [P, NI * S])
                with ExitStack() as c3:
                    mask = sb(c3, "mask", [P, NI * S], I32)
                    s_mask, s_mb = sem("s_mask"), sem("s_mb")
                    block = c3.enter_context(nc.Block())

                    @block.sync
                    def _(sp):
                        sp.dma_start(mask[:, :].rearrange("p (i s) -> p i s", s=S),
                                     a["mask"].rearrange("a b (i p) s -> p (a b i) s", p=P)).then_inc(s_mask, 16)

                    @block.vector
                    def _(dve):
                        dve.wait_ge(s_mask, 16)
                        nc.vector.tensor_scalar(mask_bias[:, :], mask[:, :], 0.0, NEG, ALU.is_equal, ALU.mult).then_inc(s_mb, 1)

                attention("c", False, V, attn, mask_bias, None)
            out_projection(nc, a, sem, sb, banks, x, attn, ident)

        layer_norm("d")
        ffn(nc, a, sem, sb, banks, x, xn, ident, out)


def out_projection(nc, a, sem, sb, banks, x, attn, ident):
    with ExitStack() as ctx:
        w = sb(ctx, "wo", [P, DK, D])
        aN = sb(ctx, "aN", [P, TT, D])
        aT = sb(ctx, "aT", [P, DK, TOK])
        pt = banks(ctx, "opt", 4)
        po = banks(ctx, "opo", 4)
        s_w, s_n, s_tr, s_ev, s_mm, s_x = (sem(f"s_op{n}") for n in ("w", "n", "tr", "ev", "mm", "x"))
        block = ctx.enter_context(nc.Block())

        @block.sync
        def _(sp):
            sp.dma_start(w[:, :, :], a["L1_WoT"].rearrange("(k p) e -> p k e", p=P)).then_inc(s_w, 16)

        @block.vector
        def _(dve):
            for t in range(TT):
                b, i = divmod(t, NI)
                nc.vector.tensor_copy(aN[:, t, :].rearrange("p (h d) -> p h d", d=DH),
                                      attn[:, b * HEADS:(b + 1) * HEADS, i, :]).then_inc(s_n, 1)
            for t in range(TT):
                dve.wait_ge(s_mm, t + 1)
                nc.vector.tensor_tensor(x[:, t, :], po[t % 4][:, 0:D], x[:, t, :], ALU.add).then_inc(s_x, 1)

        @block.tensor
        def _(pe):
            pe.wait_ge(s_w, 16)
            for c in range(B):
                for dk in range(DK):
                    u = c * DK + dk
                    pe.wait_ge(s_n, NI * (c + 1))
                    wait(pe, s_ev, u - 3)
                    for j in range(NI):
                        tr = nc.tensor.transpose(pt[u % 4][:, j * P:(j + 1) * P], aN[:, c * NI + j, dk * P:(dk + 1) * P], ident[:, :])
                    tr.then_inc(s_tr, 1)
                pe.wait_ge(s_ev, DK * (c + 1))
                for j in range(NI):
                    t = c * NI + j
                    wait(pe, s_x, t - 3)
                    for dk in range(DK):
                        mm = nc.tensor.matmul(po[t % 4][:, 0:D], aT[:, dk, t * P:(t + 1) * P], w[:, dk, :],
                                              start=(dk == 0), stop=(dk == DK - 1))
                    mm.then_inc(s_mm, 1)

        @block.scalar
        def _(act):
            for u in range(B * DK):
                c, dk = divmod(u, DK)
                act.wait_ge(s_tr, u + 1)
                nc.scalar.copy(aT[:, dk, c * S:(c + 1) * S], pt[u % 4][:, :]).then_inc(s_ev, 1)


def moe(nc, a, sem, sb, banks, x, xnT, ident):
    with ExitStack() as ctx:
        wtok = sb(ctx, "wtok", [P, TT, E])
        with ExitStack() as c1:
            rw = sb(c1, "rw", [P, DK, E])
            iota = sb(c1, "iota", [P, E])
            lg = sb(c1, "lg", [P, TT, E])
            best = sb(c1, "best", [P, TT, 8])
            bidx = sb(c1, "bidx", [P, TT, 8], U32)
            idx = sb(c1, "idx", [P, TT, 8])
            d12 = sb(c1, "d12", [P, TT])
            e12 = sb(c1, "e12", [P, TT])
            p1 = sb(c1, "p1", [P, TT])
            p2 = sb(c1, "p2", [P, TT])
            den = sb(c1, "den", [P, TT])
            oh = sb(c1, "oh", [P, 2, TT, E])
            pl = banks(c1, "pl", 1)[0]
            s_w, s_mm, s_lg, s_b, s_i, s_d, s_e, s_p, s_oh = (sem(f"s_ro{n}") for n in ("w", "mm", "lg", "b", "i", "d", "e", "p", "oh"))
            block = c1.enter_context(nc.Block())

            @block.sync
            def _(sp):
                sp.dma_start(rw[:, :, :], a["routerT"].rearrange("(k p) e -> p k e", p=P)).then_inc(s_w, 16)
                sp.dma_start(iota[:, :], a["iota"]).then_inc(s_w, 16)

            @block.tensor
            def _(pe):
                pe.wait_ge(s_w, 32)
                for t in range(TT):
                    for dk in range(DK):
                        mm = nc.tensor.matmul(pl[:, t * E:(t + 1) * E], xnT[:, dk, t * P:(t + 1) * P], rw[:, dk, :],
                                              start=(dk == 0), stop=(dk == DK - 1))
                mm.then_inc(s_mm, 1)

            @block.scalar
            def _(act):
                act.wait_ge(s_d, 1)
                nc.scalar.activation(e12[:, :], d12[:, :], ACT.Exp).then_inc(s_e, 1)

            @block.vector
            def _(dve):
                dve.wait_ge(s_mm, 1)
                nc.vector.tensor_copy(lg[:, :, :].rearrange("p t e -> p (t e)"), pl[:, 0:TT * E]).then_inc(s_lg, 1)
                dve.wait_ge(s_lg, 1)
                for t in range(TT):
                    nc.vector.max(best[:, t, :], lg[:, t, :]).then_inc(s_b, 1)
                for t in range(TT):
                    dve.wait_ge(s_b, t + 1)
                    last = nc.vector.max_index(bidx[:, t, :], best[:, t, :], lg[:, t, :])
                last.then_inc(s_i, 1)
                nc.vector.tensor_tensor(d12[:, :], best[:, :, 1], best[:, :, 0], ALU.subtract).then_inc(s_d, 1)
                dve.wait_ge(s_i, 1)
                nc.vector.tensor_copy(idx[:, :, :], bidx[:, :, :]).then_inc(s_i, 1)
                dve.wait_ge(s_e, 1)
                nc.vector.tensor_scalar(den[:, :], e12[:, :], 1.0, None, ALU.add).then_inc(s_p, 1)
                dve.wait_ge(s_p, 1)
                nc.vector.reciprocal(p1[:, :], den[:, :]).then_inc(s_p, 1)
                dve.wait_ge(s_p, 2)
                nc.vector.tensor_tensor(p2[:, :], e12[:, :], p1[:, :], ALU.mult).then_inc(s_p, 1)
                dve.wait_ge(s_i, 2)
                dve.wait_ge(s_w, 32)
                for n in range(2):
                    nc.vector.tensor_tensor(oh[:, n, :, :], iota[:, :].unsqueeze(1).broadcast_to([P, TT, E]),
                                            idx[:, :, n:n + 1].broadcast_to([P, TT, E]), ALU.is_equal).then_inc(s_oh, 1)
                dve.wait_ge(s_p, 3)
                for n, p in enumerate((p1, p2)):
                    dve.wait_ge(s_oh, n + 1)
                    nc.vector.tensor_tensor(oh[:, n, :, :], oh[:, n, :, :], p[:, :].unsqueeze(2).broadcast_to([P, TT, E]),
                                            ALU.mult).then_inc(s_oh, 1)
                dve.wait_ge(s_oh, 4)
                nc.vector.tensor_tensor(wtok[:, :, :], oh[:, 0, :, :], oh[:, 1, :, :], ALU.add).then_inc(s_oh, 1)

        w1 = [sb(ctx, f"w1_{i}", [P, DK, F]) for i in range(2)]
        w2 = [sb(ctx, f"w2_{i}", [P, FB, D]) for i in range(2)]
        b1 = [sb(ctx, f"b1_{i}", [P, FB]) for i in range(2)]
        b2 = [sb(ctx, f"b2_{i}", [1, D]) for i in range(2)]
        ones = sb(ctx, "ones1", [1, P])
        hT = [sb(ctx, f"hT{i}", [P, FB, S]) for i in range(2)]
        ph = banks(ctx, "ph", 4)
        py = banks(ctx, "py", 2)
        s_w = [sem(f"s_moew{i}") for i in range(2)]
        s_h, s_g, s_y, s_x, s_one = (sem(f"s_moe{n}") for n in ("h", "g", "y", "x", "one"))
        NS = 2 * B
        block = ctx.enter_context(nc.Block())

        def run(eng, step):
            for s in range(NS):
                step(s, s, 0)
            with eng.Fori(1, E // 2) as it:
                for s in range(NS):
                    step(it * NS + s, s, it)

        @block.sync
        def _(sp):
            def load(e, i, s):
                wait(sp, s_y, s)
                sp.dma_start(w1[i][:, :, :], a["w1T"][bass.ds(e, 1), :, :].rearrange("a (k p) f -> p (a k) f", p=P)).then_inc(s_w[i], 16)
                sp.dma_start(w2[i][:, :, :], a["w2T"][bass.ds(e, 1), :, :].rearrange("a (k p) d -> p (a k) d", p=P)).then_inc(s_w[i], 16)
                sp.dma_start(b1[i][:, :], a["b1"][bass.ds(e, 1), :, :].rearrange("a p k -> p (a k)")).then_inc(s_w[i], 16)
                sp.dma_start(b2[i][:, :], a["b2"][bass.ds(e, 1), :]).then_inc(s_w[i], 16)

            for e in range(2):
                load(e, e, 0)
            with sp.Fori(1, E // 2) as it:
                for i in range(2):
                    load(2 * it + i, i, 4 * B * (2 * it + i - 1))

        @block.tensor
        def _(pe):
            pe.wait_ge(s_one, 1)

            def step(n, s, it):
                i, c = divmod(s, B)
                if c == 0:
                    pe.wait_ge(s_w[i], 64 * (it + 1))
                for f in range(FB):
                    wait(pe, s_g, n * FB + f - 3)
                    for dk in range(DK):
                        mm = nc.tensor.matmul(ph[f % 4][:, :], w1[i][:, dk, f * P:(f + 1) * P], xnT[:, dk, c * S:(c + 1) * S],
                                              start=(dk == 0), stop=(dk == DK - 1))
                    mm.then_inc(s_h, 1)
                pe.wait_ge(s_g, (n + 1) * FB)
                for j in range(NI):
                    wait(pe, s_x, n * NI + j - 1)
                    for f in range(FB):
                        nc.tensor.matmul(py[j % 2][:, 0:D], hT[s % 2][:, f, j * P:(j + 1) * P], w2[i][:, f, :],
                                         start=(f == 0), stop=False)
                    nc.tensor.matmul(py[j % 2][:, 0:D], ones[:, :], b2[i][:, :], start=False, stop=True).then_inc(s_y, 1)
            run(pe, step)

        @block.scalar
        def _(act):
            def step(n, s, it):
                i, c = divmod(s, B)
                if c == 0:
                    act.wait_ge(s_w[i], 64 * (it + 1))
                wait(act, s_y, NI * (n - 1))
                for f in range(FB):
                    act.wait_ge(s_h, n * FB + f + 1)
                    nc.scalar.activation(hT[s % 2][:, f, :], ph[f % 4][:, :], ACT.Gelu, bias=b1[i][:, f:f + 1]).then_inc(s_g, 1)
            run(act, step)

        @block.vector
        def _(dve):
            nc.vector.memset(ones[:, :], 1.0).then_inc(s_one, 1)

            def step(n, s, it):
                i, c = divmod(s, B)
                for j in range(NI):
                    t = c * NI + j
                    dve.wait_ge(s_y, n * NI + j + 1)
                    w = wtok[:, t, i:i + 1] if isinstance(it, int) else wtok[:, t, bass.ds(2 * it + i, 1)]
                    nc.vector.scalar_tensor_tensor(out=x[:, t, :], in0=py[j % 2][:, 0:D], scalar=w, in1=x[:, t, :],
                                                   op0=ALU.mult, op1=ALU.add).then_inc(s_x, 1)
            run(dve, step)


def ffn(nc, a, sem, sb, banks, x, xn, ident, out):
    with ExitStack() as ctx:
        wq = [sb(ctx, f"wq{n}", [P, 2 * F], BF16) for n in range(3)]
        ws = sb(ctx, "ws", [P, 3])
        identb = sb(ctx, "identb", [P, P], BF16)
        with ExitStack() as c1:
            w = [sb(c1, f"wf{n}", [P, 2 * F]) for n in range(3)]
            r1 = sb(c1, "wr1", [P, 2 * F])
            r2 = sb(c1, "wr2", [P, 2 * F])
            asum = sb(c1, "asum", [P, 3])
            scale = sb(c1, "wscale", [P, 3])
            ones = sb(c1, "onesPP", [P, P])
            pm = banks(c1, "pm", 1)[0]
            s_w = [sem(f"s_fw{n}") for n in range(3)]
            s_one, s_sum, s_mm, s_sc, s_q = (sem(f"s_f{n}") for n in ("one", "sum", "mm", "sc", "q"))
            block = c1.enter_context(nc.Block())

            @block.sync
            def _(sp):
                for n, name in enumerate(("gateT", "upT", "downT")):
                    free = F if n < 2 else D
                    sp.dma_start(w[n][:, :].rearrange("p (k f) -> p k f", f=free),
                                 a[name].rearrange("(k p) f -> p k f", p=P)).then_inc(s_w[n], 16)

            @block.tensor
            def _(pe):
                pe.wait_ge(s_one, 1)
                pe.wait_ge(s_sum, 3)
                nc.tensor.matmul(pm[:, 0:3], ones[:, :], asum[:, :], start=True, stop=True).then_inc(s_mm, 1)

            @block.vector
            def _(dve):
                nc.vector.memset(ones[:, :], 1.0).then_inc(s_one, 1)
                nc.vector.tensor_copy(identb[:, :], ident[:, :])
                for n in range(3):
                    dve.wait_ge(s_w[n], 16)
                    nc.vector.tensor_reduce(asum[:, n:n + 1], w[n][:, :], AX.X, ALU.add, apply_absolute_value=True).then_inc(s_sum, 1)
                dve.wait_ge(s_mm, 1)
                nc.vector.tensor_scalar(ws[:, :], pm[:, 0:3], 1.0 / (F * D), 1e-5, ALU.mult, ALU.max).then_inc(s_sc, 1)
                dve.wait_ge(s_sc, 1)
                nc.vector.reciprocal(scale[:, :], ws[:, :]).then_inc(s_sc, 1)
                dve.wait_ge(s_sc, 2)
                for n in range(3):
                    nc.vector.tensor_scalar(r1[:, :], w[n][:, :], scale[:, n:n + 1], MAGIC, ALU.mult, ALU.add).then_inc(s_q, 1)
                    dve.wait_ge(s_q, 3 * n + 1)
                    nc.vector.tensor_scalar(r2[:, :], r1[:, :], MAGIC, 1.0, ALU.subtract, ALU.min).then_inc(s_q, 1)
                    dve.wait_ge(s_q, 3 * n + 2)
                    nc.vector.tensor_scalar(wq[n][:, :], r2[:, :], -1.0, None, ALU.max).then_inc(s_q, 1)
                    dve.wait_ge(s_q, 3 * n + 3)

        gq = wq[0][:, :].rearrange("p (k f) -> p k f", f=F)
        uq = wq[1][:, :].rearrange("p (k f) -> p k f", f=F)
        dq = wq[2][:, :].rearrange("p (k d) -> p k d", d=D)
        am = sb(ctx, "am", [P, TT])
        sx = sb(ctx, "sx", [P, TT])
        gs = sb(ctx, "gs", [P, TT])
        us = sb(ctx, "us", [P, TT])
        ys = sb(ctx, "ys", [P, TT])
        inv = sb(ctx, "inv", [P, TT])
        r = sb(ctx, "rq", [P, TT, D])
        xq = sb(ctx, "xq", [P, TT, D], BF16)
        xqT = sb(ctx, "xqT", [P, DK, TOK], BF16)
        g = [sb(ctx, f"g{i}", [P, F]) for i in range(2)]
        hh = [sb(ctx, f"hh{i}", [P, F]) for i in range(2)]
        hr = [sb(ctx, f"hr{i}", [P, F]) for i in range(2)]
        hq = [sb(ctx, f"hq{i}", [P, F], BF16) for i in range(2)]
        hqT = [sb(ctx, f"hqT{i}", [P, F], BF16) for i in range(2)]
        y = [sb(ctx, f"y{i}", [P, D]) for i in range(2)]
        ha = sb(ctx, "ha", [P, TT])
        hm = sb(ctx, "hm", [P, TT])
        hs = sb(ctx, "hs", [P, TT])
        pg = banks(ctx, "pg", 2)
        pu = banks(ctx, "pu", 2)
        ptx = [ctx.enter_context(nc.psum_tensor(f"ptx{i}", [P, F], BF16)) for i in range(2)]
        py = banks(ctx, "pfy", 2)
        s_a, s_s, s_r, s_xq, s_tr, s_ev = (sem(f"s_g{n}") for n in ("a", "s", "r", "xq", "tr", "ev"))
        s_g, s_u, s_si, s_h, s_ha, s_hs, s_hr, s_hq, s_ht, s_he, s_y, s_o = (
            sem(f"s_h{n}") for n in ("g", "u", "si", "h", "ha", "hs", "hr", "hq", "ht", "he", "y", "o"))
        s_st = [sem(f"s_st{i}") for i in range(2)]
        block = ctx.enter_context(nc.Block())
        out_v = out.rearrange("b (i p) d -> (b i) p d", p=P)

        def finish(dve, t):
            i = t % 2
            dve.wait_ge(s_y, t + 1)
            if t >= 2:
                dve.wait_ge(s_st[i], 16 * (t // 2))
            nc.vector.scalar_tensor_tensor(out=y[i][:, :], in0=py[i][:, 0:D], scalar=ys[:, t:t + 1], in1=x[:, t, :],
                                           op0=ALU.mult, op1=ALU.add).then_inc(s_o, 1)

        @block.vector
        def _(dve):
            for t in range(TT):
                nc.vector.tensor_reduce(am[:, t:t + 1], xn[:, t, :], AX.X, ALU.max, apply_absolute_value=True).then_inc(s_a, 1)
            dve.wait_ge(s_a, TT)
            nc.vector.tensor_scalar(sx[:, :], am[:, :], 1e-5, None, ALU.max).then_inc(s_s, 1)
            dve.wait_ge(s_s, 1)
            nc.vector.reciprocal(inv[:, :], sx[:, :]).then_inc(s_s, 1)
            nc.vector.tensor_scalar(gs[:, :], sx[:, :], ws[:, 0:1], 1.0 / 127, ALU.mult, ALU.mult).then_inc(s_s, 1)
            nc.vector.tensor_scalar(us[:, :], sx[:, :], ws[:, 1:2], 1.0 / 127, ALU.mult, ALU.mult).then_inc(s_s, 1)
            dve.wait_ge(s_s, 4)
            nc.vector.tensor_scalar(sx[:, :], inv[:, :], 127.0, None, ALU.mult).then_inc(s_s, 1)
            dve.wait_ge(s_s, 5)
            for t in range(TT):
                nc.vector.tensor_scalar(r[:, t, :], xn[:, t, :], sx[:, t:t + 1], MAGIC, ALU.mult, ALU.add).then_inc(s_r, 1)
            for t in range(TT):
                dve.wait_ge(s_r, t + 1)
                nc.vector.tensor_scalar(xq[:, t, :], r[:, t, :], MAGIC, None, ALU.subtract).then_inc(s_xq, 1)
            for t in range(TT):
                i = t % 2
                for n in range(2):
                    c = slice(n * 512, (n + 1) * 512)
                    dve.wait_ge(s_si, 2 * t + n + 1)
                    dve.wait_ge(s_u, 2 * t + n + 1)
                    nc.vector.scalar_tensor_tensor(out=hh[i][:, c], in0=pu[n][:, :], scalar=us[:, t:t + 1], in1=g[i][:, c],
                                                   op0=ALU.mult, op1=ALU.mult).then_inc(s_h, 1)
                dve.wait_ge(s_h, 2 * (t + 1))
                nc.vector.tensor_reduce(ha[:, t:t + 1], hh[i][:, :], AX.X, ALU.max, apply_absolute_value=True).then_inc(s_ha, 1)
                dve.wait_ge(s_ha, t + 1)
                nc.vector.tensor_scalar(hm[:, t:t + 1], ha[:, t:t + 1], 1e-5, None, ALU.max).then_inc(s_hs, 1)
                dve.wait_ge(s_hs, 4 * t + 1)
                nc.vector.reciprocal(ha[:, t:t + 1], hm[:, t:t + 1]).then_inc(s_hs, 1)
                nc.vector.tensor_scalar(ys[:, t:t + 1], hm[:, t:t + 1], ws[:, 2:3], 1.0 / 127, ALU.mult, ALU.mult).then_inc(s_hs, 1)
                dve.wait_ge(s_hs, 4 * t + 2)
                nc.vector.tensor_scalar(hs[:, t:t + 1], ha[:, t:t + 1], 127.0, None, ALU.mult).then_inc(s_hs, 1)
                dve.wait_ge(s_hs, 4 * t + 4)
                nc.vector.tensor_scalar(hr[i][:, :], hh[i][:, :], hs[:, t:t + 1], MAGIC, ALU.mult, ALU.add).then_inc(s_hr, 1)
                dve.wait_ge(s_hr, t + 1)
                wait(dve, s_ht, t - 1)
                nc.vector.tensor_scalar(hq[i][:, :], hr[i][:, :], MAGIC, None, ALU.subtract).then_inc(s_hq, 1)
                if t >= 1:
                    finish(dve, t - 1)
            finish(dve, TT - 1)

        @block.sync
        def _(sp):
            for t in range(TT):
                sp.wait_ge(s_o, t + 1)
                sp.dma_start(out_v[t], y[t % 2][:, :]).then_inc(s_st[t % 2], 16)
            for i in range(2):
                sp.wait_ge(s_st[i], 16 * TT // 2)

        @block.tensor
        def _(pe):
            for c in range(B):
                pe.wait_ge(s_xq, NI * (c + 1))
                wait(pe, s_ev, c - 1)
                for dk in range(DK):
                    for j in range(NI):
                        tr = nc.tensor.transpose(ptx[c % 2][:, (dk * NI + j) * P:(dk * NI + j + 1) * P],
                                                 xq[:, c * NI + j, dk * P:(dk + 1) * P], identb[:, :])
                tr.then_inc(s_tr, 1)

            def gate_up(t):
                pe.wait_ge(s_ev, t // NI + 1)
                if t == 0:
                    pe.wait_ge(s_ev, B)
                for n in range(2):
                    wait(pe, s_si, 2 * (t - 1) + n + 1)
                    for dk in range(DK):
                        mm = nc.tensor.matmul(pg[n][:, :], xqT[:, dk, t * P:(t + 1) * P], gq[:, dk, n * 512:(n + 1) * 512],
                                              start=(dk == 0), stop=(dk == DK - 1))
                    mm.then_inc(s_g, 1)
                    wait(pe, s_h, 2 * (t - 1) + n + 1)
                    for dk in range(DK):
                        mm = nc.tensor.matmul(pu[n][:, :], xqT[:, dk, t * P:(t + 1) * P], uq[:, dk, n * 512:(n + 1) * 512],
                                              start=(dk == 0), stop=(dk == DK - 1))
                    mm.then_inc(s_u, 1)

            gate_up(0)
            for t in range(TT):
                i = t % 2
                if t + 1 < TT:
                    gate_up(t + 1)
                pe.wait_ge(s_hq, t + 1)
                wait(pe, s_he, t - 1)
                for f in range(FB):
                    tr = nc.tensor.transpose(ptx[i][:, f * P:(f + 1) * P], hq[i][:, f * P:(f + 1) * P], identb[:, :])
                tr.then_inc(s_ht, 1)
                pe.wait_ge(s_he, t + 1)
                wait(pe, s_o, t - 1)
                for f in range(FB):
                    mm = nc.tensor.matmul(py[i][:, 0:D], hqT[i][:, f * P:(f + 1) * P], dq[:, f, :],
                                          start=(f == 0), stop=(f == FB - 1))
                mm.then_inc(s_y, 1)

        @block.scalar
        def _(act):
            for c in range(B):
                act.wait_ge(s_tr, c + 1)
                nc.scalar.copy(xqT[:, :, c * S:(c + 1) * S], ptx[c % 2][:, :].rearrange("p (k s) -> p k s", s=S)).then_inc(s_ev, 1)
            act.wait_ge(s_s, 3)

            def hidden_out(t):
                act.wait_ge(s_ht, t + 1)
                wait(act, s_y, t - 1)
                nc.scalar.copy(hqT[t % 2][:, :], ptx[t % 2][:, :]).then_inc(s_he, 1)

            for t in range(TT):
                wait(act, s_h, 2 * (t - 1))
                for n in range(2):
                    act.wait_ge(s_g, 2 * t + n + 1)
                    nc.scalar.activation(g[t % 2][:, n * 512:(n + 1) * 512], pg[n][:, :], ACT.Silu,
                                         scale=gs[:, t:t + 1]).then_inc(s_si, 1)
                if t >= 1:
                    hidden_out(t - 1)
            hidden_out(TT - 1)


def kernel(**inputs):
    import numpy as np
    import concourse.bacc as bacc
    from concourse.bass_utils import run_bass_kernel_spmd

    g = {n: np.asarray(v) for n, v in inputs.items()}
    t = lambda v: np.ascontiguousarray(np.swapaxes(v, -1, -2))
    cols = lambda v: np.ascontiguousarray(np.swapaxes(v.reshape(*v.shape[:-1], -1, P), -1, -2))
    arrays = {
        "x": g["x"],
        "ctxT": t(g["ctx_1024"].reshape(TOK, D)),
        "mask": g["mask_1x1xSxS2_ik0"],
        "ident": np.eye(P, dtype=np.float32),
        "iota": np.ascontiguousarray(np.broadcast_to(np.arange(E, dtype=np.float32), (P, E))),
        "L0_WqT": t(g["L0_xattn_Wq"]), "L0_WkT": t(g["L0_xattn_Wk"]), "L0_WvT": t(g["L0_xattn_Wv"]),
        "L0_bq": cols(g["L0_xattn_bq"]), "L0_bk": cols(g["L0_xattn_bk"]), "L0_bv": g["L0_xattn_bv"],
        "ErT": t(g["L0_xattn_Er"]),
        "routerT": t(g["L0_ffn_router_w"]),
        "w1T": t(g["L0_ffn_w1"]), "w2T": t(g["L0_ffn_w2"]), "b1": cols(g["L0_ffn_b1"]), "b2": g["L0_ffn_b2"],
        "L1_WqT": t(g["L1_xattn_w_q"]), "L1_WkT": t(g["L1_xattn_w_k"]), "L1_WvT": t(g["L1_xattn_w_v"]),
        "L1_WoT": t(g["L1_xattn_w_o"]),
        "gateT": t(g["L1_ffn_w_gate"]), "upT": t(g["L1_ffn_w_up"]), "downT": t(g["L1_ffn_w_down"]),
    }
    nc = bacc.Bacc("TRN2", target_bir_lowering=False, num_devices=1)
    aps = {n: nc.dram_tensor(f"in_{n}", v.shape, mybir.dt.from_np(v.dtype), kind="ExternalInput").ap()
           for n, v in arrays.items()}
    out = nc.dram_tensor("out", (B, S, D), F32, kind="ExternalOutput").ap()
    build(nc, aps, out)
    r = run_bass_kernel_spmd(nc, [{f"in_{n}": v for n, v in arrays.items()}], core_ids=[0])
    return r.results[0]["out"]
```

```python
from contextlib import ExitStack

import concourse.bass as bass
from concourse import mybir

ALU = mybir.AluOpType
ACT = mybir.ActivationFunctionType
AX = mybir.AxisListType
F32 = mybir.dt.float32
BF16 = mybir.dt.bfloat16
I32 = mybir.dt.int32
U32 = mybir.dt.uint32

P = 128
B, S, D = 4, 512, 256
TOK = B * S
TT = TOK // P
DK = D // P
HEADS, DH = 16, 16
NBH = B * HEADS
NI = S // P
E, F, TOPK = 8, 1024, 2
FB = F // P
SLOT_TILES = (TOK * TOPK + E * (P - 1)) // P
W1_ROW = DK * F + FB
NEG = -2.0 ** 100
LN_EPS = 1e-5
MAGIC = 1.5 * 2.0 ** 23
PIECES = 6
KP = PIECES * DH
RING = 4
GROUP = 4
ROUND = 2 * GROUP
VW = DH + 1
CG = 32
LQ, LK = (0, 0, 0, 1, 1, 2), (0, 1, 2, 0, 1, 0)

CAUSAL_UNITS = [[(3, 0, 512)], [(2, 0, 384), (0, 384, 128)], [(1, 0, 256)]]
CAUSAL_KEYS = [[(NI - 1 - i, off, w) for i, off, w in unit] for unit in CAUSAL_UNITS]


def wait(eng, sem, value):
    if isinstance(value, int) and value <= 0:
        return
    eng.wait_ge(sem, value)


def build(nc, a, out):
    top = ExitStack()

    def dram(name, shape, dt):
        return nc.dram_tensor(name, shape, dt)

    packed = dram("packed", (PIECES, B, D, 2, S), BF16)
    REL_W = sum(w for unit in CAUSAL_UNITS for _, _, w in unit)
    slots_in = dram("slots_in", (SLOT_TILES * P, D), F32)
    slots_out = dram("slots_out", (SLOT_TILES * P, D), F32)
    rel = [dram(f"rel_{r}", (P, REL_W), F32) for r in range(RING)]

    with top:
        def sem(name):
            return nc.alloc_semaphore(name)

        def sb(ctx, name, shape, dt=F32):
            return ctx.enter_context(nc.sbuf_tensor(name, shape, dt))

        def banks(ctx, name, n, dt=F32):
            return [ctx.enter_context(nc.psum_tensor(f"{name}{i}", [P, 512], dt)) for i in range(n)]

        x = sb(top, "x", [P, TT, D])
        xn = sb(top, "xn", [P, TT, D])
        xnT = sb(top, "xnT", [P, DK, TOK])
        ident = sb(top, "ident", [P, P])
        s_const = sem("s_const")
        s_ctx = sem("s_ctx")
        s_zeroed = sem("s_zeroed")

        def layer_norm(tag, load_x=False):
            with ExitStack() as ctx:
                stats = sb(ctx, f"stats{tag}", [P, TT, 6])
                mv = sb(ctx, f"mv{tag}", [P, TT, 2])
                ve = sb(ctx, f"ve{tag}", [P, TT])
                sd = sb(ctx, f"sd{tag}", [P, TT])
                rs = sb(ctx, f"rs{tag}", [P, TT])
                t1 = sb(ctx, f"t1{tag}", [P, TT])
                t2 = sb(ctx, f"t2{tag}", [P, TT])
                ps = banks(ctx, f"lnps{tag}", 4)
                s_stat, s_var, s_sd, s_rs = (sem(f"s_{n}{tag}") for n in ("stat", "var", "sd", "rs"))
                s_xn, s_tr, s_ev = (sem(f"s_{n}{tag}") for n in ("xn", "tr", "ev"))
                block = ctx.enter_context(nc.Block())

                @block.vector
                def _(dve):
                    if load_x:
                        dve.wait_ge(s_const, 32)
                    for t in range(TT):
                        nc.vector.bn_stats(stats[:, t, :], x[:, t, :]).then_inc(s_stat, 1)
                    for t in range(TT):
                        dve.wait_ge(s_stat, t + 1)
                        agg = nc.vector.bn_aggr(mv[:, t, :], stats[:, t, :])
                    agg.then_inc(s_var, 1)
                    dve.wait_ge(s_var, 1)
                    nc.vector.tensor_scalar(ve[:, :], mv[:, :, 1], LN_EPS, None, ALU.add).then_inc(s_var, 1)
                    dve.wait_ge(s_sd, 1)
                    nc.vector.reciprocal(rs[:, :], sd[:, :]).then_inc(s_rs, 1)
                    dve.wait_ge(s_rs, 1)
                    nc.vector.tensor_tensor(t1[:, :], rs[:, :], rs[:, :], ALU.mult).then_inc(s_rs, 1)
                    dve.wait_ge(s_rs, 2)
                    nc.vector.tensor_tensor(t2[:, :], t1[:, :], ve[:, :], ALU.mult).then_inc(s_rs, 1)
                    dve.wait_ge(s_rs, 3)
                    nc.vector.tensor_scalar(t1[:, :], t2[:, :], -0.5, 1.5, ALU.mult, ALU.add).then_inc(s_rs, 1)
                    dve.wait_ge(s_rs, 4)
                    nc.vector.tensor_tensor(sd[:, :], t1[:, :], rs[:, :], ALU.mult).then_inc(s_rs, 1)
                    dve.wait_ge(s_rs, 5)
                    for t in range(TT):
                        nc.vector.tensor_scalar(xn[:, t, :], x[:, t, :], mv[:, t, 0:1], sd[:, t:t + 1],
                                                ALU.subtract, ALU.mult).then_inc(s_xn, 1)

                @block.scalar
                def _(act):
                    act.wait_ge(s_var, 2)
                    nc.scalar.activation(sd[:, :], ve[:, :], ACT.Sqrt).then_inc(s_sd, 1)
                    for u in range(B * DK):
                        c, dk = divmod(u, DK)
                        act.wait_ge(s_tr, u + 1)
                        nc.scalar.copy(xnT[:, dk, c * S:(c + 1) * S], ps[u % 4][:, :]).then_inc(s_ev, 1)

                @block.tensor
                def _(pe):
                    if load_x:
                        pe.wait_ge(s_const, 32)
                    for u in range(B * DK):
                        c, dk = divmod(u, DK)
                        pe.wait_ge(s_xn, NI * (c + 1))
                        wait(pe, s_ev, u - 3)
                        for j in range(NI):
                            tr = nc.tensor.transpose(ps[u % 4][:, j * P:(j + 1) * P],
                                                     xn[:, c * NI + j, dk * P:(dk + 1) * P], ident[:, :])
                        tr.then_inc(s_tr, 1)

        def project(tag, w_q, w_k, w_v, b_q, b_k, b_v, V, ctxT):
            with ExitStack() as ctx:
                w = sb(ctx, f"wqkv{tag}", [P, 3, DK, D])
                bqk = sb(ctx, f"bqk{tag}", [P, 2, DK])
                bvb = sb(ctx, f"bvb{tag}", [P, D])
                full = sb(ctx, f"full{tag}", [P, 2, S])
                rest = sb(ctx, f"rest{tag}", [P, 2, S])
                pieces = sb(ctx, f"pieces{tag}", [P, 2, 3, S], BF16)
                ps = banks(ctx, f"prps{tag}", 4)
                pv = banks(ctx, f"pvps{tag}", 4)
                s_w, s_mm, s_full, s_r1, s_p2, s_p3 = (sem(f"s_{n}{tag}") for n in ("w", "mm", "full", "r1", "p2", "p3"))
                s_vmm, s_vev = sem(f"s_vmm{tag}"), sem(f"s_vev{tag}")
                s_out = [sem(f"s_pout{tag}{i}") for i in range(2)]
                units = [(1, c, eh) for c in range(B) for eh in range(DK)] + [(0, c, eh) for c in range(B) for eh in range(DK)]
                STORES = 3 * 16
                loads = 3 + (b_q is not None) * 3
                block = ctx.enter_context(nc.Block())

                @block.sync
                def _(sp):
                    for n, src in enumerate((w_q, w_k, w_v)):
                        sp.dma_start(w[:, n, :, :], src.rearrange("(k p) e -> p k e", p=P)).then_inc(s_w, 16)
                    if b_q is not None:
                        sp.dma_start(bqk[:, 0, :], b_q).then_inc(s_w, 16)
                        sp.dma_start(bqk[:, 1, :], b_k).then_inc(s_w, 16)
                        sp.dma_start(bvb[:, :], bass.AP(b_v.tensor, 0, [[0, P], [1, D]])).then_inc(s_w, 16)
                    for g, (qk, c, eh) in enumerate(units):
                        rows = packed[:, c, eh * P:(eh + 1) * P, qk, :].rearrange("g e s -> e g s")
                        have = pieces[:, g % 2, :, :]
                        first = [have[:, 0:3, :], have[:, 0:2, :], have[:, 0:1, :]] if qk else [
                            have[:, 0:1, :].broadcast_to([P, 3, S]), have[:, 1:2, :].broadcast_to([P, 2, S]), have[:, 2:3, :]]
                        sp.wait_ge(s_p3, g + 1)
                        for at, src in zip((0, 3, 5), first):
                            sp.dma_start(rows[:, at:at + src.shape[1], :], src).then_inc(s_out[g % 2], 16)
                    for i in range(2):
                        sp.wait_ge(s_out[i], STORES * len(units) // 2)

                @block.tensor
                def _(pe):
                    pe.wait_ge(s_w, 16 * loads)
                    pe.wait_ge(s_ctx, 16)

                    def v_tile(t):
                        wait(pe, s_vev, t - 3)
                        for dk in range(DK):
                            mm = nc.tensor.matmul(pv[t % 4][:, 0:D], ctxT[:, dk, t * P:(t + 1) * P], w[:, 2, dk, :],
                                                  start=(dk == 0), stop=(dk == DK - 1))
                        mm.then_inc(s_vmm, 1)

                    for g, (qk, c, eh) in enumerate(units):
                        src = ctxT if qk else xnT
                        wait(pe, s_full, g - 3)
                        for dk in range(DK):
                            mm = nc.tensor.matmul(ps[g % 4][:, :], w[:, qk, dk, eh * P:(eh + 1) * P],
                                                  src[:, dk, c * S:(c + 1) * S], start=(dk == 0), stop=(dk == DK - 1))
                        mm.then_inc(s_mm, 1)
                        v_tile(g)

                @block.scalar
                def _(act):
                    act.wait_ge(s_w, 16 * loads)
                    for g, (qk, c, eh) in enumerate(units):
                        act.wait_ge(s_mm, g + 1)
                        wait(act, s_p3, g - 1)
                        if g >= 2:
                            act.wait_ge(s_out[g % 2], STORES * (g // 2))
                        if b_q is not None:
                            bias = bqk[:, qk, eh:eh + 1]
                            nc.scalar.activation(full[:, g % 2, :], ps[g % 4][:, :], ACT.Identity, bias=bias)
                            nc.scalar.activation(pieces[:, g % 2, 0, :], ps[g % 4][:, :], ACT.Identity,
                                                 bias=bias).then_inc(s_full, 1)
                        else:
                            nc.scalar.copy(full[:, g % 2, :], ps[g % 4][:, :])
                            nc.scalar.copy(pieces[:, g % 2, 0, :], ps[g % 4][:, :]).then_inc(s_full, 1)

                @block.vector
                def _(dve):
                    dve.wait_ge(s_w, 16 * loads)
                    for g in range(len(units)):
                        k = g % 2
                        dve.wait_ge(s_full, g + 1)
                        nc.vector.tensor_tensor(rest[:, k, :], full[:, k, :], pieces[:, k, 0, :], ALU.subtract).then_inc(s_r1, 1)
                        dve.wait_ge(s_vmm, g + 1)
                        b, j = divmod(g, NI)
                        to = V[:, b * HEADS:(b + 1) * HEADS, j, 0:DH]
                        src = pv[g % 4][:, 0:D].rearrange("p (h d) -> p h d", d=DH)
                        if b_v is not None:
                            nc.vector.tensor_tensor(to, src, bvb[:, :].rearrange("p (h d) -> p h d", d=DH), ALU.add).then_inc(s_vev, 1)
                        else:
                            nc.vector.tensor_copy(to, src).then_inc(s_vev, 1)
                        dve.wait_ge(s_r1, g + 1)
                        nc.vector.tensor_copy(pieces[:, k, 1, :], rest[:, k, :]).then_inc(s_p2, 1)
                        dve.wait_ge(s_p2, g + 1)
                        nc.vector.tensor_tensor(pieces[:, k, 2, :], rest[:, k, :], pieces[:, k, 1, :], ALU.subtract).then_inc(s_p3, 1)

        def run_heads(eng, first, last, step):
            for n in range(first, ROUND):
                step(n, n % ROUND, n // ROUND)
            rounds = NBH // ROUND - 2
            with eng.Fori(1, rounds + 1) as it:
                for r in range(ROUND):
                    step(it * ROUND + r, r, it)
            for n in range((rounds + 1) * ROUND, last + 1):
                step(n, n % ROUND, n // ROUND)

        def stage_of(n, r, it, ahead):
            if isinstance(n, int) and not 0 <= n + ahead < NBH:
                return None
            return n + ahead, (r + ahead) % RING, it * (ROUND // RING) + (r + ahead) // RING

        def group_of(n, r, it, back):
            g = it * (ROUND // GROUP) + (r // GROUP - back)
            if isinstance(n, int) and not 0 <= g < NBH // GROUP:
                return None
            return g, (r // GROUP - back) % 2

        def load_head(sp, m, dst, s_qk):
            sp.dma_start(dst, bass.AP(packed.ap().tensor, m * (DH * 2 * S),
                                      [[B * D * 2 * S, PIECES], [2 * S, DH], [1, 2 * S]])).then_inc(s_qk, 16)

        class Values:

            def __init__(self, ctx, tag):
                self.spread = [sb(ctx, f"spread{tag}{i}", [P, GROUP, NI, CG]) for i in range(2)]
                self.zeros = sb(ctx, f"zeros{tag}", [P, VW])
                self.heads = sb(ctx, f"heads{tag}", [P, S])
                self.rinv = sb(ctx, f"rinv{tag}", [P, 2, NI, GROUP])
                self.psO = banks(ctx, f"psO{tag}", 1)[0]
                self.psX = banks(ctx, f"psX{tag}", 1)[0]
                names = ("zero", "spread", "pv", "heads", "turned", "rinv", "o")
                (self.s_zero, self.s_spread, self.s_pv, self.s_heads, self.s_turned, self.s_rinv, self.s_o) = (
                    sem(f"s_{n}{tag}") for n in names)

            def clear(self, dve):
                for i in range(2):
                    nc.vector.memset(self.spread[i][:, :, :, :], 0.0).then_inc(self.s_zero, 1)
                nc.vector.memset(self.zeros[:, :], 0.0).then_inc(self.s_zero, 1)

            def spread_values(self, pool, g, par):
                wait(pool, self.s_pv, NI * (g - 1))
                wait(pool, self.s_spread, g)
                src = V[:, bass.ds(GROUP * g, GROUP), :, :]
                nc.gpsimd.tensor_tensor(self.spread[par][:, :, :, 0:VW].rearrange("p h j d -> p (h j) d"),
                                        src.rearrange("p h j d -> p (h j) d"),
                                        self.zeros[:, :].unsqueeze(1).broadcast_to([P, GROUP * NI, VW]),
                                        ALU.add).then_inc(self.s_spread, 1)

            def weigh(self, pe, g, par, j, s_prob, count, keys):
                if j == 0:
                    pe.wait_ge(self.s_spread, g + 1)
                    pe.wait_ge(s_prob, count)
                    wait(pe, self.s_heads, g)
                for h in range(GROUP):
                    probs = keys(h)
                    w = probs.shape[-1]
                    mm = nc.tensor.matmul(self.psO[h * CG:(h + 1) * CG, S - w:S], self.spread[par][:, h, j, :], probs,
                                          start=(j == 0), stop=(j == NI - 1))
                mm.then_inc(self.s_pv, 1)

            def copy_out(self, act, g, par):
                act.wait_ge(self.s_pv, NI * (g + 1))
                wait(act, self.s_turned, g)
                nc.scalar.copy(self.heads[:, :], self.psO[:, :]).then_inc(self.s_heads, 1)

            def turn(self, pe, g, par):
                pe.wait_ge(self.s_heads, g + 1)
                wait(pe, self.s_o, g)
                for i in range(NI):
                    tr = nc.tensor.transpose(self.psX[:, i * P:(i + 1) * P], self.heads[:, i * P:(i + 1) * P], ident[:, :])
                tr.then_inc(self.s_turned, 1)

            def divide(self, dve, g, par):
                dve.wait_ge(self.s_turned, g + 1)
                got = self.psX[:, :].rearrange("p (i h d) -> p i h d", h=GROUP, d=CG)
                nc.vector.reciprocal(self.rinv[:, par, :, :], got[:, :, :, DH]).then_inc(self.s_rinv, 1)
                dve.wait_ge(self.s_rinv, g + 1)
                nc.vector.tensor_tensor(attn[:, bass.ds(GROUP * g, GROUP), :, :].rearrange("p h i d -> p i h d"),
                                        got[:, :, :, 0:DH],
                                        self.rinv[:, par, :, :].unsqueeze(3).broadcast_to([P, NI, GROUP, DH]),
                                        ALU.mult).then_inc(self.s_o, 1)

        def causal_attention(ErP, identb, dmask):
            units = CAUSAL_UNITS
            NU = len(units)
            WU = [u[-1][1] + u[-1][2] for u in units]
            place = {i: (512 * u + off, w) for u, unit in enumerate(units) for i, off, w in unit}
            key_place = {j: (512 * u + off, w) for u, unit in enumerate(CAUSAL_KEYS) for j, off, w in unit}
            last = NBH + 2 * GROUP
            LOAD, REL, READ, SOFT, EXP = 6, 5, 3, 2, 1
            with ExitStack() as ctx:
                qk = [sb(ctx, f"qk{r}", [KP, 2 * S], BF16) for r in range(ROUND)]
                stage = [sb(ctx, f"stage{r}", [P, REL_W]) for r in range(2)]
                bias = [sb(ctx, f"bias{r}", [P, REL_W]) for r in range(RING)]
                scores = [sb(ctx, f"scores{r}", [P, REL_W]) for r in range(RING)]
                PT = [sb(ctx, f"PT{r}", [P, REL_W]) for r in range(ROUND)]
                mx = sb(ctx, "mx", [P, RING, NI])
                nm = sb(ctx, "nm", [P, RING, NI])
                vals = Values(ctx, "a")
                psE = banks(ctx, "psE", 2)
                psS = banks(ctx, "psS", 2)
                psT = banks(ctx, "psT", 2)
                s_qk = [sem(f"s_qk{r}") for r in range(ROUND)]
                s_wr = [sem(f"s_wr{r}") for r in range(RING)]
                s_rd = [sem(f"s_rd{r}") for r in range(RING)]
                names = ("emm", "eev", "smm", "soft", "nm", "exp", "tmm", "tev", "seen", "seensp")
                s_emm, s_eev, s_smm, s_soft, s_nm, s_exp, s_tmm, s_tev, s_seen, s_seen_sp = (
                    sem(f"s_{n}") for n in names)
                block = ctx.enter_context(nc.Block())

                @block.sync
                def _(sp):
                    def step(n, r, it):
                        if h := stage_of(n, r, it, READ):
                            m, slot, turn = h
                            sp.wait_ge(s_wr[slot], 16 * (turn + 1))
                            sp.sem_inc(s_seen_sp, 1)
                            wait(sp, s_soft, NU * (m - RING + 1))
                            skewed = bass.AP(rel[slot].ap().tensor, P - 1, [[REL_W - 1, P], [1, REL_W]])
                            sp.dma_start(bias[slot][:, :], skewed).then_inc(s_rd[slot], 16)
                        if h := stage_of(n, r, it, LOAD):
                            m, slot, turn = h
                            wait(sp, s_smm, NU * (m - ROUND + 1))
                            slot = (r + LOAD) % ROUND
                            load_head(sp, m, qk[slot][:, :], s_qk[slot])
                        if h := stage_of(n, r, it, REL):
                            m, slot, turn = h
                            sp.wait_ge(s_eev, NU * (m + 1))
                            wait(sp, s_rd[slot], 16 * turn)
                            sp.dma_start(rel[slot][:, :], stage[slot % 2][:, :]).then_inc(s_wr[slot], 16)
                    run_heads(sp, -LOAD, last, step)

                @block.tensor
                def _(pe):
                    def relative(m, slot, q_k, u):
                        bank = (NU * slot + u) % 2
                        wait(pe, s_eev, NU * m + u - 1)
                        for i, off, w in units[u]:
                            mm = nc.tensor.matmul(psE[bank][:, off:off + w], q_k[:, i * P:(i + 1) * P],
                                                  ErP[:, S - w:S], start=True, stop=True)
                        mm.then_inc(s_emm, 1)

                    def score(m, slot, q_k, u):
                        bank = (NU * slot + u) % 2
                        wait(pe, s_soft, NU * m + u - 1)
                        for i, off, w in units[u]:
                            nc.tensor.matmul(psS[bank][:, off:off + w], q_k[:, i * P:(i + 1) * P],
                                             q_k[:, S:S + w], start=True, stop=False)
                            mm = nc.tensor.matmul(psS[bank][:, off + w - P:off + w], identb[:, :], dmask[:, :],
                                                  start=False, stop=True)
                        mm.then_inc(s_smm, 1)

                    def turn_probs(m, slot, u):
                        bank = (NU * slot + u) % 2
                        wait(pe, s_tev, NU * m + u - 1)
                        for j, off, w in CAUSAL_KEYS[u]:
                            for i in range(j, NI):
                                at = place[i][0] + j * P
                                to = off + (i - j) * P
                                tr = nc.tensor.transpose(psT[bank][:, to:to + P], scores[slot][:, at:at + P], ident[:, :])
                        tr.then_inc(s_tmm, 1)

                    def step(n, r, it):
                        early, soft, late = (stage_of(n, r, it, k) for k in (REL, SOFT, 0))
                        for u in range(NU):
                            if soft:
                                score(soft[0], soft[1], qk[(r + SOFT) % ROUND], u)
                            if late:
                                if u == 0:
                                    pe.wait_ge(s_exp, late[0] + 1)
                                turn_probs(late[0], late[1], u)
                            if early:
                                at = (r + REL) % ROUND
                                if u == 0:
                                    pe.wait_ge(s_qk[at], 16 * (it + (r + REL) // ROUND + 1))
                                relative(early[0], early[1], qk[at], u)
                        if h := group_of(n, r, it, 1):
                            g, par = h
                            at, w = key_place[r % GROUP]
                            vals.weigh(pe, g, par, r % GROUP, s_tev, NU * GROUP * (g + 1),
                                       lambda h: PT[par * GROUP + h][:, at:at + w])
                        if r % GROUP == 1 and (h := group_of(n, r, it, 2)):
                            vals.turn(pe, *h)
                    run_heads(pe, -LOAD, last, step)

                @block.vector
                def _(dve):
                    vals.clear(dve)

                    def step(n, r, it):
                        if r % GROUP == 2 and (h := group_of(n, r, it, 2)):
                            vals.divide(dve, *h)
                        soft, late = (stage_of(n, r, it, k) for k in (SOFT, 0))
                        if late and r % GROUP == 0:
                            g, par = group_of(n, r, it, 0)
                            wait(dve, vals.s_pv, NI * (g - 1))
                        if soft:
                            m, slot, turn = soft
                            dve.wait_ge(s_rd[slot], 16 * (turn + 1))
                            wait(dve, s_tmm, NU * (m - RING + 1))
                        for u, unit in enumerate(units):
                            if soft:
                                m, slot, turn = soft
                                dve.wait_ge(s_smm, NU * m + u + 1)
                                dve.sem_inc(s_seen, 1)
                                for i, off, w in unit:
                                    at = 512 * u + off
                                    ttr = nc.vector.tensor_tensor_reduce(
                                        out=scores[slot][:, at:at + w], in0=psS[(NU * slot + u) % 2][:, off:off + w],
                                        in1=bias[slot][:, at:at + w], scale=1.0, scalar=-3.0e38, op0=ALU.add, op1=ALU.max,
                                        accum_out=mx[:, slot, i:i + 1])
                                ttr.then_inc(s_soft, 1)
                            if late:
                                m, slot, turn = late
                                dve.wait_ge(s_tmm, NU * m + u + 1)
                                nc.vector.tensor_copy(PT[r][:, 512 * u:512 * u + WU[u]],
                                                      psT[(NU * slot + u) % 2][:, 0:WU[u]]).then_inc(s_tev, 1)
                        if soft:
                            m, slot, turn = soft
                            dve.wait_ge(s_soft, NU * (m + 1))
                            nc.vector.tensor_scalar(nm[:, slot, :], mx[:, slot, :], -1.0 / 4, None, ALU.mult).then_inc(s_nm, 1)
                    run_heads(dve, -LOAD, last, step)

                @block.gpsimd
                def _(pool):
                    pool.wait_ge(vals.s_zero, 3)

                    def step(n, r, it):
                        if r % GROUP == 0 and (h := group_of(n, r, it, 0)):
                            vals.spread_values(pool, *h)
                    run_heads(pool, 0, NBH - 1, step)

                @block.scalar
                def _(act):
                    def step(n, r, it):
                        if r % GROUP == 0 and (h := group_of(n, r, it, 2)):
                            vals.copy_out(act, *h)
                        early, soft = (stage_of(n, r, it, k) for k in (REL, EXP))
                        if early and (not isinstance(n, int) or early[0] >= 2):
                            act.wait_ge(s_wr[(r + REL - 2) % RING], 16 * (it * (ROUND // RING) + (r + REL - 2) // RING + 1))
                        if soft:
                            act.wait_ge(s_nm, soft[0] + 1)
                        for i in range(NI):
                            if early and i < NU:
                                m, slot, turn = early
                                act.wait_ge(s_emm, NU * m + i + 1)
                                nc.scalar.copy(stage[slot % 2][:, 512 * i:512 * i + WU[i]],
                                               psE[(NU * slot + i) % 2][:, 0:WU[i]]).then_inc(s_eev, 1)
                            if soft:
                                m, slot, turn = soft
                                at, w = place[i]
                                ex = nc.scalar.activation(scores[slot][:, at:at + w], scores[slot][:, at:at + w], ACT.Exp,
                                                          bias=nm[:, slot, i:i + 1], scale=1.0 / 4)
                                if i == NI - 1:
                                    ex.then_inc(s_exp, 1)
                    run_heads(act, -LOAD, last, step)

        def masked_attention(mask_bias, maskT, identb):
            KM = KP + 3
            LOAD, SOFT, ROWS = 3, 2, 1
            last = NBH + 2 * GROUP
            with ExitStack() as ctx:
                qk = [sb(ctx, f"mqk{r}", [KM, 2 * S], BF16) for r in range(RING)]
                PT = [sb(ctx, f"mPT{r}", [P, NI, S]) for r in range(ROUND)]
                unused = sb(ctx, "unused", [P, NI, S], BF16)
                mx = sb(ctx, "mmx", [P, RING, NI])
                neg = sb(ctx, "mneg", [P, RING, NI])
                zero = sb(ctx, "mzero", [P, NI])
                rest = sb(ctx, "mrest", [P, RING, NI])
                mp = sb(ctx, "mpieces", [P, RING, NI, 4], BF16)
                vals = Values(ctx, "m")
                psS = banks(ctx, "mpsS", 2)
                psB = banks(ctx, "mpsB", 2)
                psM = ctx.enter_context(nc.psum_tensor("mpsM", [P, 1024], BF16))
                s_qk = [sem(f"s_mqk{r}") for r in range(RING)]
                names = ("one", "smm", "soft", "mp", "mt", "row", "bmm", "exp", "seen")
                s_seen_p = sem("s_mseenp")
                s_one, s_smm, s_soft, s_mp, s_mt, s_row, s_bmm, s_exp, s_seen = (sem(f"s_m{n}") for n in names)
                block = ctx.enter_context(nc.Block())

                @block.sync
                def _(sp):
                    def step(n, r, it):
                        if h := stage_of(n, r, it, LOAD):
                            m, slot, turn = h
                            wait(sp, s_bmm, NI * (m - RING + 1))
                            load_head(sp, m, qk[slot][0:KP, :], s_qk[slot])
                    run_heads(sp, -LOAD, last, step)

                @block.tensor
                def _(pe):
                    pe.wait_ge(s_one, RING)

                    def step(n, r, it):
                        soft, rows, late = (stage_of(n, r, it, k) for k in (SOFT, ROWS, 0))
                        if soft:
                            pe.wait_ge(s_qk[soft[1]], 16 * (soft[2] + 1))
                        if late:
                            pe.wait_ge(s_row, late[0] + 1)
                        for i in range(NI):
                            if soft:
                                m, slot, turn = soft
                                wait(pe, s_soft, NI * m + i - 1)
                                nc.tensor.matmul(psS[i % 2][:, :], qk[slot][0:KP, i * P:(i + 1) * P], qk[slot][0:KP, S:2 * S],
                                                 start=True, stop=True).then_inc(s_smm, 1)
                            if late:
                                m, slot, turn = late
                                wait(pe, s_exp, NI * m + i - 1)
                                nc.tensor.matmul(psB[i % 2][:, :], qk[slot][:, S + i * P:S + (i + 1) * P], qk[slot][:, 0:S],
                                                 start=True, stop=False)
                                nc.tensor.matmul(psB[i % 2][:, :], identb[:, :], maskT[:, i, :],
                                                 start=False, stop=True).then_inc(s_bmm, 1)
                            if rows and i == 1:
                                m, slot, turn = rows
                                pe.wait_ge(s_mp, 5 * (m + 1))
                                wait(pe, s_row, m)
                                for k in range(NI):
                                    tr = nc.tensor.transpose(psM[KP:KP + 3, k * P:(k + 1) * P], mp[:, slot, k, 0:3], identb[:, :])
                                tr.then_inc(s_mt, 1)
                        if h := group_of(n, r, it, 1):
                            g, par = h
                            vals.weigh(pe, g, par, r % GROUP, s_exp, NI * GROUP * (g + 1),
                                       lambda h: PT[par * GROUP + h][:, r % GROUP, :])
                        if r % GROUP == 1 and (h := group_of(n, r, it, 2)):
                            vals.turn(pe, *h)
                    run_heads(pe, -LOAD, last, step)

                @block.gpsimd
                def _(pool):
                    pool.wait_ge(s_one, RING + 1)
                    pool.wait_ge(vals.s_zero, 3)

                    def step(n, r, it):
                        if r % GROUP == 0 and (h := group_of(n, r, it, 0)):
                            vals.spread_values(pool, *h)
                        if h := stage_of(n, r, it, SOFT):
                            m, slot, turn = h
                            pool.wait_ge(s_soft, NI * (m + 1))
                            wait(pool, s_mt, m - RING + 1)
                            wait(pool, s_mp, 5 * m)
                            pool.sem_inc(s_seen_p, 1)
                            nc.gpsimd.tensor_scalar(neg[:, slot, :], mx[:, slot, :], -1.0, 0.0, ALU.mult, ALU.add).then_inc(s_mp, 1)
                            pool.wait_ge(s_mp, 5 * m + 1)
                            nc.gpsimd.tensor_tensor(mp[:, slot, :, 0], neg[:, slot, :], zero[:, :], ALU.add).then_inc(s_mp, 1)
                            pool.wait_ge(s_mp, 5 * m + 2)
                            nc.gpsimd.tensor_tensor(rest[:, slot, :], neg[:, slot, :], mp[:, slot, :, 0], ALU.subtract).then_inc(s_mp, 1)
                            pool.wait_ge(s_mp, 5 * m + 3)
                            nc.gpsimd.tensor_tensor(mp[:, slot, :, 1], rest[:, slot, :], zero[:, :], ALU.add).then_inc(s_mp, 1)
                            pool.wait_ge(s_mp, 5 * m + 4)
                            nc.gpsimd.tensor_tensor(mp[:, slot, :, 2], rest[:, slot, :], mp[:, slot, :, 1], ALU.subtract).then_inc(s_mp, 1)
                    run_heads(pool, -LOAD, NBH - 1, step)

                @block.vector
                def _(dve):
                    for r in range(RING):
                        nc.vector.memset(qk[r][KP:KM, :], 1.0).then_inc(s_one, 1)
                    nc.vector.memset(zero[:, :], 0.0).then_inc(s_one, 1)
                    vals.clear(dve)

                    def step(n, r, it):
                        if h := stage_of(n, r, it, SOFT):
                            m, slot, turn = h
                            wait(dve, s_soft, NI * m)
                            for i in range(NI):
                                dve.wait_ge(s_smm, NI * m + i + 1)
                                dve.sem_inc(s_seen, 1)
                                nc.vector.tensor_tensor_reduce(
                                    out=unused[:, i, :], in0=psS[i % 2][:, :], in1=mask_bias[:, i, :], scale=1.0, scalar=-3.0e38,
                                    op0=ALU.add, op1=ALU.max, accum_out=mx[:, slot, i:i + 1]).then_inc(s_soft, 1)
                        if r % GROUP == 2 and (h := group_of(n, r, it, 2)):
                            vals.divide(dve, *h)
                    run_heads(dve, -LOAD, last, step)

                @block.scalar
                def _(act):
                    def step(n, r, it):
                        if r % GROUP == 0 and (h := group_of(n, r, it, 2)):
                            vals.copy_out(act, *h)
                        rows, late = (stage_of(n, r, it, k) for k in (ROWS, 0))
                        if late and r % GROUP == 0:
                            g, par = group_of(n, r, it, 0)
                            wait(act, vals.s_pv, NI * (g - 1))
                        for j in range(NI):
                            if late:
                                m, slot, turn = late
                                act.wait_ge(s_bmm, NI * m + j + 1)
                                nc.scalar.activation(PT[r][:, j, :], psB[j % 2][:, :], ACT.Exp, scale=1.0 / 4).then_inc(s_exp, 1)
                            if rows and j == 2:
                                m, slot, turn = rows
                                act.wait_ge(s_mt, m + 1)
                                nc.scalar.copy(qk[slot][KP:KM, 0:S], psM[KP:KM, 0:S]).then_inc(s_row, 1)
                    run_heads(act, -LOAD, last, step)

        with ExitStack() as ctx:
            ctxT = sb(ctx, "ctxT", [P, DK, TOK])
            zero_row = sb(ctx, "zero_row", [P, D])
            V = sb(ctx, "V", [P, NBH, NI, VW])
            identb = sb(ctx, "identb0", [P, P], BF16)
            dmask = sb(ctx, "dmask", [P, P], BF16)
            attn = xn[:, :, :].rearrange("p t d -> p (t d)").rearrange("p (m i d) -> p m i d", i=NI, d=DH)

            with ExitStack() as c0:
                ErP = sb(c0, "ErP", [KP, S], BF16)
                with ExitStack() as c1:
                    er = sb(c1, "er", [KP, S])
                    ep = sb(c1, "ep", [KP, 2, S])
                    eb = sb(c1, "eb", [KP, 3, S], BF16)
                    above = sb(c1, "above", [P, P])
                    s_er, s_above, s_cc, s_es, s_pick = (sem(f"s_{n}") for n in ("er", "above", "cc", "es", "pick"))
                    block = c1.enter_context(nc.Block())

                    @block.sync
                    def _(sp):
                        sp.dma_start(x[:, :, :], a["x"].rearrange("b (i p) d -> p (b i) d", p=P)).then_inc(s_const, 16)
                        sp.dma_start(ident[:, :], a["ident"]).then_inc(s_const, 16)
                        sp.dma_start(ctxT[:, :, :], a["ctxT"].rearrange("(k p) t -> p k t", p=P)).then_inc(s_ctx, 16)
                        er_t = a["ErT"].tensor
                        sp.dma_start(er[:, :], bass.AP(er_t, 0, [[0, PIECES], [S, DH], [1, S]])).then_inc(s_er, 16)
                        sp.dma_start(above[:, :], a["above"]).then_inc(s_above, 16)
                        sp.wait_ge(s_cc, 1)
                        sp.dma_start(slots_in[:, :].rearrange("(n p) d -> p n d", p=P),
                                     zero_row[:, :].unsqueeze(1).broadcast_to([P, SLOT_TILES, D])).then_inc(s_zeroed, 16)
                        sp.wait_ge(s_es, 5)
                        for g, piece in enumerate(LK):
                            rows = slice(g * DH, (g + 1) * DH)
                            sp.dma_start(ErP[rows, :], eb[rows, piece, :]).then_inc(s_pick, 16)
                        sp.wait_ge(s_pick, 16 * PIECES)

                    @block.vector
                    def _(dve):
                        nc.vector.memset(zero_row[:, :], 0.0).then_inc(s_cc, 1)
                        nc.vector.memset(V[:, :, :, DH:VW], 1.0).then_inc(s_cc, 1)
                        dve.wait_ge(s_above, 16)
                        nc.vector.tensor_scalar(dmask[:, :], above[:, :], NEG, None, ALU.mult).then_inc(s_cc, 1)
                        dve.wait_ge(s_const, 32)
                        nc.vector.tensor_copy(identb[:, :], ident[:, :]).then_inc(s_cc, 1)
                        dve.wait_ge(s_er, 16)
                        nc.vector.tensor_copy(eb[:, 0, :], er[:, :]).then_inc(s_es, 1)
                        dve.wait_ge(s_es, 1)
                        nc.vector.tensor_tensor(ep[:, 0, :], er[:, :], eb[:, 0, :], ALU.subtract).then_inc(s_es, 1)
                        dve.wait_ge(s_es, 2)
                        nc.vector.tensor_copy(eb[:, 1, :], ep[:, 0, :]).then_inc(s_es, 1)
                        dve.wait_ge(s_es, 3)
                        nc.vector.tensor_tensor(ep[:, 1, :], ep[:, 0, :], eb[:, 1, :], ALU.subtract).then_inc(s_es, 1)
                        dve.wait_ge(s_es, 4)
                        nc.vector.tensor_copy(eb[:, 2, :], ep[:, 1, :]).then_inc(s_es, 1)

                with nc.cleanup_on_exit():
                    layer_norm("a", load_x=True)
                    project("a", a["L0_WqT"], a["L0_WkT"], a["L0_WvT"], a["L0_bq"], a["L0_bk"], a["L0_bv"], V, ctxT)
                    causal_attention(ErP, identb, dmask)

            def add_attention():
                s_res = sem("s_res")
                with nc.Block() as block:
                    @block.vector
                    def _(dve):
                        for b in range(B):
                            to = x[:, b * NI:(b + 1) * NI, :].rearrange("p i (h d) -> p i h d", d=DH)
                            src = attn[:, b * HEADS:(b + 1) * HEADS, :, :].rearrange("p h i d -> p i h d")
                            for i in range(NI):
                                nc.vector.tensor_tensor(to[:, i], to[:, i], src[:, i], ALU.add).then_inc(s_res, 1)

            with nc.cleanup_on_exit():
                add_attention()
                layer_norm("b")
                moe(nc, a, sem, sb, banks, x, xn, xnT, ident, slots_in, slots_out, s_zeroed)

            layer_norm("c")
            project("c", a["L1_WqT"], a["L1_WkT"], a["L1_WvT"], None, None, None, V, ctxT)
            with ExitStack() as c2:
                mask_bias = sb(c2, "mask_bias", [P, NI, S])
                maskT = sb(c2, "maskT", [P, NI, S], BF16)
                with ExitStack() as c3:
                    mask = sb(c3, "mask", [P, 2, NI, S], I32)
                    s_mask, s_mb = sem("s_mask"), sem("s_mb")
                    block = c3.enter_context(nc.Block())

                    @block.sync
                    def _(sp):
                        for n, name in enumerate(("mask", "maskT")):
                            sp.dma_start(mask[:, n, :, :], a[name].rearrange("a b (i p) s -> p (a b i) s", p=P)).then_inc(s_mask, 16)

                    @block.vector
                    def _(dve):
                        dve.wait_ge(s_mask, 32)
                        for n, to in enumerate((mask_bias, maskT)):
                            nc.vector.tensor_scalar(to[:, :, :], mask[:, n, :, :], 0.0, NEG, ALU.is_equal, ALU.mult).then_inc(s_mb, 1)

                masked_attention(mask_bias, maskT, identb)
            out_projection(nc, a, sem, sb, banks, x, attn, ident)

        layer_norm("d")
        ffn(nc, a, sem, sb, banks, x, xn, ident, out)


def out_projection(nc, a, sem, sb, banks, x, attn, ident):
    with ExitStack() as ctx:
        w = sb(ctx, "wo", [P, DK, D])
        aN = sb(ctx, "aN", [P, TT, D])
        aT = sb(ctx, "aT", [P, DK, TOK])
        pt = banks(ctx, "opt", 4)
        po = banks(ctx, "opo", 4)
        s_w, s_n, s_tr, s_ev, s_mm, s_x = (sem(f"s_op{n}") for n in ("w", "n", "tr", "ev", "mm", "x"))
        block = ctx.enter_context(nc.Block())

        @block.sync
        def _(sp):
            sp.dma_start(w[:, :, :], a["L1_WoT"].rearrange("(k p) e -> p k e", p=P)).then_inc(s_w, 16)

        @block.vector
        def _(dve):
            for t in range(TT):
                b, i = divmod(t, NI)
                nc.vector.tensor_copy(aN[:, t, :].rearrange("p (h d) -> p h d", d=DH),
                                      attn[:, b * HEADS:(b + 1) * HEADS, i, :]).then_inc(s_n, 1)
            for t in range(TT):
                dve.wait_ge(s_mm, t + 1)
                nc.vector.tensor_tensor(x[:, t, :], po[t % 4][:, 0:D], x[:, t, :], ALU.add).then_inc(s_x, 1)

        @block.tensor
        def _(pe):
            pe.wait_ge(s_w, 16)
            for c in range(B):
                for dk in range(DK):
                    u = c * DK + dk
                    pe.wait_ge(s_n, NI * (c + 1))
                    wait(pe, s_ev, u - 3)
                    for j in range(NI):
                        tr = nc.tensor.transpose(pt[u % 4][:, j * P:(j + 1) * P], aN[:, c * NI + j, dk * P:(dk + 1) * P], ident[:, :])
                    tr.then_inc(s_tr, 1)
                pe.wait_ge(s_ev, DK * (c + 1))
                for j in range(NI):
                    t = c * NI + j
                    wait(pe, s_x, t - 3)
                    for dk in range(DK):
                        mm = nc.tensor.matmul(po[t % 4][:, 0:D], aT[:, dk, t * P:(t + 1) * P], w[:, dk, :],
                                              start=(dk == 0), stop=(dk == DK - 1))
                    mm.then_inc(s_mm, 1)

        @block.scalar
        def _(act):
            for u in range(B * DK):
                c, dk = divmod(u, DK)
                act.wait_ge(s_tr, u + 1)
                nc.scalar.copy(aT[:, dk, c * S:(c + 1) * S], pt[u % 4][:, :]).then_inc(s_ev, 1)


def moe(nc, a, sem, sb, banks, x, xn, xnT, ident, slots_in, slots_out, s_zeroed):
    with ExitStack() as ctx:
        prob = sb(ctx, "prob", [P, TOPK, TT])
        slot_of = sb(ctx, "slot_of", [P, TOPK * TT], U32)
        expert_of = sb(ctx, "expert_of", [P, SLOT_TILES], I32)
        with ExitStack() as c2:
            w2 = sb(c2, "w2", [P, E, FB * D])
            s_w2 = sem("s_moew2")
            s_scattered = sem("s_scattered")
            route(nc, a, sem, sb, banks, xn, xnT, prob, slot_of, expert_of, w2, s_w2, slots_in, s_zeroed, s_scattered)
            experts(nc, a, sem, sb, banks, ident, expert_of, w2, s_w2, slots_in, slots_out, s_scattered)
        combine(nc, sem, sb, x, prob, slot_of, slots_out)


def route(nc, a, sem, sb, banks, xn, xnT, prob, slot_of, expert_of, w2, s_w2, slots_in, s_zeroed, s_scattered):
    C = TT * E
    with ExitStack() as c1:
        rw = sb(c1, "rw", [P, DK, E])
        iota = sb(c1, "iota", [P, E])
        tile_no = sb(c1, "tile_no", [P, SLOT_TILES])
        before = sb(c1, "before", [P, P])
        prior = sb(c1, "prior", [P, TOPK, TOPK * C])
        same = sb(c1, "same", [P, E])
        ones = sb(c1, "onesr", [P, P])
        lg = sb(c1, "lg", [P, TT, E])
        best = sb(c1, "best", [P, TT, 8])
        bidx = sb(c1, "bidx", [P, TT, 8], U32)
        idx = sb(c1, "idx", [P, TT, 8])
        d12 = sb(c1, "d12", [P, TT])
        e12 = sb(c1, "e12", [P, TT])
        den = sb(c1, "den", [P, TT])
        chosen = sb(c1, "chosen", [P, TOPK, C])
        totals = sb(c1, "totals", [P, TOPK, P])
        place = sb(c1, "place", [P, TOPK * C])
        picked = sb(c1, "picked", [P, TOPK * C])
        slot = sb(c1, "slot", [P, TOPK * TT])
        frac = sb(c1, "frac", [P, E])
        whole = sb(c1, "whole", [P, E])
        tiles = sb(c1, "tiles", [P, E])
        ends = sb(c1, "ends", [P, E + 1])
        past = sb(c1, "past", [P, SLOT_TILES, E])
        past_n = sb(c1, "past_n", [P, SLOT_TILES])
        expert = sb(c1, "expert", [P, SLOT_TILES])
        pl = banks(c1, "pl", 1)[0]
        pt = banks(c1, "ptot", 1)[0]
        pr = banks(c1, "prank", 1)[0]
        pc = banks(c1, "pcount", 1)[0]
        s_w, s_k, s_mm, s_lg, s_b, s_i, s_d, s_e, s_p, s_oh, s_tot, s_totc, s_rank, s_cnt, s_one, s_place, s_slot = (
            sem(f"s_ro{n}") for n in ("w", "k", "mm", "lg", "b", "i", "d", "e", "p", "oh", "tot", "totc", "rank",
                                      "cnt", "one", "place", "slot"))
        block = c1.enter_context(nc.Block())

        @block.sync
        def _(sp):
            sp.dma_start(rw[:, :, :], a["routerT"].rearrange("(k p) e -> p k e", p=P)).then_inc(s_w, 16)
            for dst, name in ((iota, "iota"), (tile_no, "tile_no"), (before, "above"), (same, "same")):
                sp.dma_start(dst[:, :], a[name]).then_inc(s_k, 16)
            sp.dma_start(prior[:, :, :], a["prior"]).then_inc(s_k, 16)
            for e in range(E):
                sp.dma_start(w2[:, e, :], a["w2p"][e]).then_inc(s_w2, 16)

        @block.tensor
        def _(pe):
            pe.wait_ge(s_w, 16)
            for t in range(TT):
                for dk in range(DK):
                    mm = nc.tensor.matmul(pl[:, t * E:(t + 1) * E], xnT[:, dk, t * P:(t + 1) * P], rw[:, dk, :],
                                          start=(dk == 0), stop=(dk == DK - 1))
            mm.then_inc(s_mm, 1)
            pe.wait_ge(s_one, 1)
            pe.wait_ge(s_oh, TOPK)
            pe.wait_ge(s_k, 16 * 5)
            for k in range(TOPK):
                mm = nc.tensor.matmul(pt[:, k * P:(k + 1) * P], chosen[:, k, :], ones[:, :], start=True, stop=True)
            mm.then_inc(s_tot, 1)
            nc.tensor.matmul(pr[:, 0:TOPK * C], before[:, :], chosen[:, :, :].rearrange("p k c -> p (k c)"),
                             start=True, stop=False)
            pe.wait_ge(s_totc, 1)
            for k in range(TOPK):
                mm = nc.tensor.matmul(pc[:, 0:E], totals[:, k, :], same[:, :], start=(k == 0), stop=(k == TOPK - 1))
            mm.then_inc(s_cnt, 1)
            for k in range(TOPK):
                mm = nc.tensor.matmul(pr[:, 0:TOPK * C], totals[:, k, :], prior[:, k, :], start=False, stop=(k == TOPK - 1))
            mm.then_inc(s_rank, 1)

        @block.scalar
        def _(act):
            act.wait_ge(s_d, 1)
            nc.scalar.activation(e12[:, :], d12[:, :], ACT.Exp).then_inc(s_e, 1)

        @block.vector
        def _(dve):
            nc.vector.memset(ones[:, :], 1.0).then_inc(s_one, 1)
            nc.vector.memset(ends[:, 0:1], 0.0).then_inc(s_one, 1)
            dve.wait_ge(s_mm, 1)
            nc.vector.tensor_copy(lg[:, :, :].rearrange("p t e -> p (t e)"), pl[:, 0:TT * E]).then_inc(s_lg, 1)
            dve.wait_ge(s_lg, 1)
            for t in range(TT):
                nc.vector.max(best[:, t, :], lg[:, t, :]).then_inc(s_b, 1)
            for t in range(TT):
                dve.wait_ge(s_b, t + 1)
                last = nc.vector.max_index(bidx[:, t, :], best[:, t, :], lg[:, t, :])
            last.then_inc(s_i, 1)
            nc.vector.tensor_tensor(d12[:, :], best[:, :, 1], best[:, :, 0], ALU.subtract).then_inc(s_d, 1)
            dve.wait_ge(s_i, 1)
            nc.vector.tensor_copy(idx[:, :, :], bidx[:, :, :]).then_inc(s_i, 1)
            dve.wait_ge(s_i, 2)
            dve.wait_ge(s_k, 16 * 5)
            for k in range(TOPK):
                nc.vector.tensor_tensor(chosen[:, k, :].rearrange("p (t e) -> p t e", e=E),
                                        iota[:, :].unsqueeze(1).broadcast_to([P, TT, E]),
                                        idx[:, :, k:k + 1].broadcast_to([P, TT, E]), ALU.is_equal).then_inc(s_oh, 1)
            dve.wait_ge(s_tot, 1)
            nc.vector.tensor_copy(totals[:, :, :].rearrange("p k c -> p (k c)"), pt[:, 0:TOPK * P]).then_inc(s_totc, 1)
            dve.wait_ge(s_e, 1)
            nc.vector.tensor_scalar(den[:, :], e12[:, :], 1.0, None, ALU.add).then_inc(s_p, 1)
            dve.wait_ge(s_p, 1)
            nc.vector.reciprocal(prob[:, 0, :], den[:, :]).then_inc(s_p, 1)
            dve.wait_ge(s_p, 2)
            nc.vector.tensor_tensor(prob[:, 1, :], e12[:, :], prob[:, 0, :], ALU.mult).then_inc(s_p, 1)
            dve.wait_ge(s_cnt, 1)
            nc.vector.tensor_scalar(frac[:, :], pc[:, 0:E], 1.0 / P, (P - 1) / P - 0.5 + 0.5 / P,
                                    ALU.mult, ALU.add).then_inc(s_place, 1)
            dve.wait_ge(s_place, 1)
            nc.vector.tensor_scalar(whole[:, :], frac[:, :], MAGIC, None, ALU.add).then_inc(s_place, 1)
            dve.wait_ge(s_place, 2)
            nc.vector.tensor_scalar(tiles[:, :], whole[:, :], MAGIC, None, ALU.subtract).then_inc(s_place, 1)
            dve.wait_ge(s_place, 3)
            dve.wait_ge(s_one, 2)
            for e in range(E):
                dve.wait_ge(s_place, 3 + e)
                nc.vector.tensor_tensor(ends[:, e + 1:e + 2], ends[:, e:e + 1], tiles[:, e:e + 1], ALU.add).then_inc(s_place, 1)
            dve.wait_ge(s_place, 3 + E)
            dve.wait_ge(s_rank, 1)
            nc.vector.scalar_tensor_tensor(out=place[:, :].rearrange("p (t e) -> p t e", e=E),
                                           in0=ends[:, 0:E].unsqueeze(1).broadcast_to([P, TOPK * TT, E]), scalar=float(P),
                                           in1=pr[:, 0:TOPK * C].rearrange("p (t e) -> p t e", e=E),
                                           op0=ALU.mult, op1=ALU.add).then_inc(s_slot, 1)
            dve.wait_ge(s_slot, 1)
            nc.vector.tensor_tensor(picked[:, :], place[:, :], chosen[:, :, :].rearrange("p k c -> p (k c)"),
                                    ALU.mult).then_inc(s_slot, 1)
            dve.wait_ge(s_slot, 2)
            nc.vector.tensor_reduce(slot[:, :], picked[:, :].rearrange("p (t e) -> p t e", e=E), AX.X, ALU.add).then_inc(s_slot, 1)
            dve.wait_ge(s_slot, 3)
            nc.vector.tensor_copy(slot_of[:, :], slot[:, :]).then_inc(s_slot, 1)
            nc.vector.tensor_tensor(past[:, :, :], tile_no[:, :].unsqueeze(2).broadcast_to([P, SLOT_TILES, E]),
                                    ends[:, 1:E + 1].unsqueeze(1).broadcast_to([P, SLOT_TILES, E]), ALU.is_ge).then_inc(s_slot, 1)
            dve.wait_ge(s_slot, 5)
            nc.vector.tensor_reduce(past_n[:, :], past[:, :, :], AX.X, ALU.add).then_inc(s_slot, 1)
            dve.wait_ge(s_slot, 6)
            nc.vector.tensor_scalar(expert[:, :], past_n[:, :], float(E - 1), None, ALU.min).then_inc(s_slot, 1)
            dve.wait_ge(s_slot, 7)
            nc.vector.tensor_copy(expert_of[:, :], expert[:, :]).then_inc(s_slot, 1)

        @block.gpsimd
        def _(pool):
            pool.wait_ge(s_slot, 4)
            pool.wait_ge(s_zeroed, 16)
            for k in range(TOPK):
                for t in range(TT):
                    c = k * TT + t
                    pool.indirect_dma_start(slots_in[:, :], bass.IndirectOffsetOnAxis(slot_of[:, c:c + 1], 0),
                                            xn[:, t, :], None).then_inc(s_scattered, 16)


def experts(nc, a, sem, sb, banks, ident, expert_of, w2, s_w2, slots_in, slots_out, s_scattered):
    RING3 = 3
    with ExitStack() as ctx:
        w1 = [sb(ctx, f"w1_{i}", [P, W1_ROW]) for i in range(RING3)]
        b2 = [sb(ctx, f"b2_{i}", [P, D]) for i in range(RING3)]
        xs = [sb(ctx, f"xs{i}", [P, D]) for i in range(RING3)]
        xT = [sb(ctx, f"xT{i}", [P, DK, P]) for i in range(RING3)]
        hT = [sb(ctx, f"hT{i}", [P, FB, P]) for i in range(RING3)]
        ys = [sb(ctx, f"ys{i}", [P, D]) for i in range(RING3)]
        px = banks(ctx, "px", 1)[0]
        ph = banks(ctx, "ph", 2)
        py = banks(ctx, "py", 1)[0]
        s_xs = [sem(f"s_moexs{i}") for i in range(RING3)]
        s_w1 = [sem(f"s_moew1{i}") for i in range(RING3)]
        s_b2 = [sem(f"s_moeb2{i}") for i in range(RING3)]
        s_st = [sem(f"s_moest{i}") for i in range(RING3)]
        s_xt, s_xc, s_h, s_g, s_y, s_ye = (sem(f"s_moe{n}") for n in ("xt", "xc", "h", "g", "y", "ye"))
        HALF = FB // 2
        block = ctx.enter_context(nc.Block())

        def run(eng, first, last, step):
            for n in range(first, RING3):
                step(n, n % RING3, n // RING3)
            rounds = SLOT_TILES // RING3 - 1
            with eng.Fori(1, rounds) as it:
                for r in range(RING3):
                    step(it * RING3 + r, r, it)
            for n in range(rounds * RING3, last + 1):
                step(n, n % RING3, n // RING3)

        def tile_at(n, r, it, ahead):
            if isinstance(n, int) and not 0 <= n + ahead < SLOT_TILES:
                return None
            return n + ahead, (r + ahead) % RING3, it + (r + ahead) // RING3

        def rows_of(n):
            return bass.ds(n * P, P)

        @block.sync
        def _(sp):
            sp.wait_ge(s_scattered, 16 * TOPK * TT)

            def step(n, r, it):
                if h := tile_at(n, r, it, 2):
                    m, i, turn = h
                    e = sp.value_load(expert_of[0:1, bass.ds(m, 1)], min_val=0, max_val=E - 1)
                    wait(sp, s_g, 2 * (m - 2))
                    sp.dma_start(xs[i][:, :], slots_in[rows_of(m), :]).then_inc(s_xs[i], 16)
                    sp.dma_start(w1[i][:, :], a["w1p"][bass.ds(e, 1), :, :].rearrange("a p w -> p (a w)")).then_inc(s_w1[i], 16)
            run(sp, -2, SLOT_TILES - 1, step)

        @block.gpsimd
        def _(pool):
            def step(n, r, it):
                if h := tile_at(n, r, it, -1):
                    m, i, turn = h
                    pool.wait_ge(s_ye, m + 1)
                    pool.dma_start(slots_out[rows_of(m), :], ys[i][:, :]).then_inc(s_st[i], 16)
                if h := tile_at(n, r, it, 2):
                    m, i, turn = h
                    e = pool.value_load(expert_of[0:1, bass.ds(m, 1)], min_val=0, max_val=E - 1)
                    pool.dma_start(b2[i][:, :], a["b2"][bass.ds(e, 1), :].broadcast_to([P, D])).then_inc(s_b2[i], 16)
            run(pool, -2, SLOT_TILES, step)
            for i in range(RING3):
                pool.wait_ge(s_st[i], 16 * (SLOT_TILES // RING3))

        @block.tensor
        def _(pe):
            pe.wait_ge(s_w2, 16 * E)

            def step(n, r, it):
                if h := tile_at(n, r, it, 1):
                    m, i, turn = h
                    pe.wait_ge(s_xs[i], 16 * (turn + 1))
                    wait(pe, s_xc, m)
                    for dk in range(DK):
                        tr = nc.tensor.transpose(px[:, dk * P:(dk + 1) * P], xs[i][:, dk * P:(dk + 1) * P], ident[:, :])
                    tr.then_inc(s_xt, 1)
                if h := tile_at(n, r, it, 0):
                    m, i, turn = h
                    pe.wait_ge(s_xc, m + 1)
                    pe.wait_ge(s_w1[i], 16 * (turn + 1))
                    for half in range(2):
                        wait(pe, s_g, 2 * (m - 1) + half + 1)
                        for q in range(HALF):
                            f = half * HALF + q
                            for dk in range(DK):
                                mm = nc.tensor.matmul(ph[half][:, q * P:(q + 1) * P],
                                                      w1[i][:, dk * F + f * P:dk * F + (f + 1) * P], xT[i][:, dk, :],
                                                      start=(dk == 0), stop=(dk == DK - 1))
                        mm.then_inc(s_h, 1)
                if h := tile_at(n, r, it, -1):
                    m, i, turn = h
                    e = pe.value_load(expert_of[0:1, bass.ds(m, 1)], min_val=0, max_val=E - 1)
                    pe.wait_ge(s_g, 2 * (m + 1))
                    wait(pe, s_ye, m)
                    for f in range(FB):
                        mm = nc.tensor.matmul(py[:, 0:D], hT[i][:, f, :],
                                              w2[:, bass.ds(e, 1), f * D:(f + 1) * D].rearrange("p a d -> p (a d)"),
                                              start=(f == 0), stop=(f == FB - 1))
                    mm.then_inc(s_y, 1)
            run(pe, -1, SLOT_TILES, step)

        @block.scalar
        def _(act):
            def step(n, r, it):
                if h := tile_at(n, r, it, 0):
                    m, i, turn = h
                    wait(act, s_y, m - 2)
                    for half in range(2):
                        act.wait_ge(s_h, 2 * m + half + 1)
                        for q in range(HALF):
                            f = half * HALF + q
                            g = nc.scalar.activation(hT[i][:, f, :], ph[half][:, q * P:(q + 1) * P], ACT.Gelu,
                                                     bias=w1[i][:, DK * F + f:DK * F + f + 1])
                        g.then_inc(s_g, 1)
            run(act, 0, SLOT_TILES - 1, step)

        @block.vector
        def _(dve):
            def step(n, r, it):
                if h := tile_at(n, r, it, 1):
                    m, i, turn = h
                    dve.wait_ge(s_xt, m + 1)
                    wait(dve, s_h, 2 * (m - 2))
                    nc.vector.tensor_copy(xT[i][:, :, :].rearrange("p k t -> p (k t)"), px[:, 0:D]).then_inc(s_xc, 1)
                if h := tile_at(n, r, it, -1):
                    m, i, turn = h
                    dve.wait_ge(s_y, m + 1)
                    if not isinstance(m, int) or m >= RING3:
                        dve.wait_ge(s_st[i], 16 * turn)
                    dve.wait_ge(s_b2[i], 16 * (turn + 1))
                    nc.vector.tensor_tensor(ys[i][:, :], py[:, 0:D], b2[i][:, :], ALU.add).then_inc(s_ye, 1)
            run(dve, -1, SLOT_TILES, step)


def combine(nc, sem, sb, x, prob, slot_of, slots_out):
    with ExitStack() as ctx:
        got = sb(ctx, "got", [P, TT, TOPK, D])
        s_got = [sem(f"s_got{i}") for i in range(TT)]
        s_x = sem("s_combined")
        block = ctx.enter_context(nc.Block())

        @block.gpsimd
        def _(pool):
            for t in range(TT):
                for k in range(TOPK):
                    c = k * TT + t
                    pool.indirect_dma_start(got[:, t, k, :], None, slots_out[:, :],
                                            bass.IndirectOffsetOnAxis(slot_of[:, c:c + 1], 0)).then_inc(s_got[t], 16)

        @block.vector
        def _(dve):
            for t in range(TT):
                dve.wait_ge(s_got[t], 16 * TOPK)
                for k in range(TOPK):
                    wait(dve, s_x, TOPK * t + k)
                    nc.vector.scalar_tensor_tensor(out=x[:, t, :], in0=got[:, t, k, :], scalar=prob[:, k, t:t + 1],
                                                   in1=x[:, t, :], op0=ALU.mult, op1=ALU.add).then_inc(s_x, 1)


def ffn(nc, a, sem, sb, banks, x, xn, ident, out):
    with ExitStack() as ctx:
        wq = [sb(ctx, f"wq{n}", [P, 2 * F], BF16) for n in range(3)]
        ws = sb(ctx, "ws", [P, 3])
        identb = sb(ctx, "identb", [P, P], BF16)
        with ExitStack() as c1:
            w = [sb(c1, f"wf{n}", [P, 2 * F]) for n in range(3)]
            r1 = sb(c1, "wr1", [P, 2 * F])
            r2 = sb(c1, "wr2", [P, 2 * F])
            asum = sb(c1, "asum", [P, 3])
            scale = sb(c1, "wscale", [P, 3])
            ones = sb(c1, "onesPP", [P, P])
            pm = banks(c1, "pm", 1)[0]
            s_w = [sem(f"s_fw{n}") for n in range(3)]
            s_one, s_sum, s_mm, s_sc, s_q = (sem(f"s_f{n}") for n in ("one", "sum", "mm", "sc", "q"))
            block = c1.enter_context(nc.Block())

            @block.sync
            def _(sp):
                for n, name in enumerate(("gateT", "upT", "downT")):
                    free = F if n < 2 else D
                    sp.dma_start(w[n][:, :].rearrange("p (k f) -> p k f", f=free),
                                 a[name].rearrange("(k p) f -> p k f", p=P)).then_inc(s_w[n], 16)

            @block.tensor
            def _(pe):
                pe.wait_ge(s_one, 1)
                pe.wait_ge(s_sum, 3)
                nc.tensor.matmul(pm[:, 0:3], ones[:, :], asum[:, :], start=True, stop=True).then_inc(s_mm, 1)

            @block.vector
            def _(dve):
                nc.vector.memset(ones[:, :], 1.0).then_inc(s_one, 1)
                nc.vector.tensor_copy(identb[:, :], ident[:, :])
                for n in range(3):
                    dve.wait_ge(s_w[n], 16)
                    nc.vector.tensor_reduce(asum[:, n:n + 1], w[n][:, :], AX.X, ALU.add, apply_absolute_value=True).then_inc(s_sum, 1)
                dve.wait_ge(s_mm, 1)
                nc.vector.tensor_scalar(ws[:, :], pm[:, 0:3], 1.0 / (F * D), 1e-5, ALU.mult, ALU.max).then_inc(s_sc, 1)
                dve.wait_ge(s_sc, 1)
                nc.vector.reciprocal(scale[:, :], ws[:, :]).then_inc(s_sc, 1)
                dve.wait_ge(s_sc, 2)
                for n in range(3):
                    nc.vector.tensor_scalar(r1[:, :], w[n][:, :], scale[:, n:n + 1], MAGIC, ALU.mult, ALU.add).then_inc(s_q, 1)
                    dve.wait_ge(s_q, 3 * n + 1)
                    nc.vector.tensor_scalar(r2[:, :], r1[:, :], MAGIC, 1.0, ALU.subtract, ALU.min).then_inc(s_q, 1)
                    dve.wait_ge(s_q, 3 * n + 2)
                    nc.vector.tensor_scalar(wq[n][:, :], r2[:, :], -1.0, None, ALU.max).then_inc(s_q, 1)
                    dve.wait_ge(s_q, 3 * n + 3)

        gq = wq[0][:, :].rearrange("p (k f) -> p k f", f=F)
        uq = wq[1][:, :].rearrange("p (k f) -> p k f", f=F)
        dq = wq[2][:, :].rearrange("p (k d) -> p k d", d=D)
        am = sb(ctx, "am", [P, TT])
        sx = sb(ctx, "sx", [P, TT])
        gs = sb(ctx, "gs", [P, TT])
        us = sb(ctx, "us", [P, TT])
        ys = sb(ctx, "ys", [P, TT])
        inv = sb(ctx, "inv", [P, TT])
        r = sb(ctx, "rq", [P, TT, D])
        xq = sb(ctx, "xq", [P, TT, D], BF16)
        xqT = sb(ctx, "xqT", [P, DK, TOK], BF16)
        g = [sb(ctx, f"g{i}", [P, F]) for i in range(2)]
        hh = [sb(ctx, f"hh{i}", [P, F]) for i in range(2)]
        hr = [sb(ctx, f"hr{i}", [P, F]) for i in range(2)]
        hq = [sb(ctx, f"hq{i}", [P, F], BF16) for i in range(2)]
        hqT = [sb(ctx, f"hqT{i}", [P, F], BF16) for i in range(2)]
        y = [sb(ctx, f"y{i}", [P, D]) for i in range(2)]
        ha = sb(ctx, "ha", [P, TT])
        hm = sb(ctx, "hm", [P, TT])
        hs = sb(ctx, "hs", [P, TT])
        pg = banks(ctx, "pg", 2)
        pu = banks(ctx, "pu", 2)
        ptx = [ctx.enter_context(nc.psum_tensor(f"ptx{i}", [P, F], BF16)) for i in range(2)]
        py = banks(ctx, "pfy", 2)
        s_a, s_s, s_r, s_xq, s_tr, s_ev = (sem(f"s_g{n}") for n in ("a", "s", "r", "xq", "tr", "ev"))
        s_g, s_u, s_si, s_h, s_ha, s_hs, s_hr, s_hq, s_ht, s_he, s_y, s_o = (
            sem(f"s_h{n}") for n in ("g", "u", "si", "h", "ha", "hs", "hr", "hq", "ht", "he", "y", "o"))
        s_st = [sem(f"s_st{i}") for i in range(2)]
        block = ctx.enter_context(nc.Block())
        out_v = out.rearrange("b (i p) d -> (b i) p d", p=P)

        def finish(dve, t):
            i = t % 2
            dve.wait_ge(s_y, t + 1)
            if t >= 2:
                dve.wait_ge(s_st[i], 16 * (t // 2))
            nc.vector.scalar_tensor_tensor(out=y[i][:, :], in0=py[i][:, 0:D], scalar=ys[:, t:t + 1], in1=x[:, t, :],
                                           op0=ALU.mult, op1=ALU.add).then_inc(s_o, 1)

        @block.vector
        def _(dve):
            for t in range(TT):
                nc.vector.tensor_reduce(am[:, t:t + 1], xn[:, t, :], AX.X, ALU.max, apply_absolute_value=True).then_inc(s_a, 1)
            dve.wait_ge(s_a, TT)
            nc.vector.tensor_scalar(sx[:, :], am[:, :], 1e-5, None, ALU.max).then_inc(s_s, 1)
            dve.wait_ge(s_s, 1)
            nc.vector.reciprocal(inv[:, :], sx[:, :]).then_inc(s_s, 1)
            nc.vector.tensor_scalar(gs[:, :], sx[:, :], ws[:, 0:1], 1.0 / 127, ALU.mult, ALU.mult).then_inc(s_s, 1)
            nc.vector.tensor_scalar(us[:, :], sx[:, :], ws[:, 1:2], 1.0 / 127, ALU.mult, ALU.mult).then_inc(s_s, 1)
            dve.wait_ge(s_s, 4)
            nc.vector.tensor_scalar(sx[:, :], inv[:, :], 127.0, None, ALU.mult).then_inc(s_s, 1)
            dve.wait_ge(s_s, 5)
            for t in range(TT):
                nc.vector.tensor_scalar(r[:, t, :], xn[:, t, :], sx[:, t:t + 1], MAGIC, ALU.mult, ALU.add).then_inc(s_r, 1)
            for t in range(TT):
                dve.wait_ge(s_r, t + 1)
                nc.vector.tensor_scalar(xq[:, t, :], r[:, t, :], MAGIC, None, ALU.subtract).then_inc(s_xq, 1)
            for t in range(TT):
                i = t % 2
                for n in range(2):
                    c = slice(n * 512, (n + 1) * 512)
                    dve.wait_ge(s_si, 2 * t + n + 1)
                    dve.wait_ge(s_u, 2 * t + n + 1)
                    nc.vector.scalar_tensor_tensor(out=hh[i][:, c], in0=pu[n][:, :], scalar=us[:, t:t + 1], in1=g[i][:, c],
                                                   op0=ALU.mult, op1=ALU.mult).then_inc(s_h, 1)
                dve.wait_ge(s_h, 2 * (t + 1))
                nc.vector.tensor_reduce(ha[:, t:t + 1], hh[i][:, :], AX.X, ALU.max, apply_absolute_value=True).then_inc(s_ha, 1)
                dve.wait_ge(s_ha, t + 1)
                nc.vector.tensor_scalar(hm[:, t:t + 1], ha[:, t:t + 1], 1e-5, None, ALU.max).then_inc(s_hs, 1)
                dve.wait_ge(s_hs, 4 * t + 1)
                nc.vector.reciprocal(ha[:, t:t + 1], hm[:, t:t + 1]).then_inc(s_hs, 1)
                nc.vector.tensor_scalar(ys[:, t:t + 1], hm[:, t:t + 1], ws[:, 2:3], 1.0 / 127, ALU.mult, ALU.mult).then_inc(s_hs, 1)
                dve.wait_ge(s_hs, 4 * t + 2)
                nc.vector.tensor_scalar(hs[:, t:t + 1], ha[:, t:t + 1], 127.0, None, ALU.mult).then_inc(s_hs, 1)
                dve.wait_ge(s_hs, 4 * t + 4)
                nc.vector.tensor_scalar(hr[i][:, :], hh[i][:, :], hs[:, t:t + 1], MAGIC, ALU.mult, ALU.add).then_inc(s_hr, 1)
                dve.wait_ge(s_hr, t + 1)
                wait(dve, s_ht, t - 1)
                nc.vector.tensor_scalar(hq[i][:, :], hr[i][:, :], MAGIC, None, ALU.subtract).then_inc(s_hq, 1)
                if t >= 1:
                    finish(dve, t - 1)
            finish(dve, TT - 1)

        @block.sync
        def _(sp):
            for t in range(TT):
                sp.wait_ge(s_o, t + 1)
                sp.dma_start(out_v[t], y[t % 2][:, :]).then_inc(s_st[t % 2], 16)
            for i in range(2):
                sp.wait_ge(s_st[i], 16 * TT // 2)

        @block.tensor
        def _(pe):
            for c in range(B):
                pe.wait_ge(s_xq, NI * (c + 1))
                wait(pe, s_ev, c - 1)
                for dk in range(DK):
                    for j in range(NI):
                        tr = nc.tensor.transpose(ptx[c % 2][:, (dk * NI + j) * P:(dk * NI + j + 1) * P],
                                                 xq[:, c * NI + j, dk * P:(dk + 1) * P], identb[:, :])
                tr.then_inc(s_tr, 1)

            def gate_up(t):
                pe.wait_ge(s_ev, t // NI + 1)
                if t == 0:
                    pe.wait_ge(s_ev, B)
                for n in range(2):
                    wait(pe, s_si, 2 * (t - 1) + n + 1)
                    for dk in range(DK):
                        mm = nc.tensor.matmul(pg[n][:, :], xqT[:, dk, t * P:(t + 1) * P], gq[:, dk, n * 512:(n + 1) * 512],
                                              start=(dk == 0), stop=(dk == DK - 1))
                    mm.then_inc(s_g, 1)
                    wait(pe, s_h, 2 * (t - 1) + n + 1)
                    for dk in range(DK):
                        mm = nc.tensor.matmul(pu[n][:, :], xqT[:, dk, t * P:(t + 1) * P], uq[:, dk, n * 512:(n + 1) * 512],
                                              start=(dk == 0), stop=(dk == DK - 1))
                    mm.then_inc(s_u, 1)

            gate_up(0)
            for t in range(TT):
                i = t % 2
                if t + 1 < TT:
                    gate_up(t + 1)
                pe.wait_ge(s_hq, t + 1)
                wait(pe, s_he, t - 1)
                for f in range(FB):
                    tr = nc.tensor.transpose(ptx[i][:, f * P:(f + 1) * P], hq[i][:, f * P:(f + 1) * P], identb[:, :])
                tr.then_inc(s_ht, 1)
                pe.wait_ge(s_he, t + 1)
                wait(pe, s_o, t - 1)
                for f in range(FB):
                    mm = nc.tensor.matmul(py[i][:, 0:D], hqT[i][:, f * P:(f + 1) * P], dq[:, f, :],
                                          start=(f == 0), stop=(f == FB - 1))
                mm.then_inc(s_y, 1)

        @block.scalar
        def _(act):
            for c in range(B):
                act.wait_ge(s_tr, c + 1)
                nc.scalar.copy(xqT[:, :, c * S:(c + 1) * S], ptx[c % 2][:, :].rearrange("p (k s) -> p k s", s=S)).then_inc(s_ev, 1)
            act.wait_ge(s_s, 3)

            def hidden_out(t):
                act.wait_ge(s_ht, t + 1)
                wait(act, s_y, t - 1)
                nc.scalar.copy(hqT[t % 2][:, :], ptx[t % 2][:, :]).then_inc(s_he, 1)

            for t in range(TT):
                wait(act, s_h, 2 * (t - 1))
                for n in range(2):
                    act.wait_ge(s_g, 2 * t + n + 1)
                    nc.scalar.activation(g[t % 2][:, n * 512:(n + 1) * 512], pg[n][:, :], ACT.Silu,
                                         scale=gs[:, t:t + 1]).then_inc(s_si, 1)
                if t >= 1:
                    hidden_out(t - 1)
            hidden_out(TT - 1)


def kernel(**inputs):
    import numpy as np
    import concourse.bacc as bacc
    from concourse.bass_utils import run_bass_kernel_spmd

    g = {n: np.asarray(v) for n, v in inputs.items()}
    t = lambda v: np.ascontiguousarray(np.swapaxes(v, -1, -2))
    cols = lambda v: np.ascontiguousarray(np.swapaxes(v.reshape(*v.shape[:-1], -1, P), -1, -2))
    by_partition = lambda v: np.ascontiguousarray(np.swapaxes(v.reshape(E, -1, P, v.shape[-1]), 1, 2).reshape(E, P, -1))
    arrays = {
        "x": g["x"],
        "ctxT": t(g["ctx_1024"].reshape(TOK, D)),
        "mask": g["mask_1x1xSxS2_ik0"], "maskT": t(g["mask_1x1xSxS2_ik0"]),
        "above": np.triu(np.ones((P, P), np.float32), 1),
        "ident": np.eye(P, dtype=np.float32),
        "iota": np.ascontiguousarray(np.broadcast_to(np.arange(E, dtype=np.float32), (P, E))),
        "L0_WqT": t(g["L0_xattn_Wq"]), "L0_WkT": t(g["L0_xattn_Wk"]), "L0_WvT": t(g["L0_xattn_Wv"]),
        "L0_bq": cols(g["L0_xattn_bq"]), "L0_bk": cols(g["L0_xattn_bk"]), "L0_bv": g["L0_xattn_bv"],
        "ErT": t(g["L0_xattn_Er"]),
        "routerT": t(g["L0_ffn_router_w"]),
        "w1p": np.ascontiguousarray(np.concatenate([by_partition(t(g["L0_ffn_w1"])), cols(g["L0_ffn_b1"])], axis=-1)),
        "w2p": by_partition(t(g["L0_ffn_w2"])), "b2": g["L0_ffn_b2"],
        "tile_no": np.ascontiguousarray(np.broadcast_to(np.arange(SLOT_TILES, dtype=np.float32), (P, SLOT_TILES))),
        "same": np.tile(np.eye(E, dtype=np.float32), (TT, 1)),
        "prior": np.ascontiguousarray(np.kron(np.triu(np.ones((TOPK * TT,) * 2, np.float32), 1), np.eye(E, dtype=np.float32))
                                      .reshape(TOPK, P, TOPK * P).swapaxes(0, 1)),
        "L1_WqT": t(g["L1_xattn_w_q"]), "L1_WkT": t(g["L1_xattn_w_k"]), "L1_WvT": t(g["L1_xattn_w_v"]),
        "L1_WoT": t(g["L1_xattn_w_o"]),
        "gateT": t(g["L1_ffn_w_gate"]), "upT": t(g["L1_ffn_w_up"]), "downT": t(g["L1_ffn_w_down"]),
    }
    nc = bacc.Bacc("TRN2", target_bir_lowering=False, num_devices=1)
    aps = {n: nc.dram_tensor(f"in_{n}", v.shape, mybir.dt.from_np(v.dtype), kind="ExternalInput").ap()
           for n, v in arrays.items()}
    out = nc.dram_tensor("out", (B, S, D), F32, kind="ExternalOutput").ap()
    build(nc, aps, out)
    r = run_bass_kernel_spmd(nc, [{f"in_{n}": v for n, v in arrays.items()}], core_ids=[0])
    return r.results[0]["out"]
```

```python
from contextlib import ExitStack

import concourse.bass as bass
from concourse import mybir

ALU = mybir.AluOpType
ACT = mybir.ActivationFunctionType
AX = mybir.AxisListType
F32 = mybir.dt.float32
BF16 = mybir.dt.bfloat16
I32 = mybir.dt.int32
U32 = mybir.dt.uint32

P = 128
B, S, D = 4, 512, 256
TOK = B * S
TT = TOK // P
DK = D // P
HEADS, DH = 16, 16
NBH = B * HEADS
NI = S // P
E, F, TOPK = 8, 1024, 2
FB = F // P
SLOT_TILES = (TOK * TOPK + E * (P - 1)) // P
W1_ROW = DK * F + FB
NEG = -2.0 ** 100
LN_EPS = 1e-5
MAGIC = 1.5 * 2.0 ** 23
PIECES = 6
KP = PIECES * DH
RING = 4
GROUP = 4
ROUND = 2 * GROUP
VW = DH + 1
CG = 32
LQ, LK = (0, 0, 0, 1, 1, 2), (0, 1, 2, 0, 1, 0)

CAUSAL_UNITS = [[(3, 0, 512)], [(2, 0, 384), (0, 384, 128)], [(1, 0, 256)]]
CAUSAL_KEYS = [[(NI - 1 - i, off, w) for i, off, w in unit] for unit in CAUSAL_UNITS]


def wait(eng, sem, value):
    if isinstance(value, int) and value <= 0:
        return
    eng.wait_ge(sem, value)


def build(nc, a, out):
    top = ExitStack()

    def dram(name, shape, dt):
        return nc.dram_tensor(name, shape, dt)

    packed = dram("packed", (PIECES, B, D, 2, S), BF16)
    REL_W = sum(w for unit in CAUSAL_UNITS for _, _, w in unit)
    slots_in = dram("slots_in", (SLOT_TILES * P, D), F32)
    slots_out = dram("slots_out", (SLOT_TILES * P, D), F32)
    rel = [dram(f"rel_{r}", (P, REL_W), F32) for r in range(RING)]

    with top:
        def sem(name):
            return nc.alloc_semaphore(name)

        def sb(ctx, name, shape, dt=F32):
            return ctx.enter_context(nc.sbuf_tensor(name, shape, dt))

        def banks(ctx, name, n, dt=F32):
            return [ctx.enter_context(nc.psum_tensor(f"{name}{i}", [P, 512], dt)) for i in range(n)]

        x = sb(top, "x", [P, TT, D])
        xn = sb(top, "xn", [P, TT, D])
        xnT = sb(top, "xnT", [P, DK, TOK])
        ident = sb(top, "ident", [P, P])
        s_zeroed = sem("s_zeroed")
        s_const = sem("s_const")
        s_ctx = [sem(f"s_ctx{i}") for i in range(2)]

        class LayerNorm:

            def __init__(self, ctx, tag, calls=1, transposed=True, on_scalar=False):
                self.tiles = TT // calls
                self.stats_ = sb(ctx, f"stats{tag}", [P, TT, 6])
                self.mv = sb(ctx, f"mv{tag}", [P, TT, 2])
                self.ve, self.sd, self.rs, self.t1, self.t2 = (
                    sb(ctx, f"{n}{tag}", [P, TT]) for n in ("ve", "sd", "rs", "t1", "t2"))
                self.ps = banks(ctx, f"lnps{tag}", 2) if transposed else None
                self.s_stat, self.s_var, self.s_sd, self.s_rs = (sem(f"s_{n}{tag}") for n in ("stat", "var", "sd", "rs"))
                self.s_xn, self.s_tr, self.s_ev = (sem(f"s_{n}{tag}") for n in ("xn", "tr", "ev"))
                self.shift = sb(ctx, f"shift{tag}", [P, TT]) if on_scalar else None
                self.s_shift = sem(f"s_shift{tag}") if on_scalar else None

            def stats(self, dve, t):
                nc.vector.bn_stats(self.stats_[:, t, :], x[:, t, :]).then_inc(self.s_stat, 1)

            def norm(self, dve, c):
                ts = range(c * self.tiles, (c + 1) * self.tiles)
                part = slice(ts.start, ts.stop)
                ve, sd, rs, t1, t2 = (v[:, part] for v in (self.ve, self.sd, self.rs, self.t1, self.t2))
                for t in ts:
                    dve.wait_ge(self.s_stat, t + 1)
                    agg = nc.vector.bn_aggr(self.mv[:, t, :], self.stats_[:, t, :])
                agg.then_inc(self.s_var, 1)
                dve.wait_ge(self.s_var, 2 * c + 1)
                nc.vector.tensor_scalar(ve, self.mv[:, part, 1], LN_EPS, None, ALU.add).then_inc(self.s_var, 1)
                dve.wait_ge(self.s_sd, c + 1)
                nc.vector.reciprocal(rs, sd).then_inc(self.s_rs, 1)
                dve.wait_ge(self.s_rs, 5 * c + 1)
                nc.vector.tensor_tensor(t1, rs, rs, ALU.mult).then_inc(self.s_rs, 1)
                dve.wait_ge(self.s_rs, 5 * c + 2)
                nc.vector.tensor_tensor(t2, t1, ve, ALU.mult).then_inc(self.s_rs, 1)
                dve.wait_ge(self.s_rs, 5 * c + 3)
                nc.vector.tensor_scalar(t1, t2, -0.5, 1.5, ALU.mult, ALU.add).then_inc(self.s_rs, 1)
                dve.wait_ge(self.s_rs, 5 * c + 4)
                nc.vector.tensor_tensor(sd, t1, rs, ALU.mult).then_inc(self.s_rs, 1)
                if self.shift is not None:
                    return
                dve.wait_ge(self.s_rs, 5 * c + 5)
                for t in ts:
                    nc.vector.tensor_scalar(xn[:, t, :], x[:, t, :], self.mv[:, t, 0:1], self.sd[:, t:t + 1],
                                            ALU.subtract, ALU.mult).then_inc(self.s_xn, 1)

            def shifts(self, dve, c):
                part = slice(c * self.tiles, (c + 1) * self.tiles)
                dve.wait_ge(self.s_rs, 5 * c + 5)
                nc.vector.scalar_tensor_tensor(out=self.shift[:, part], in0=self.mv[:, part, 0], scalar=-1.0,
                                               in1=self.sd[:, part], op0=ALU.mult, op1=ALU.mult).then_inc(self.s_shift, 1)

            def apply(self, act, c):
                act.wait_ge(self.s_shift, c + 1)
                for t in range(c * self.tiles, (c + 1) * self.tiles):
                    nc.scalar.activation(xn[:, t, :], x[:, t, :], ACT.Identity, bias=self.shift[:, t:t + 1],
                                         scale=self.sd[:, t:t + 1]).then_inc(self.s_xn, 1)

            def root(self, act, c):
                part = slice(c * self.tiles, (c + 1) * self.tiles)
                act.wait_ge(self.s_var, 2 * c + 2)
                nc.scalar.activation(self.sd[:, part], self.ve[:, part], ACT.Sqrt).then_inc(self.s_sd, 1)

            def turn(self, pe, b):
                pe.wait_ge(self.s_xn, NI * (b + 1))
                for dk in range(DK):
                    wait(pe, self.s_ev, DK * b + dk - 1)
                    for j in range(NI):
                        tr = nc.tensor.transpose(self.ps[dk][:, j * P:(j + 1) * P],
                                                 xn[:, b * NI + j, dk * P:(dk + 1) * P], ident[:, :])
                    tr.then_inc(self.s_tr, 1)

            def copy(self, act, b):
                for dk in range(DK):
                    act.wait_ge(self.s_tr, DK * b + dk + 1)
                    nc.scalar.copy(xnT[:, dk, b * S:(b + 1) * S], self.ps[dk][:, :]).then_inc(self.s_ev, 1)

        class PieceProjection:
            PARTS = B * DK

            def __init__(self, ctx, tag, side, src, w, bias, depth):
                self.depth = depth
                self.side, self.src, self.w_, self.bias_ = side, src, w, bias
                self.w = sb(ctx, f"w{tag}", [P, DK, D])
                self.bias = sb(ctx, f"bias{tag}", [P, DK])
                self.full = sb(ctx, f"full{tag}", [P, depth, S])
                self.rest = sb(ctx, f"rest{tag}", [P, depth, S])
                self.pieces = sb(ctx, f"pieces{tag}", [P, depth, 3, S], BF16)
                self.ps = banks(ctx, f"prps{tag}", 2)
                self.s_w, self.s_mm, self.s_full, self.s_r1, self.s_p2, self.s_p3 = (
                    sem(f"s_{n}{tag}") for n in ("w", "mm", "full", "r1", "p2", "p3"))
                self.s_out = [sem(f"s_pout{tag}{i}") for i in range(depth)]

            def load(self, sp):
                sp.dma_start(self.w[:, :, :], self.w_.rearrange("(k p) e -> p k e", p=P)).then_inc(self.s_w, 16)
                if self.bias_ is not None:
                    sp.dma_start(self.bias[:, :], self.bias_).then_inc(self.s_w, 16)

            def wait_load(self, eng):
                eng.wait_ge(self.s_w, 16 if self.bias_ is None else 32)

            def product(self, pe, g):
                b, eh = divmod(g, DK)
                if g == 0:
                    self.wait_load(pe)
                wait(pe, self.s_full, g - 1)
                for dk in range(DK):
                    mm = nc.tensor.matmul(self.ps[g % 2][:, :], self.w[:, dk, eh * P:(eh + 1) * P],
                                          self.src[:, dk, b * S:(b + 1) * S], start=(dk == 0), stop=(dk == DK - 1))
                mm.then_inc(self.s_mm, 1)

            def copies(self, act, g):
                act.wait_ge(self.s_mm, g + 1)
                k = g % self.depth
                wait(act, self.s_p3, g + 1 - self.depth)
                if g >= self.depth:
                    act.wait_ge(self.s_out[k], 3 * 16 * (g // self.depth))
                if self.bias_ is not None:
                    bias = self.bias[:, g % DK:g % DK + 1]
                    nc.scalar.activation(self.full[:, k, :], self.ps[g % 2][:, :], ACT.Identity, bias=bias)
                    nc.scalar.activation(self.pieces[:, k, 0, :], self.ps[g % 2][:, :], ACT.Identity,
                                         bias=bias).then_inc(self.s_full, 1)
                else:
                    nc.scalar.copy(self.full[:, k, :], self.ps[g % 2][:, :])
                    nc.scalar.copy(self.pieces[:, k, 0, :], self.ps[g % 2][:, :]).then_inc(self.s_full, 1)

            def split(self, dve, g):
                k = g % self.depth
                dve.wait_ge(self.s_full, g + 1)
                nc.vector.tensor_tensor(self.rest[:, k, :], self.full[:, k, :], self.pieces[:, k, 0, :],
                                        ALU.subtract).then_inc(self.s_r1, 1)
                dve.wait_ge(self.s_r1, g + 1)
                nc.vector.tensor_copy(self.pieces[:, k, 1, :], self.rest[:, k, :]).then_inc(self.s_p2, 1)
                dve.wait_ge(self.s_p2, g + 1)
                nc.vector.tensor_tensor(self.pieces[:, k, 2, :], self.rest[:, k, :], self.pieces[:, k, 1, :],
                                        ALU.subtract).then_inc(self.s_p3, 1)

            def store(self, sp, g):
                b, eh = divmod(g, DK)
                rows = packed[:, b, eh * P:(eh + 1) * P, self.side, :].rearrange("g e s -> e g s")
                have = self.pieces[:, g % self.depth, :, :]
                first = [have[:, 0:3, :], have[:, 0:2, :], have[:, 0:1, :]] if self.side else [
                    have[:, 0:1, :].broadcast_to([P, 3, S]), have[:, 1:2, :].broadcast_to([P, 2, S]), have[:, 2:3, :]]
                sp.wait_ge(self.s_p3, g + 1)
                for at, src in zip((0, 3, 5), first):
                    sp.dma_start(rows[:, at:at + src.shape[1], :], src).then_inc(self.s_out[g % self.depth], 16)

            def stored(self, sp):
                for i in range(self.depth):
                    sp.wait_ge(self.s_out[i], 3 * 16 * self.PARTS // self.depth)

        class ValueProjection:

            def __init__(self, ctx, tag, ctxT, V, w, bias):
                self.ctxT, self.V, self.w_, self.bias_ = ctxT, V, w, bias
                self.w = sb(ctx, f"wv{tag}", [P, DK, D])
                self.bias = sb(ctx, f"bv{tag}", [P, D])
                self.ps = banks(ctx, f"pvps{tag}", 2)
                self.s_w, self.s_mm, self.s_ev = (sem(f"s_v{n}{tag}") for n in ("w", "mm", "ev"))

            def load(self, sp):
                sp.dma_start(self.w[:, :, :], self.w_.rearrange("(k p) e -> p k e", p=P)).then_inc(self.s_w, 16)
                if self.bias_ is not None:
                    sp.dma_start(self.bias[:, :], bass.AP(self.bias_.tensor, 0, [[0, P], [1, D]])).then_inc(self.s_w, 16)

            def wait_load(self, eng):
                eng.wait_ge(self.s_w, 16 if self.bias_ is None else 32)

            def product(self, pe, t):
                if t == 0:
                    self.wait_load(pe)
                wait(pe, self.s_ev, t - 1)
                for dk in range(DK):
                    mm = nc.tensor.matmul(self.ps[t % 2][:, 0:D], self.ctxT[:, dk, t * P:(t + 1) * P], self.w[:, dk, :],
                                          start=(dk == 0), stop=(dk == DK - 1))
                mm.then_inc(self.s_mm, 1)

            def out(self, dve, t):
                dve.wait_ge(self.s_mm, t + 1)
                b, j = divmod(t, NI)
                to = self.V[:, b * HEADS:(b + 1) * HEADS, j, 0:DH]
                src = self.ps[t % 2][:, 0:D].rearrange("p (h d) -> p h d", d=DH)
                if self.bias_ is not None:
                    nc.vector.tensor_tensor(to, src, self.bias[:, :].rearrange("p (h d) -> p h d", d=DH),
                                            ALU.add).then_inc(self.s_ev, 1)
                else:
                    nc.vector.tensor_copy(to, src).then_inc(self.s_ev, 1)

        def run_heads(eng, first, last, step):
            for n in range(first, ROUND):
                step(n, n % ROUND, n // ROUND)
            rounds = NBH // ROUND - 2
            with eng.Fori(1, rounds + 1) as it:
                for r in range(ROUND):
                    step(it * ROUND + r, r, it)
            for n in range((rounds + 1) * ROUND, last + 1):
                step(n, n % ROUND, n // ROUND)

        def stage_of(n, r, it, ahead):
            if isinstance(n, int) and not 0 <= n + ahead < NBH:
                return None
            return n + ahead, (r + ahead) % RING, it * (ROUND // RING) + (r + ahead) // RING

        def group_of(n, r, it, back):
            g = it * (ROUND // GROUP) + (r // GROUP - back)
            if isinstance(n, int) and not 0 <= g < NBH // GROUP:
                return None
            return g, (r // GROUP - back) % 2

        def load_head(sp, m, dst, s_qk):
            sp.dma_start(dst, bass.AP(packed.ap().tensor, m * (DH * 2 * S),
                                      [[B * D * 2 * S, PIECES], [2 * S, DH], [1, 2 * S]])).then_inc(s_qk, 16)

        class Values:

            def __init__(self, ctx, tag):
                self.spread = [sb(ctx, f"spread{tag}{i}", [P, GROUP, NI, CG]) for i in range(2)]
                self.zeros = sb(ctx, f"zeros{tag}", [P, VW])
                self.heads = sb(ctx, f"heads{tag}", [P, S])
                self.rinv = sb(ctx, f"rinv{tag}", [P, 2, NI, GROUP])
                self.psO = banks(ctx, f"psO{tag}", 1)[0]
                self.psX = banks(ctx, f"psX{tag}", 1)[0]
                names = ("zero", "spread", "pv", "heads", "turned", "rinv", "o")
                (self.s_zero, self.s_spread, self.s_pv, self.s_heads, self.s_turned, self.s_rinv, self.s_o) = (
                    sem(f"s_{n}{tag}") for n in names)

            def clear(self, dve):
                for i in range(2):
                    nc.vector.memset(self.spread[i][:, :, :, :], 0.0).then_inc(self.s_zero, 1)
                nc.vector.memset(self.zeros[:, :], 0.0).then_inc(self.s_zero, 1)

            def spread_values(self, pool, g, par):
                wait(pool, self.s_pv, NI * (g - 1))
                wait(pool, self.s_spread, g)
                src = V[:, bass.ds(GROUP * g, GROUP), :, :]
                nc.gpsimd.tensor_tensor(self.spread[par][:, :, :, 0:VW].rearrange("p h j d -> p (h j) d"),
                                        src.rearrange("p h j d -> p (h j) d"),
                                        self.zeros[:, :].unsqueeze(1).broadcast_to([P, GROUP * NI, VW]),
                                        ALU.add).then_inc(self.s_spread, 1)

            def weigh(self, pe, g, par, j, s_prob, count, keys):
                if j == 0:
                    pe.wait_ge(self.s_spread, g + 1)
                    pe.wait_ge(s_prob, count)
                    wait(pe, self.s_heads, g)
                for h in range(GROUP):
                    probs = keys(h)
                    w = probs.shape[-1]
                    mm = nc.tensor.matmul(self.psO[h * CG:(h + 1) * CG, S - w:S], self.spread[par][:, h, j, :], probs,
                                          start=(j == 0), stop=(j == NI - 1))
                mm.then_inc(self.s_pv, 1)

            def copy_out(self, act, g, par):
                act.wait_ge(self.s_pv, NI * (g + 1))
                wait(act, self.s_turned, g)
                nc.scalar.copy(self.heads[:, :], self.psO[:, :]).then_inc(self.s_heads, 1)

            def turn(self, pe, g, par):
                pe.wait_ge(self.s_heads, g + 1)
                wait(pe, self.s_o, g)
                for i in range(NI):
                    tr = nc.tensor.transpose(self.psX[:, i * P:(i + 1) * P], self.heads[:, i * P:(i + 1) * P], ident[:, :])
                tr.then_inc(self.s_turned, 1)

            def divide(self, dve, g, par):
                dve.wait_ge(self.s_turned, g + 1)
                got = self.psX[:, :].rearrange("p (i h d) -> p i h d", h=GROUP, d=CG)
                nc.vector.reciprocal(self.rinv[:, par, :, :], got[:, :, :, DH]).then_inc(self.s_rinv, 1)
                dve.wait_ge(self.s_rinv, g + 1)
                nc.vector.tensor_tensor(attn[:, bass.ds(GROUP * g, GROUP), :, :].rearrange("p h i d -> p i h d"),
                                        got[:, :, :, 0:DH],
                                        self.rinv[:, par, :, :].unsqueeze(3).broadcast_to([P, NI, GROUP, DH]),
                                        ALU.mult).then_inc(self.s_o, 1)

        def causal_attention(ErP, identb, dmask):
            units = CAUSAL_UNITS
            NU = len(units)
            WU = [u[-1][1] + u[-1][2] for u in units]
            place = {i: (512 * u + off, w) for u, unit in enumerate(units) for i, off, w in unit}
            key_place = {j: (512 * u + off, w) for u, unit in enumerate(CAUSAL_KEYS) for j, off, w in unit}
            last = NBH + 2 * GROUP
            LOAD, REL, READ, SOFT, EXP = 6, 5, 3, 2, 1
            with ExitStack() as ctx:
                qk = [sb(ctx, f"qk{r}", [KP, 2 * S], BF16) for r in range(ROUND)]
                stage = [sb(ctx, f"stage{r}", [P, REL_W]) for r in range(2)]
                bias = [sb(ctx, f"bias{r}", [P, REL_W]) for r in range(RING)]
                scores = [sb(ctx, f"scores{r}", [P, REL_W]) for r in range(RING)]
                PT = [sb(ctx, f"PT{r}", [P, REL_W]) for r in range(ROUND)]
                mx = sb(ctx, "mx", [P, RING, NI])
                nm = sb(ctx, "nm", [P, RING, NI])
                vals = Values(ctx, "a")
                psE = banks(ctx, "psE", 2)
                psS = banks(ctx, "psS", 2)
                psT = banks(ctx, "psT", 2)
                s_qk = [sem(f"s_qk{r}") for r in range(ROUND)]
                s_wr = [sem(f"s_wr{r}") for r in range(RING)]
                s_rd = [sem(f"s_rd{r}") for r in range(RING)]
                names = ("emm", "eev", "smm", "soft", "nm", "exp", "tmm", "tev", "seen", "seensp")
                s_emm, s_eev, s_smm, s_soft, s_nm, s_exp, s_tmm, s_tev, s_seen, s_seen_sp = (
                    sem(f"s_{n}") for n in names)
                block = ctx.enter_context(nc.Block())

                @block.sync
                def _(sp):
                    def step(n, r, it):
                        if h := stage_of(n, r, it, READ):
                            m, slot, turn = h
                            sp.wait_ge(s_wr[slot], 16 * (turn + 1))
                            sp.sem_inc(s_seen_sp, 1)
                            wait(sp, s_soft, NU * (m - RING + 1))
                            skewed = bass.AP(rel[slot].ap().tensor, P - 1, [[REL_W - 1, P], [1, REL_W]])
                            sp.dma_start(bias[slot][:, :], skewed).then_inc(s_rd[slot], 16)
                        if h := stage_of(n, r, it, LOAD):
                            m, slot, turn = h
                            wait(sp, s_smm, NU * (m - ROUND + 1))
                            slot = (r + LOAD) % ROUND
                            load_head(sp, m, qk[slot][:, :], s_qk[slot])
                        if h := stage_of(n, r, it, REL):
                            m, slot, turn = h
                            sp.wait_ge(s_eev, NU * (m + 1))
                            wait(sp, s_rd[slot], 16 * turn)
                            sp.dma_start(rel[slot][:, :], stage[slot % 2][:, :]).then_inc(s_wr[slot], 16)
                        if isinstance(n, int) and n + READ == NBH:
                            sp.dma_start(slots_in[:, :].rearrange("(n p) d -> p n d", p=P),
                                         zero_row[:, :].unsqueeze(1).broadcast_to([P, SLOT_TILES, D])).then_inc(s_zeroed, 16)
                    run_heads(sp, -LOAD, last, step)

                @block.tensor
                def _(pe):
                    def relative(m, slot, q_k, u):
                        bank = (NU * slot + u) % 2
                        wait(pe, s_eev, NU * m + u - 1)
                        for i, off, w in units[u]:
                            mm = nc.tensor.matmul(psE[bank][:, off:off + w], q_k[:, i * P:(i + 1) * P],
                                                  ErP[:, S - w:S], start=True, stop=True)
                        mm.then_inc(s_emm, 1)

                    def score(m, slot, q_k, u):
                        bank = (NU * slot + u) % 2
                        wait(pe, s_soft, NU * m + u - 1)
                        for i, off, w in units[u]:
                            nc.tensor.matmul(psS[bank][:, off:off + w], q_k[:, i * P:(i + 1) * P],
                                             q_k[:, S:S + w], start=True, stop=False)
                            mm = nc.tensor.matmul(psS[bank][:, off + w - P:off + w], identb[:, :], dmask[:, :],
                                                  start=False, stop=True)
                        mm.then_inc(s_smm, 1)

                    def turn_probs(m, slot, u):
                        bank = (NU * slot + u) % 2
                        wait(pe, s_tev, NU * m + u - 1)
                        for j, off, w in CAUSAL_KEYS[u]:
                            for i in range(j, NI):
                                at = place[i][0] + j * P
                                to = off + (i - j) * P
                                tr = nc.tensor.transpose(psT[bank][:, to:to + P], scores[slot][:, at:at + P], ident[:, :])
                        tr.then_inc(s_tmm, 1)

                    def step(n, r, it):
                        early, soft, late = (stage_of(n, r, it, k) for k in (REL, SOFT, 0))
                        for u in range(NU):
                            if soft:
                                score(soft[0], soft[1], qk[(r + SOFT) % ROUND], u)
                            if late:
                                if u == 0:
                                    pe.wait_ge(s_exp, late[0] + 1)
                                turn_probs(late[0], late[1], u)
                            if early:
                                at = (r + REL) % ROUND
                                if u == 0:
                                    pe.wait_ge(s_qk[at], 16 * (it + (r + REL) // ROUND + 1))
                                relative(early[0], early[1], qk[at], u)
                        if h := group_of(n, r, it, 1):
                            g, par = h
                            at, w = key_place[r % GROUP]
                            vals.weigh(pe, g, par, r % GROUP, s_tev, NU * GROUP * (g + 1),
                                       lambda h: PT[par * GROUP + h][:, at:at + w])
                        if r % GROUP == 1 and (h := group_of(n, r, it, 2)):
                            vals.turn(pe, *h)
                    run_heads(pe, -LOAD, last, step)

                @block.vector
                def _(dve):
                    vals.clear(dve)

                    def step(n, r, it):
                        if r % GROUP == 2 and (h := group_of(n, r, it, 2)):
                            vals.divide(dve, *h)
                        soft, late = (stage_of(n, r, it, k) for k in (SOFT, 0))
                        if late and r % GROUP == 0:
                            g, par = group_of(n, r, it, 0)
                            wait(dve, vals.s_pv, NI * (g - 1))
                        if soft:
                            m, slot, turn = soft
                            dve.wait_ge(s_rd[slot], 16 * (turn + 1))
                            wait(dve, s_tmm, NU * (m - RING + 1))
                        for u, unit in enumerate(units):
                            if soft:
                                m, slot, turn = soft
                                dve.wait_ge(s_smm, NU * m + u + 1)
                                dve.sem_inc(s_seen, 1)
                                for i, off, w in unit:
                                    at = 512 * u + off
                                    ttr = nc.vector.tensor_tensor_reduce(
                                        out=scores[slot][:, at:at + w], in0=psS[(NU * slot + u) % 2][:, off:off + w],
                                        in1=bias[slot][:, at:at + w], scale=1.0, scalar=-3.0e38, op0=ALU.add, op1=ALU.max,
                                        accum_out=mx[:, slot, i:i + 1])
                                ttr.then_inc(s_soft, 1)
                            if late:
                                m, slot, turn = late
                                dve.wait_ge(s_tmm, NU * m + u + 1)
                                nc.vector.tensor_copy(PT[r][:, 512 * u:512 * u + WU[u]],
                                                      psT[(NU * slot + u) % 2][:, 0:WU[u]]).then_inc(s_tev, 1)
                        if soft:
                            m, slot, turn = soft
                            dve.wait_ge(s_soft, NU * (m + 1))
                            nc.vector.tensor_scalar(nm[:, slot, :], mx[:, slot, :], -1.0 / 4, None, ALU.mult).then_inc(s_nm, 1)
                    run_heads(dve, -LOAD, last, step)

                @block.gpsimd
                def _(pool):
                    pool.wait_ge(vals.s_zero, 3)

                    def step(n, r, it):
                        if r % GROUP == 0 and (h := group_of(n, r, it, 0)):
                            vals.spread_values(pool, *h)
                    run_heads(pool, 0, NBH - 1, step)

                @block.scalar
                def _(act):
                    def step(n, r, it):
                        if r % GROUP == 0 and (h := group_of(n, r, it, 2)):
                            vals.copy_out(act, *h)
                        early, soft = (stage_of(n, r, it, k) for k in (REL, EXP))
                        if early and (not isinstance(n, int) or early[0] >= 2):
                            act.wait_ge(s_wr[(r + REL - 2) % RING], 16 * (it * (ROUND // RING) + (r + REL - 2) // RING + 1))
                        if soft:
                            act.wait_ge(s_nm, soft[0] + 1)
                        for i in range(NI):
                            if early and i < NU:
                                m, slot, turn = early
                                act.wait_ge(s_emm, NU * m + i + 1)
                                nc.scalar.copy(stage[slot % 2][:, 512 * i:512 * i + WU[i]],
                                               psE[(NU * slot + i) % 2][:, 0:WU[i]]).then_inc(s_eev, 1)
                            if soft:
                                m, slot, turn = soft
                                at, w = place[i]
                                ex = nc.scalar.activation(scores[slot][:, at:at + w], scores[slot][:, at:at + w], ACT.Exp,
                                                          bias=nm[:, slot, i:i + 1], scale=1.0 / 4)
                                if i == NI - 1:
                                    ex.then_inc(s_exp, 1)
                    run_heads(act, -LOAD, last, step)

        def masked_attention(mask_bias, maskT, identb, weights):
            KM = KP + 3
            LOAD, SOFT, ROWS = 3, 2, 1
            last = NBH + 2 * GROUP
            with ExitStack() as ctx:
                qk = [sb(ctx, f"mqk{r}", [KM, 2 * S], BF16) for r in range(RING)]
                PT = [sb(ctx, f"mPT{r}", [P, NI, S]) for r in range(ROUND)]
                unused = sb(ctx, "unused", [P, NI, S], BF16)
                mx = sb(ctx, "mmx", [P, RING, NI])
                neg = sb(ctx, "mneg", [P, RING, NI])
                zero = sb(ctx, "mzero", [P, NI])
                rest = sb(ctx, "mrest", [P, RING, NI])
                mp = sb(ctx, "mpieces", [P, RING, NI, 4], BF16)
                vals = Values(ctx, "m")
                weights.begin(ctx)
                psS = banks(ctx, "mpsS", 2)
                psB = banks(ctx, "mpsB", 2)
                psM = ctx.enter_context(nc.psum_tensor("mpsM", [P, 1024], BF16))
                s_qk = [sem(f"s_mqk{r}") for r in range(RING)]
                names = ("one", "smm", "soft", "mp", "mt", "row", "bmm", "exp", "seen")
                s_seen_p = sem("s_mseenp")
                s_one, s_smm, s_soft, s_mp, s_mt, s_row, s_bmm, s_exp, s_seen = (sem(f"s_m{n}") for n in names)
                block = ctx.enter_context(nc.Block())

                @block.sync
                def _(sp):
                    def step(n, r, it):
                        if h := stage_of(n, r, it, LOAD):
                            m, slot, turn = h
                            wait(sp, s_bmm, NI * (m - RING + 1))
                            load_head(sp, m, qk[slot][0:KP, :], s_qk[slot])
                        if isinstance(n, int) and 0 <= n < 3:
                            weights.load(sp, n)
                    run_heads(sp, -LOAD, last, step)

                @block.tensor
                def _(pe):
                    pe.wait_ge(s_one, RING)

                    def step(n, r, it):
                        soft, rows, late = (stage_of(n, r, it, k) for k in (SOFT, ROWS, 0))
                        if soft:
                            pe.wait_ge(s_qk[soft[1]], 16 * (soft[2] + 1))
                        if late:
                            pe.wait_ge(s_row, late[0] + 1)
                        for i in range(NI):
                            if soft:
                                m, slot, turn = soft
                                wait(pe, s_soft, NI * m + i - 1)
                                nc.tensor.matmul(psS[i % 2][:, :], qk[slot][0:KP, i * P:(i + 1) * P], qk[slot][0:KP, S:2 * S],
                                                 start=True, stop=True).then_inc(s_smm, 1)
                            if late:
                                m, slot, turn = late
                                wait(pe, s_exp, NI * m + i - 1)
                                nc.tensor.matmul(psB[i % 2][:, :], qk[slot][:, S + i * P:S + (i + 1) * P], qk[slot][:, 0:S],
                                                 start=True, stop=False)
                                nc.tensor.matmul(psB[i % 2][:, :], identb[:, :], maskT[:, i, :],
                                                 start=False, stop=True).then_inc(s_bmm, 1)
                            if rows and i == 1:
                                m, slot, turn = rows
                                pe.wait_ge(s_mp, 5 * (m + 1))
                                wait(pe, s_row, m)
                                for k in range(NI):
                                    tr = nc.tensor.transpose(psM[KP:KP + 3, k * P:(k + 1) * P], mp[:, slot, k, 0:3], identb[:, :])
                                tr.then_inc(s_mt, 1)
                        if h := group_of(n, r, it, 1):
                            g, par = h
                            vals.weigh(pe, g, par, r % GROUP, s_exp, NI * GROUP * (g + 1),
                                       lambda h: PT[par * GROUP + h][:, r % GROUP, :])
                        if r % GROUP == 1 and (h := group_of(n, r, it, 2)):
                            vals.turn(pe, *h)
                        if isinstance(n, int) and n == 6:
                            weights.total(pe)
                    run_heads(pe, -LOAD, last, step)

                @block.gpsimd
                def _(pool):
                    pool.wait_ge(s_one, RING + 1)
                    pool.wait_ge(vals.s_zero, 3)

                    def step(n, r, it):
                        if r % GROUP == 0 and (h := group_of(n, r, it, 0)):
                            vals.spread_values(pool, *h)
                        if h := stage_of(n, r, it, SOFT):
                            m, slot, turn = h
                            pool.wait_ge(s_soft, NI * (m + 1))
                            wait(pool, s_mt, m - RING + 1)
                            wait(pool, s_mp, 5 * m)
                            pool.sem_inc(s_seen_p, 1)
                            nc.gpsimd.tensor_scalar(neg[:, slot, :], mx[:, slot, :], -1.0, 0.0, ALU.mult, ALU.add).then_inc(s_mp, 1)
                            pool.wait_ge(s_mp, 5 * m + 1)
                            nc.gpsimd.tensor_tensor(mp[:, slot, :, 0], neg[:, slot, :], zero[:, :], ALU.add).then_inc(s_mp, 1)
                            pool.wait_ge(s_mp, 5 * m + 2)
                            nc.gpsimd.tensor_tensor(rest[:, slot, :], neg[:, slot, :], mp[:, slot, :, 0], ALU.subtract).then_inc(s_mp, 1)
                            pool.wait_ge(s_mp, 5 * m + 3)
                            nc.gpsimd.tensor_tensor(mp[:, slot, :, 1], rest[:, slot, :], zero[:, :], ALU.add).then_inc(s_mp, 1)
                            pool.wait_ge(s_mp, 5 * m + 4)
                            nc.gpsimd.tensor_tensor(mp[:, slot, :, 2], rest[:, slot, :], mp[:, slot, :, 1], ALU.subtract).then_inc(s_mp, 1)
                    run_heads(pool, -LOAD, NBH - 1, step)

                @block.vector
                def _(dve):
                    for r in range(RING):
                        nc.vector.memset(qk[r][KP:KM, S:2 * S], 1.0).then_inc(s_one, 1)
                    nc.vector.memset(zero[:, :], 0.0).then_inc(s_one, 1)
                    vals.clear(dve)
                    weights.clear(dve)

                    def step(n, r, it):
                        if h := stage_of(n, r, it, SOFT):
                            m, slot, turn = h
                            wait(dve, s_soft, NI * m)
                            for i in range(NI):
                                dve.wait_ge(s_smm, NI * m + i + 1)
                                dve.sem_inc(s_seen, 1)
                                nc.vector.tensor_tensor_reduce(
                                    out=unused[:, i, :], in0=psS[i % 2][:, :], in1=mask_bias[:, i, :], scale=1.0, scalar=-3.0e38,
                                    op0=ALU.add, op1=ALU.max, accum_out=mx[:, slot, i:i + 1]).then_inc(s_soft, 1)
                        if r % GROUP == 2 and (h := group_of(n, r, it, 2)):
                            vals.divide(dve, *h)
                        if isinstance(n, int) and 3 <= n < 6:
                            weights.magnitudes(dve, n - 3)
                        if isinstance(n, int) and n == 7:
                            weights.scales(dve)
                        if isinstance(n, int) and 0 <= n - (NBH - ROUND) < 9:
                            weights.round(dve, *divmod(n - (NBH - ROUND), 3))
                    run_heads(dve, -LOAD, last, step)

                @block.scalar
                def _(act):
                    def step(n, r, it):
                        if r % GROUP == 0 and (h := group_of(n, r, it, 2)):
                            vals.copy_out(act, *h)
                        rows, late = (stage_of(n, r, it, k) for k in (ROWS, 0))
                        if late and r % GROUP == 0:
                            g, par = group_of(n, r, it, 0)
                            wait(act, vals.s_pv, NI * (g - 1))
                        for j in range(NI):
                            if late:
                                m, slot, turn = late
                                act.wait_ge(s_bmm, NI * m + j + 1)
                                nc.scalar.activation(PT[r][:, j, :], psB[j % 2][:, :], ACT.Exp, scale=1.0 / 4).then_inc(s_exp, 1)
                            if rows and j == 2:
                                m, slot, turn = rows
                                act.wait_ge(s_mt, m + 1)
                                nc.scalar.copy(qk[slot][KP:KM, 0:S], psM[KP:KM, 0:S]).then_inc(s_row, 1)
                    run_heads(act, -LOAD, last, step)

        with ExitStack() as ctx:
            ctxT = sb(ctx, "ctxT", [P, DK, TOK])
            zero_row = sb(ctx, "zero_row", [P, D])
            V = sb(ctx, "V", [P, NBH, NI, VW])
            identb = sb(ctx, "identb0", [P, P], BF16)
            dmask = sb(ctx, "dmask", [P, P], BF16)
            attn = xn[:, :, :].rearrange("p t d -> p (t d)").rearrange("p (m i d) -> p m i d", i=NI, d=DH)

            def opening(ErP):
                with ExitStack() as c1:
                    er = sb(c1, "er", [KP, S])
                    ep = sb(c1, "ep", [KP, 2, S])
                    eb = sb(c1, "eb", [KP, 3, S], BF16)
                    above = sb(c1, "above", [P, P])
                    s_er, s_above, s_cc, s_es, s_pick = (sem(f"s_{n}") for n in ("er", "above", "cc", "es", "pick"))
                    ln = LayerNorm(c1, "a")
                    q = PieceProjection(c1, "aq", 0, xnT, a["L0_WqT"], a["L0_bq"], 4)
                    k = PieceProjection(c1, "ak", 1, ctxT, a["L0_WkT"], a["L0_bk"], 4)
                    v = ValueProjection(c1, "a", ctxT, V, a["L0_WvT"], a["L0_bv"])
                    block = c1.enter_context(nc.Block())

                    @block.sync
                    def _(sp):
                        er_t = a["ErT"].tensor
                        sp.dma_start(er[:, :], bass.AP(er_t, 0, [[0, PIECES], [S, DH], [1, S]])).then_inc(s_er, 16)
                        k.load(sp)
                        v.load(sp)
                        for half in range(2):
                            part = slice(half * TOK // 2, (half + 1) * TOK // 2)
                            sp.dma_start(ctxT[:, :, part], a["ctxT"].rearrange("(k p) t -> p k t", p=P)[:, :, part]).then_inc(s_ctx[half], 16)
                        sp.dma_start(x[:, :, :], a["x"].rearrange("b (i p) d -> p (b i) d", p=P)).then_inc(s_const, 16)
                        sp.dma_start(ident[:, :], a["ident"]).then_inc(s_const, 16)
                        q.load(sp)
                        sp.dma_start(above[:, :], a["above"]).then_inc(s_above, 16)
                        sp.wait_ge(s_es, 5)
                        for g, piece in enumerate(LK):
                            rows = slice(g * DH, (g + 1) * DH)
                            sp.dma_start(ErP[rows, :], eb[rows, piece, :]).then_inc(s_pick, 16)
                        for g in range(k.PARTS):
                            k.store(sp, g)
                        for g in range(q.PARTS):
                            q.store(sp, g)
                        sp.wait_ge(s_pick, 16 * PIECES)
                        k.stored(sp)
                        q.stored(sp)

                    @block.tensor
                    def _(pe):
                        for g in range(k.PARTS):
                            if g % (k.PARTS // 2) == 0:
                                pe.wait_ge(s_ctx[g // (k.PARTS // 2)], 16)
                            k.product(pe, g)
                            v.product(pe, 2 * g)
                            v.product(pe, 2 * g + 1)
                        pe.wait_ge(s_const, 32)
                        ln.turn(pe, 0)
                        for b in range(B):
                            if b + 1 < B:
                                ln.turn(pe, b + 1)
                            pe.wait_ge(ln.s_ev, DK * (b + 1))
                            for eh in range(DK):
                                q.product(pe, DK * b + eh)

                    @block.scalar
                    def _(act):
                        k.wait_load(act)
                        for g in range(k.PARTS):
                            k.copies(act, g)
                        ln.root(act, 0)
                        q.wait_load(act)
                        ln.copy(act, 0)
                        for b in range(B):
                            if b + 1 < B:
                                ln.copy(act, b + 1)
                            for eh in range(DK):
                                q.copies(act, DK * b + eh)

                    @block.vector
                    def _(dve):
                        nc.vector.memset(zero_row[:, :], 0.0).then_inc(s_cc, 1)
                        nc.vector.memset(V[:, :, :, DH:VW], 1.0).then_inc(s_cc, 1)
                        dve.wait_ge(s_er, 16)
                        nc.vector.tensor_copy(eb[:, 0, :], er[:, :]).then_inc(s_es, 1)
                        dve.wait_ge(s_es, 1)
                        nc.vector.tensor_tensor(ep[:, 0, :], er[:, :], eb[:, 0, :], ALU.subtract).then_inc(s_es, 1)
                        dve.wait_ge(s_es, 2)
                        nc.vector.tensor_copy(eb[:, 1, :], ep[:, 0, :]).then_inc(s_es, 1)
                        dve.wait_ge(s_es, 3)
                        nc.vector.tensor_tensor(ep[:, 1, :], ep[:, 0, :], eb[:, 1, :], ALU.subtract).then_inc(s_es, 1)
                        dve.wait_ge(s_es, 4)
                        nc.vector.tensor_copy(eb[:, 2, :], ep[:, 1, :]).then_inc(s_es, 1)
                        v.wait_load(dve)
                        for g in range(k.PARTS):
                            k.split(dve, g)
                            for t in (2 * g, 2 * g + 1):
                                v.out(dve, t)
                                if t == 0:
                                    dve.wait_ge(s_const, 32)
                                ln.stats(dve, t)
                        ln.norm(dve, 0)
                        dve.wait_ge(s_above, 16)
                        nc.vector.tensor_scalar(dmask[:, :], above[:, :], NEG, None, ALU.mult).then_inc(s_cc, 1)
                        nc.vector.tensor_copy(identb[:, :], ident[:, :]).then_inc(s_cc, 1)
                        for g in range(q.PARTS):
                            q.split(dve, g)

            with ExitStack() as c0:
                ErP = sb(c0, "ErP", [KP, S], BF16)
                with nc.cleanup_on_exit():
                    opening(ErP)
                    causal_attention(ErP, identb, dmask)

            mask_bias = sb(ctx, "mask_bias", [P, NI, S])
            maskT = sb(ctx, "maskT", [P, NI, S], BF16)
            with nc.cleanup_on_exit():
                with ExitStack() as c1:
                    prob = sb(c1, "prob", [P, TOPK, TT])
                    slot_of = sb(c1, "slot_of", [P, TOPK * TT], U32)
                    expert_of = sb(c1, "expert_of", [P, SLOT_TILES], I32)
                    with ExitStack() as c2:
                        w2 = sb(c2, "w2", [P, E, FB * D])
                        s_w2 = sem("s_moew2")
                        s_scattered = sem("s_scattered")
                        with ExitStack() as c3:
                            ln = LayerNorm(c3, "b")
                            k = PieceProjection(c3, "ck", 1, ctxT, a["L1_WkT"], None, 2)
                            v = ValueProjection(c3, "c", ctxT, V, a["L1_WvT"], None)
                            route(nc, a, sem, sb, banks, x, attn, ln, s_zeroed, ident, xn, xnT, prob, slot_of, expert_of,
                                  w2, s_w2, slots_in, s_scattered, k, v, mask_bias, maskT)
                        experts(nc, a, sem, sb, banks, ident, expert_of, w2, s_w2, slots_in, slots_out, s_scattered)
                    ln = LayerNorm(c1, "c", calls=B, on_scalar=True)
                    q = PieceProjection(c1, "cq", 0, xnT, a["L1_WqT"], None, 4)
                    combine(nc, sem, sb, x, prob, slot_of, slots_out, ln, q)

            weights = TernaryWeights(nc, a, ctx, sem, sb, banks, xnT)
            masked_attention(mask_bias, maskT, identb, weights)
            tokens = Tokens(ctx, sb)
            closing(nc, a, sem, sb, banks, x, xn, attn, ident, identb, LayerNorm(ctx, "d", calls=B, transposed=False, on_scalar=True), weights, tokens)
            ffn(nc, sem, sb, banks, x, identb, weights, tokens, out)


def closing(nc, a, sem, sb, banks, x, xn, attn, ident, identb, ln, weights, tokens):
    ws = weights.ws
    with ExitStack() as ctx:
        w = sb(ctx, "wo", [P, DK, D])
        aN = sb(ctx, "aN", [P, TT, D])
        aT = sb(ctx, "aT", [P, DK, TOK])
        minus_magic = sb(ctx, "minus_magic0", [P, 1])
        s_mag = sem("s_gmag")
        am = sb(ctx, "am", [P, TT])
        top = sb(ctx, "top_", [P, TT])
        sx = sb(ctx, "sx", [P, TT])
        inv = sb(ctx, "inv", [P, TT])
        r = sb(ctx, "rq", [P, TT, D])
        xq = sb(ctx, "xq", [P, TT, D], BF16)
        pt = banks(ctx, "opt", 2)
        po = banks(ctx, "opo", 4)
        pxt = [ctx.enter_context(nc.psum_tensor(f"pxt{i}", [P, 2 * S], BF16)) for i in range(2)]
        s_w, s_n, s_tr, s_ev, s_mm, s_x = (sem(f"s_op{n}") for n in ("w", "n", "tr", "ev", "mm", "x"))
        s_a, s_s, s_r, s_xq, s_qt, s_qc = (sem(f"s_g{n}") for n in ("a", "s", "r", "xq", "qt", "qc"))
        block = ctx.enter_context(nc.Block())

        @block.sync
        def _(sp):
            sp.dma_start(w[:, :, :], a["L1_WoT"].rearrange("(k p) e -> p k e", p=P)).then_inc(s_w, 16)

        @block.vector
        def _(dve):
            def copy(b):
                for i in range(NI):
                    nc.vector.tensor_copy(aN[:, b * NI + i, :].rearrange("p (h d) -> p h d", d=DH),
                                          attn[:, b * HEADS:(b + 1) * HEADS, i, :]).then_inc(s_n, 1)

            nc.vector.memset(minus_magic[:, :], -MAGIC).then_inc(s_mag, 1)
            for b in range(B):
                copy(b)
            def residual(b):
                for t in range(b * NI, (b + 1) * NI):
                    dve.wait_ge(s_mm, t + 1)
                    nc.vector.tensor_tensor(x[:, t, :], po[t % 4][:, 0:D], x[:, t, :], ALU.add).then_inc(s_x, 1)
                    if t > b * NI:
                        dve.wait_ge(s_x, t)
                        ln.stats(dve, t - 1)
                dve.wait_ge(s_x, (b + 1) * NI)
                ln.stats(dve, (b + 1) * NI - 1)

            def scales(b):
                ts = slice(b * NI, (b + 1) * NI)
                for t in range(b * NI, (b + 1) * NI):
                    dve.wait_ge(ln.s_xn, t + 1)
                    nc.vector.tensor_reduce(am[:, t:t + 1], xn[:, t, :], AX.X, ALU.max, apply_absolute_value=True).then_inc(s_a, 1)
                dve.wait_ge(s_a, (b + 1) * NI)
                nc.vector.tensor_scalar(top[:, ts], am[:, ts], 1e-5, None, ALU.max).then_inc(s_s, 1)
                dve.wait_ge(s_s, 5 * b + 1)
                nc.vector.reciprocal(inv[:, ts], top[:, ts]).then_inc(s_s, 1)
                nc.vector.tensor_scalar(tokens.gs[:, ts], top[:, ts], ws[:, 0:1], 1.0 / 127, ALU.mult, ALU.mult).then_inc(s_s, 1)
                nc.vector.tensor_scalar(tokens.us[:, ts], top[:, ts], ws[:, 1:2], 1.0 / 127, ALU.mult, ALU.mult).then_inc(s_s, 1)
                dve.wait_ge(s_s, 5 * b + 4)
                nc.vector.tensor_scalar(sx[:, ts], inv[:, ts], 127.0, None, ALU.mult).then_inc(s_s, 1)

            for b in range(B):
                residual(b)
                ln.norm(dve, b)
                ln.shifts(dve, b)
                if b >= 1:
                    scales(b - 1)
            scales(B - 1)

        @block.gpsimd
        def _(pool):
            for t in range(TT):
                if t % NI == 0:
                    pool.wait_ge(s_s, 5 * (t // NI + 1))
                wait(pool, s_r, t)
                nc.gpsimd.tensor_scalar(r[:, t, :], xn[:, t, :], sx[:, t:t + 1], MAGIC, ALU.mult, ALU.add).then_inc(s_r, 1)

        @block.tensor
        def _(pe):
            pe.wait_ge(s_w, 16)

            def integers_turned(c):
                pe.wait_ge(s_xq, NI * (c + 1))
                wait(pe, s_qc, c - 1)
                for dk in range(DK):
                    for j in range(NI):
                        tr = nc.tensor.transpose(pxt[c % 2][:, (dk * NI + j) * P:(dk * NI + j + 1) * P],
                                                 xq[:, c * NI + j, dk * P:(dk + 1) * P], identb[:, :])
                tr.then_inc(s_qt, 1)

            for c in range(B):
                for dk in range(DK):
                    u = c * DK + dk
                    pe.wait_ge(s_n, NI * (c + 1))
                    wait(pe, s_ev, u - 1)
                    for j in range(NI):
                        tr = nc.tensor.transpose(pt[u % 2][:, j * P:(j + 1) * P], aN[:, c * NI + j, dk * P:(dk + 1) * P], ident[:, :])
                    tr.then_inc(s_tr, 1)
                pe.wait_ge(s_ev, DK * (c + 1))
                for j in range(NI):
                    t = c * NI + j
                    wait(pe, s_x, t - 3)
                    for dk in range(DK):
                        mm = nc.tensor.matmul(po[t % 4][:, 0:D], aT[:, dk, t * P:(t + 1) * P], w[:, dk, :],
                                              start=(dk == 0), stop=(dk == DK - 1))
                    mm.then_inc(s_mm, 1)
                if c == B - 1:
                    for d in range(B):
                        integers_turned(d)

        @block.scalar
        def _(act):
            def copies(c):
                for u in range(c * DK, (c + 1) * DK):
                    dk = u % DK
                    act.wait_ge(s_tr, u + 1)
                    nc.scalar.copy(aT[:, dk, c * S:(c + 1) * S], pt[u % 2][:, :]).then_inc(s_ev, 1)

            def integers(b):
                for t in range(b * NI, (b + 1) * NI):
                    act.wait_ge(s_r, t + 1)
                    nc.scalar.activation(xq[:, t, :], r[:, t, :], ACT.Identity, bias=minus_magic[:, :]).then_inc(s_xq, 1)

            def integers_out(c):
                act.wait_ge(s_qt, c + 1)
                nc.scalar.copy(tokens.xqT[:, :, c * S:(c + 1) * S], pxt[c % 2][:, :].rearrange("p (k s) -> p k s", s=S)).then_inc(s_qc, 1)

            copies(0)
            copies(1)
            act.wait_ge(s_mag, 1)
            act.wait_ge(s_n, TT)
            for b in range(B):
                ln.root(act, b)
                if b + 2 < B:
                    copies(b + 2)
                ln.apply(act, b)
                if b >= 1:
                    integers(b - 1)
                if b >= 2:
                    integers_out(b - 2)
            integers_out(B - 2)
            integers(B - 1)
            integers_out(B - 1)



class Tokens:

    def __init__(self, ctx, sb):
        self.xqT = sb(ctx, "xqT", [P, DK, TOK], BF16)
        self.gs = sb(ctx, "gs", [P, TT])
        self.us = sb(ctx, "us", [P, TT])



def route(nc, a, sem, sb, banks, x, attn, ln, s_zeroed, ident, xn, xnT, prob, slot_of, expert_of, w2, s_w2, slots_in,
          s_scattered, k_proj, v_proj, mask_bias, maskT):
    C = TT * E
    with ExitStack() as c1:
        rw = sb(c1, "rw", [P, DK, CG])
        by_expert = sb(c1, "by_expert", [P, S])
        iota = sb(c1, "iota", [P, E])
        tile_no = sb(c1, "tile_no", [P, SLOT_TILES])
        before = sb(c1, "before", [P, P])
        prior = sb(c1, "prior", [P, TOPK, TOPK * C])
        same = sb(c1, "same", [P, E])
        ones = sb(c1, "onesr", [P, P])
        lg = sb(c1, "lg", [P, TT, E])
        best = sb(c1, "best", [P, TT, 8])
        bidx = sb(c1, "bidx", [P, TT, 8], U32)
        idx = sb(c1, "idx", [P, TT, 8])
        d12 = sb(c1, "d12", [P, TT])
        e12 = sb(c1, "e12", [P, TT])
        den = sb(c1, "den", [P, TT])
        chosen = sb(c1, "chosen", [P, TOPK, C])
        totals = sb(c1, "totals", [P, TOPK, P])
        place = sb(c1, "place", [P, TOPK * C])
        slot = sb(c1, "slot", [P, TOPK * TT])
        frac = sb(c1, "frac", [P, E])
        whole = sb(c1, "whole", [P, E])
        tiles = sb(c1, "tiles", [P, E])
        ends = sb(c1, "ends", [P, E + 1])
        past = sb(c1, "past", [P, SLOT_TILES, E])
        past_n = sb(c1, "past_n", [P, SLOT_TILES])
        expert = sb(c1, "expert", [P, SLOT_TILES])
        mask = [sb(c1, f"mask{n}", [P, NI, S], I32) for n in range(2)]
        pl, plt = ln.ps
        pt = banks(c1, "ptot", 1)[0]
        pc = pt[:, TOPK * P:TOPK * P + E]
        pr = banks(c1, "prank", 1)[0]
        s_res, s_rz, s_lt, s_turned = (sem(f"s_{n}") for n in ("res", "rz", "lt", "turned"))
        s_mask, s_mb = sem("s_mask"), sem("s_mb")
        s_w, s_k, s_mm, s_lg, s_b, s_i, s_d, s_e, s_p, s_oh, s_tot, s_totc, s_rank, s_cnt, s_one, s_place, s_slot = (
            sem(f"s_ro{n}") for n in ("w", "k", "mm", "lg", "b", "i", "d", "e", "p", "oh", "tot", "totc", "rank",
                                      "cnt", "one", "place", "slot"))
        block = c1.enter_context(nc.Block())

        @block.sync
        def _(sp):
            for n, name in enumerate(("mask", "maskT")):
                sp.dma_start(mask[n][:, :, :], a[name].rearrange("a b (i p) s -> p (a b i) s", p=P)).then_inc(s_mask, 16)
            sp.wait_ge(s_rz, 1)
            sp.dma_start(rw[:, :, 0:E], a["routerT"].rearrange("(k p) e -> p k e", p=P)).then_inc(s_w, 16)
            for dst, name in ((iota, "iota"), (tile_no, "tile_no"), (before, "above"), (same, "same")):
                sp.dma_start(dst[:, :], a[name]).then_inc(s_k, 16)
            sp.dma_start(prior[:, :, :], a["prior"]).then_inc(s_k, 16)
            k_proj.load(sp)
            v_proj.load(sp)
            for e in range(E):
                sp.dma_start(w2[:, e, :], a["w2p"][e]).then_inc(s_w2, 16)
            for g in range(k_proj.PARTS):
                k_proj.store(sp, g)
            k_proj.stored(sp)

        @block.tensor
        def _(pe):
            for b in range(B):
                ln.turn(pe, b)
            pe.wait_ge(s_w, 16)
            pe.wait_ge(ln.s_ev, DK * B)
            for dk in range(DK):
                for b in range(B):
                    mm = nc.tensor.matmul(pl[b * CG:(b + 1) * CG, :], rw[:, dk, :], xnT[:, dk, b * S:(b + 1) * S],
                                          start=(dk == 0), stop=(dk == DK - 1))
            mm.then_inc(s_mm, 1)
            pe.wait_ge(s_lt, 1)
            for j in range(NI):
                mm = nc.tensor.transpose(plt[:, j * P:(j + 1) * P], by_expert[:, j * P:(j + 1) * P], ident[:, :])
            mm.then_inc(s_turned, 1)
            pe.wait_ge(s_one, 1)
            pe.wait_ge(s_oh, TOPK)
            pe.wait_ge(s_k, 16 * 5)
            for k in range(TOPK):
                mm = nc.tensor.matmul(pt[:, k * P:(k + 1) * P], chosen[:, k, :], ones[:, :], start=True, stop=True)
            mm.then_inc(s_tot, 1)
            nc.tensor.matmul(pr[:, 0:TOPK * C], before[:, :], chosen[:, :, :].rearrange("p k c -> p (k c)"),
                             start=True, stop=False)
            pe.wait_ge(s_totc, 1)
            for k in range(TOPK):
                mm = nc.tensor.matmul(pc, totals[:, k, :], same[:, :], start=(k == 0), stop=(k == TOPK - 1))
            mm.then_inc(s_cnt, 1)
            for k in range(TOPK):
                mm = nc.tensor.matmul(pr[:, 0:TOPK * C], totals[:, k, :], prior[:, k, :], start=False, stop=(k == TOPK - 1))
            mm.then_inc(s_rank, 1)
            for g in range(k_proj.PARTS):
                k_proj.product(pe, g)
                v_proj.product(pe, 2 * g)
                v_proj.product(pe, 2 * g + 1)

        @block.scalar
        def _(act):
            ln.root(act, 0)
            for b in range(B):
                ln.copy(act, b)
            act.wait_ge(s_mm, 1)
            nc.scalar.copy(by_expert[:, :], pl[:, :]).then_inc(s_lt, 1)
            act.wait_ge(s_d, 1)
            nc.scalar.activation(e12[:, :], d12[:, :], ACT.Exp).then_inc(s_e, 1)
            for g in range(k_proj.PARTS):
                k_proj.copies(act, g)

        @block.vector
        def _(dve):
            nc.vector.memset(rw[:, :, :], 0.0).then_inc(s_rz, 1)
            nc.vector.memset(ones[:, :], 1.0).then_inc(s_one, 1)
            nc.vector.memset(ends[:, 0:1], 0.0).then_inc(s_one, 1)
            for t in range(TT):
                b, i = divmod(t, NI)
                to = x[:, t, :].rearrange("p (h d) -> p h d", d=DH)
                nc.vector.tensor_tensor(to, to, attn[:, b * HEADS:(b + 1) * HEADS, i, :], ALU.add).then_inc(s_res, 1)
                if t >= 1:
                    dve.wait_ge(s_res, t)
                    ln.stats(dve, t - 1)
            dve.wait_ge(s_res, TT)
            ln.stats(dve, TT - 1)
            ln.norm(dve, 0)
            dve.wait_ge(s_mask, 32)
            for n, to in enumerate((mask_bias, maskT)):
                nc.vector.tensor_scalar(to[:, :, :], mask[n][:, :, :], 0.0, NEG, ALU.is_equal, ALU.mult).then_inc(s_mb, 1)
            dve.wait_ge(s_turned, 1)
            nc.vector.tensor_copy(lg[:, :, :].rearrange("p (b j) e -> p b j e", b=B),
                                  plt[:, :].rearrange("p (j b e) -> p b j e", b=B, e=CG)[:, :, :, 0:E]).then_inc(s_lg, 1)
            dve.wait_ge(s_lg, 1)
            for t in range(TT):
                nc.vector.max(best[:, t, :], lg[:, t, :]).then_inc(s_b, 1)
            for t in range(TT):
                dve.wait_ge(s_b, t + 1)
                last = nc.vector.max_index(bidx[:, t, :], best[:, t, :], lg[:, t, :])
            last.then_inc(s_i, 1)
            nc.vector.tensor_tensor(d12[:, :], best[:, :, 1], best[:, :, 0], ALU.subtract).then_inc(s_d, 1)
            dve.wait_ge(s_i, 1)
            nc.vector.tensor_copy(idx[:, :, :], bidx[:, :, :]).then_inc(s_i, 1)
            dve.wait_ge(s_i, 2)
            dve.wait_ge(s_k, 16 * 5)
            for k in range(TOPK):
                nc.vector.tensor_tensor(chosen[:, k, :].rearrange("p (t e) -> p t e", e=E),
                                        iota[:, :].unsqueeze(1).broadcast_to([P, TT, E]),
                                        idx[:, :, k:k + 1].broadcast_to([P, TT, E]), ALU.is_equal).then_inc(s_oh, 1)
            dve.wait_ge(s_tot, 1)
            nc.vector.tensor_copy(totals[:, :, :].rearrange("p k c -> p (k c)"), pt[:, 0:TOPK * P]).then_inc(s_totc, 1)
            dve.wait_ge(s_e, 1)
            nc.vector.tensor_scalar(den[:, :], e12[:, :], 1.0, None, ALU.add).then_inc(s_p, 1)
            dve.wait_ge(s_p, 1)
            nc.vector.reciprocal(prob[:, 0, :], den[:, :]).then_inc(s_p, 1)
            dve.wait_ge(s_p, 2)
            nc.vector.tensor_tensor(prob[:, 1, :], e12[:, :], prob[:, 0, :], ALU.mult).then_inc(s_p, 1)
            dve.wait_ge(s_cnt, 1)
            nc.vector.tensor_scalar(frac[:, :], pc, 1.0 / P, (P - 1) / P - 0.5 + 0.5 / P,
                                    ALU.mult, ALU.add).then_inc(s_place, 1)
            dve.wait_ge(s_place, 1)
            nc.vector.tensor_scalar(whole[:, :], frac[:, :], MAGIC, None, ALU.add).then_inc(s_place, 1)
            dve.wait_ge(s_place, 2)
            nc.vector.tensor_scalar(tiles[:, :], whole[:, :], MAGIC, None, ALU.subtract).then_inc(s_place, 1)
            dve.wait_ge(s_place, 3)
            dve.wait_ge(s_one, 2)
            for e in range(E):
                dve.wait_ge(s_place, 3 + e)
                nc.vector.tensor_tensor(ends[:, e + 1:e + 2], ends[:, e:e + 1], tiles[:, e:e + 1], ALU.add).then_inc(s_place, 1)
            dve.wait_ge(s_place, 3 + E)
            dve.wait_ge(s_rank, 1)
            nc.vector.scalar_tensor_tensor(out=place[:, :].rearrange("p (t e) -> p t e", e=E),
                                           in0=ends[:, 0:E].unsqueeze(1).broadcast_to([P, TOPK * TT, E]), scalar=float(P),
                                           in1=pr[:, 0:TOPK * C].rearrange("p (t e) -> p t e", e=E),
                                           op0=ALU.mult, op1=ALU.add).then_inc(s_slot, 1)
            dve.wait_ge(s_slot, 1)
            nc.vector.tensor_tensor(place[:, :], place[:, :], chosen[:, :, :].rearrange("p k c -> p (k c)"),
                                    ALU.mult).then_inc(s_slot, 1)
            dve.wait_ge(s_slot, 2)
            nc.vector.tensor_reduce(slot[:, :], place[:, :].rearrange("p (t e) -> p t e", e=E), AX.X, ALU.add).then_inc(s_slot, 1)
            dve.wait_ge(s_slot, 3)
            nc.vector.tensor_copy(slot_of[:, :], slot[:, :]).then_inc(s_slot, 1)
            nc.vector.tensor_tensor(past[:, :, :], tile_no[:, :].unsqueeze(2).broadcast_to([P, SLOT_TILES, E]),
                                    ends[:, 1:E + 1].unsqueeze(1).broadcast_to([P, SLOT_TILES, E]), ALU.is_ge).then_inc(s_slot, 1)
            dve.wait_ge(s_slot, 5)
            nc.vector.tensor_reduce(past_n[:, :], past[:, :, :], AX.X, ALU.add).then_inc(s_slot, 1)
            dve.wait_ge(s_slot, 6)
            nc.vector.tensor_scalar(expert[:, :], past_n[:, :], float(E - 1), None, ALU.min).then_inc(s_slot, 1)
            dve.wait_ge(s_slot, 7)
            nc.vector.tensor_copy(expert_of[:, :], expert[:, :]).then_inc(s_slot, 1)
            for g in range(k_proj.PARTS):
                k_proj.split(dve, g)
                v_proj.out(dve, 2 * g)
                v_proj.out(dve, 2 * g + 1)

        @block.gpsimd
        def _(pool):
            pool.wait_ge(s_slot, 4)
            pool.wait_ge(s_zeroed, 16)
            for k in range(TOPK):
                for t in range(TT):
                    c = k * TT + t
                    pool.indirect_dma_start(slots_in[:, :], bass.IndirectOffsetOnAxis(slot_of[:, c:c + 1], 0),
                                            xn[:, t, :], None).then_inc(s_scattered, 16)


def experts(nc, a, sem, sb, banks, ident, expert_of, w2, s_w2, slots_in, slots_out, s_scattered):
    RING3 = 3
    with ExitStack() as ctx:
        w1 = [sb(ctx, f"w1_{i}", [P, W1_ROW]) for i in range(RING3)]
        b2 = [sb(ctx, f"b2_{i}", [P, D]) for i in range(RING3)]
        xs = [sb(ctx, f"xs{i}", [P, D]) for i in range(RING3)]
        xT = [sb(ctx, f"xT{i}", [P, DK, P]) for i in range(RING3)]
        hT = [sb(ctx, f"hT{i}", [P, FB, P]) for i in range(RING3)]
        ys = [sb(ctx, f"ys{i}", [P, D]) for i in range(RING3)]
        px = banks(ctx, "px", 1)[0]
        ph = banks(ctx, "ph", 2)
        py = banks(ctx, "py", 1)[0]
        s_xs = [sem(f"s_moexs{i}") for i in range(RING3)]
        s_w1 = [sem(f"s_moew1{i}") for i in range(RING3)]
        s_b2 = [sem(f"s_moeb2{i}") for i in range(RING3)]
        s_st = [sem(f"s_moest{i}") for i in range(RING3)]
        s_xt, s_xc, s_h, s_g, s_y, s_ye = (sem(f"s_moe{n}") for n in ("xt", "xc", "h", "g", "y", "ye"))
        HALF = FB // 2
        block = ctx.enter_context(nc.Block())

        def run(eng, first, last, step):
            for n in range(first, RING3):
                step(n, n % RING3, n // RING3)
            rounds = SLOT_TILES // RING3 - 1
            with eng.Fori(1, rounds) as it:
                for r in range(RING3):
                    step(it * RING3 + r, r, it)
            for n in range(rounds * RING3, last + 1):
                step(n, n % RING3, n // RING3)

        def tile_at(n, r, it, ahead):
            if isinstance(n, int) and not 0 <= n + ahead < SLOT_TILES:
                return None
            return n + ahead, (r + ahead) % RING3, it + (r + ahead) // RING3

        def rows_of(n):
            return bass.ds(n * P, P)

        @block.sync
        def _(sp):
            def load_weights(e, i):
                sp.dma_start(w1[i][:, :], a["w1p"][bass.ds(e, 1), :, :].rearrange("a p w -> p (a w)")).then_inc(s_w1[i], 16)

            def step(n, r, it):
                if h := tile_at(n, r, it, 2):
                    m, i, turn = h
                    e = sp.value_load(expert_of[0:1, bass.ds(m, 1)], min_val=0, max_val=E - 1)
                    wait(sp, s_g, 2 * (m - 2))
                    first = isinstance(m, int) and m == 0
                    if first:
                        load_weights(e, i)
                        sp.wait_ge(s_scattered, 16 * TOPK * TT)
                    sp.dma_start(xs[i][:, :], slots_in[rows_of(m), :]).then_inc(s_xs[i], 16)
                    if not first:
                        load_weights(e, i)
            run(sp, -2, SLOT_TILES - 1, step)

        @block.gpsimd
        def _(pool):
            def step(n, r, it):
                if h := tile_at(n, r, it, -1):
                    m, i, turn = h
                    pool.wait_ge(s_ye, m + 1)
                    pool.dma_start(slots_out[rows_of(m), :], ys[i][:, :]).then_inc(s_st[i], 16)
                if h := tile_at(n, r, it, 2):
                    m, i, turn = h
                    e = pool.value_load(expert_of[0:1, bass.ds(m, 1)], min_val=0, max_val=E - 1)
                    pool.dma_start(b2[i][:, :], a["b2"][bass.ds(e, 1), :].broadcast_to([P, D])).then_inc(s_b2[i], 16)
            run(pool, -2, SLOT_TILES, step)
            for i in range(RING3):
                pool.wait_ge(s_st[i], 16 * (SLOT_TILES // RING3))

        @block.tensor
        def _(pe):
            pe.wait_ge(s_w2, 16 * E)

            def step(n, r, it):
                if h := tile_at(n, r, it, 1):
                    m, i, turn = h
                    pe.wait_ge(s_xs[i], 16 * (turn + 1))
                    wait(pe, s_xc, m)
                    for dk in range(DK):
                        tr = nc.tensor.transpose(px[:, dk * P:(dk + 1) * P], xs[i][:, dk * P:(dk + 1) * P], ident[:, :])
                    tr.then_inc(s_xt, 1)
                if h := tile_at(n, r, it, 0):
                    m, i, turn = h
                    pe.wait_ge(s_xc, m + 1)
                    pe.wait_ge(s_w1[i], 16 * (turn + 1))
                    for half in range(2):
                        wait(pe, s_g, 2 * (m - 1) + half + 1)
                        for q in range(HALF):
                            f = half * HALF + q
                            for dk in range(DK):
                                mm = nc.tensor.matmul(ph[half][:, q * P:(q + 1) * P],
                                                      w1[i][:, dk * F + f * P:dk * F + (f + 1) * P], xT[i][:, dk, :],
                                                      start=(dk == 0), stop=(dk == DK - 1))
                        mm.then_inc(s_h, 1)
                if h := tile_at(n, r, it, -1):
                    m, i, turn = h
                    e = pe.value_load(expert_of[0:1, bass.ds(m, 1)], min_val=0, max_val=E - 1)
                    pe.wait_ge(s_g, 2 * (m + 1))
                    wait(pe, s_ye, m)
                    for f in range(FB):
                        mm = nc.tensor.matmul(py[:, 0:D], hT[i][:, f, :],
                                              w2[:, bass.ds(e, 1), f * D:(f + 1) * D].rearrange("p a d -> p (a d)"),
                                              start=(f == 0), stop=(f == FB - 1))
                    mm.then_inc(s_y, 1)
            run(pe, -1, SLOT_TILES, step)

        @block.scalar
        def _(act):
            def step(n, r, it):
                if h := tile_at(n, r, it, 0):
                    m, i, turn = h
                    wait(act, s_y, m - 2)
                    for half in range(2):
                        act.wait_ge(s_h, 2 * m + half + 1)
                        for q in range(HALF):
                            f = half * HALF + q
                            g = nc.scalar.activation(hT[i][:, f, :], ph[half][:, q * P:(q + 1) * P], ACT.Gelu,
                                                     bias=w1[i][:, DK * F + f:DK * F + f + 1])
                        g.then_inc(s_g, 1)
            run(act, 0, SLOT_TILES - 1, step)

        @block.vector
        def _(dve):
            def step(n, r, it):
                if h := tile_at(n, r, it, 1):
                    m, i, turn = h
                    dve.wait_ge(s_xt, m + 1)
                    wait(dve, s_h, 2 * (m - 2))
                    nc.vector.tensor_copy(xT[i][:, :, :].rearrange("p k t -> p (k t)"), px[:, 0:D]).then_inc(s_xc, 1)
                if h := tile_at(n, r, it, -1):
                    m, i, turn = h
                    dve.wait_ge(s_y, m + 1)
                    if not isinstance(m, int) or m >= RING3:
                        dve.wait_ge(s_st[i], 16 * turn)
                    dve.wait_ge(s_b2[i], 16 * (turn + 1))
                    nc.vector.tensor_tensor(ys[i][:, :], py[:, 0:D], b2[i][:, :], ALU.add).then_inc(s_ye, 1)
            run(dve, -1, SLOT_TILES, step)


def combine(nc, sem, sb, x, prob, slot_of, slots_out, ln, q_proj):
    with ExitStack() as ctx:
        got = sb(ctx, "got", [P, TT, TOPK, D])
        s_got = [sem(f"s_got{i}") for i in range(TT)]
        s_x = sem("s_combined")
        block = ctx.enter_context(nc.Block())

        @block.sync
        def _(sp):
            q_proj.load(sp)
            for g in range(q_proj.PARTS):
                q_proj.store(sp, g)
            q_proj.stored(sp)

        @block.gpsimd
        def _(pool):
            for t in range(TT):
                for k in range(TOPK):
                    c = k * TT + t
                    pool.indirect_dma_start(got[:, t, k, :], None, slots_out[:, :],
                                            bass.IndirectOffsetOnAxis(slot_of[:, c:c + 1], 0)).then_inc(s_got[t], 16)

        @block.vector
        def _(dve):
            def split(b):
                for eh in range(DK):
                    q_proj.split(dve, DK * b + eh)

            for b in range(B):
                for t in range(b * NI, (b + 1) * NI):
                    dve.wait_ge(s_got[t], 16 * TOPK)
                    for k in range(TOPK):
                        wait(dve, s_x, TOPK * t + k)
                        nc.vector.scalar_tensor_tensor(out=x[:, t, :], in0=got[:, t, k, :], scalar=prob[:, k, t:t + 1],
                                                       in1=x[:, t, :], op0=ALU.mult, op1=ALU.add).then_inc(s_x, 1)
                    dve.wait_ge(s_x, TOPK * (t + 1))
                    ln.stats(dve, t)
                ln.norm(dve, b)
                ln.shifts(dve, b)
                if b >= 2:
                    split(b - 2)
            split(B - 2)
            split(B - 1)

        @block.tensor
        def _(pe):
            for b in range(B):
                ln.turn(pe, b)
                pe.wait_ge(ln.s_ev, DK * (b + 1))
                for eh in range(DK):
                    q_proj.product(pe, DK * b + eh)

        @block.scalar
        def _(act):
            def copies(b):
                for eh in range(DK):
                    q_proj.copies(act, DK * b + eh)

            for b in range(B):
                ln.root(act, b)
                ln.apply(act, b)
                ln.copy(act, b)
                if b >= 1:
                    copies(b - 1)
            copies(B - 1)


class TernaryWeights:

    def __init__(self, nc, a, ctx, sem, sb, banks, spare):
        self.nc, self.a, self.sem, self.sb, self.banks, self.spare = nc, a, sem, sb, banks, spare
        self.q = [sb(ctx, f"wq{n}", [P, 2 * F], BF16) for n in range(3)]
        self.ws = sb(ctx, "ws", [P, 3])

    def begin(self, ctx):
        sem, sb = self.sem, self.sb
        self.w = [self.spare[:, 0, :], self.spare[:, 1, :], sb(ctx, "wf2", [P, 2 * F])]
        self.asum = sb(ctx, "asum", [P, 3])
        self.scale = sb(ctx, "wscale", [P, 3])
        self.ones = sb(ctx, "onesPP", [P, P])
        self.pm = self.banks(ctx, "pm", 1)[0]
        self.s_w = [sem(f"s_fw{n}") for n in range(3)]
        self.s_one, self.s_sum, self.s_mm, self.s_sc, self.s_q = (sem(f"s_f{n}") for n in ("one", "sum", "mm", "sc", "q"))

    def load(self, sp, n):
        free = F if n < 2 else D
        sp.dma_start(self.w[n][:, :].rearrange("p (k f) -> p k f", f=free),
                     self.a[("gateT", "upT", "downT")[n]].rearrange("(k p) f -> p k f", p=P)).then_inc(self.s_w[n], 16)

    def clear(self, dve):
        self.nc.vector.memset(self.ones[:, :], 1.0).then_inc(self.s_one, 1)

    def magnitudes(self, dve, n):
        dve.wait_ge(self.s_w[n], 16)
        self.nc.vector.tensor_reduce(self.asum[:, n:n + 1], self.w[n][:, :], AX.X, ALU.add,
                                     apply_absolute_value=True).then_inc(self.s_sum, 1)

    def total(self, pe):
        pe.wait_ge(self.s_one, 1)
        pe.wait_ge(self.s_sum, 3)
        self.nc.tensor.matmul(self.pm[:, 0:3], self.ones[:, :], self.asum[:, :], start=True, stop=True).then_inc(self.s_mm, 1)

    def scales(self, dve):
        dve.wait_ge(self.s_mm, 1)
        self.nc.vector.tensor_scalar(self.ws[:, :], self.pm[:, 0:3], 1.0 / (F * D), 1e-5, ALU.mult, ALU.max).then_inc(self.s_sc, 1)
        dve.wait_ge(self.s_sc, 1)
        self.nc.vector.reciprocal(self.scale[:, :], self.ws[:, :]).then_inc(self.s_sc, 1)

    def round(self, dve, n, stage):
        w, q = self.w[n][:, :], self.q[n][:, :]
        if stage == 0:
            dve.wait_ge(self.s_sc, 2)
            self.nc.vector.tensor_scalar(w, w, self.scale[:, n:n + 1], MAGIC, ALU.mult, ALU.add).then_inc(self.s_q, 1)
        elif stage == 1:
            dve.wait_ge(self.s_q, 3 * n + 1)
            self.nc.vector.tensor_scalar(w, w, MAGIC, 1.0, ALU.subtract, ALU.min).then_inc(self.s_q, 1)
        else:
            dve.wait_ge(self.s_q, 3 * n + 2)
            self.nc.vector.tensor_scalar(q, w, -1.0, None, ALU.max).then_inc(self.s_q, 1)


def ffn(nc, sem, sb, banks, x, identb, weights, tokens, out):
    wq, ws = weights.q, weights.ws
    xqT, gs, us = tokens.xqT, tokens.gs, tokens.us
    with ExitStack() as ctx:
        gq = wq[0][:, :].rearrange("p (k f) -> p k f", f=F)
        uq = wq[1][:, :].rearrange("p (k f) -> p k f", f=F)
        dq = wq[2][:, :].rearrange("p (k d) -> p k d", d=D)
        ys = sb(ctx, "ys", [P, TT])
        g = [sb(ctx, f"g{i}", [P, F]) for i in range(2)]
        hh = [sb(ctx, f"hh{i}", [P, F]) for i in range(2)]
        hr = [sb(ctx, f"hr{i}", [P, F]) for i in range(2)]
        hq = [sb(ctx, f"hq{i}", [P, F], BF16) for i in range(2)]
        minus_magic = sb(ctx, "minus_magic", [P, 1])
        hqT = [sb(ctx, f"hqT{i}", [P, F], BF16) for i in range(2)]
        y = [sb(ctx, f"y{i}", [P, D]) for i in range(2)]
        ha = sb(ctx, "ha", [P, TT])
        hm = sb(ctx, "hm", [P, TT])
        hs = sb(ctx, "hs", [P, TT])
        pg = banks(ctx, "pg", 2)
        pu = banks(ctx, "pu", 2)
        ptx = [ctx.enter_context(nc.psum_tensor(f"ptx{i}", [P, F], BF16)) for i in range(2)]
        py = banks(ctx, "pfy", 2)
        s_g, s_u, s_si, s_h, s_ha, s_hs, s_hr, s_hq, s_ht, s_he, s_y, s_o = (
            sem(f"s_h{n}") for n in ("g", "u", "si", "h", "ha", "hs", "hr", "hq", "ht", "he", "y", "o"))
        s_mag = sem("s_hmag")
        s_st = [sem(f"s_st{i}") for i in range(2)]
        block = ctx.enter_context(nc.Block())
        out_v = out.rearrange("b (i p) d -> (b i) p d", p=P)

        def finish(dve, t):
            i = t % 2
            dve.wait_ge(s_y, t + 1)
            if t >= 2:
                dve.wait_ge(s_st[i], 16 * (t // 2))
            nc.vector.scalar_tensor_tensor(out=y[i][:, :], in0=py[i][:, 0:D], scalar=ys[:, t:t + 1], in1=x[:, t, :],
                                           op0=ALU.mult, op1=ALU.add).then_inc(s_o, 1)

        @block.vector
        def _(dve):
            nc.vector.memset(minus_magic[:, :], -MAGIC).then_inc(s_mag, 1)
            for t in range(TT):
                i = t % 2
                wait(dve, s_hr, t - 1)
                for n in range(2):
                    c = slice(n * 512, (n + 1) * 512)
                    dve.wait_ge(s_si, 2 * t + n + 1)
                    dve.wait_ge(s_u, 2 * t + n + 1)
                    nc.vector.tensor_tensor(hh[i][:, c], pu[n][:, :], g[i][:, c], ALU.mult).then_inc(s_h, 1)
                dve.wait_ge(s_h, 2 * (t + 1))
                nc.vector.tensor_reduce(ha[:, t:t + 1], hh[i][:, :], AX.X, ALU.max, apply_absolute_value=True).then_inc(s_ha, 1)
                dve.wait_ge(s_ha, t + 1)
                nc.vector.tensor_scalar(hm[:, t:t + 1], ha[:, t:t + 1], us[:, t:t + 1], 1e-5, ALU.mult, ALU.max).then_inc(s_hs, 1)
                dve.wait_ge(s_hs, 4 * t + 1)
                nc.vector.reciprocal(ha[:, t:t + 1], hm[:, t:t + 1]).then_inc(s_hs, 1)
                nc.vector.tensor_scalar(ys[:, t:t + 1], hm[:, t:t + 1], ws[:, 2:3], 1.0 / 127, ALU.mult, ALU.mult).then_inc(s_hs, 1)
                dve.wait_ge(s_hs, 4 * t + 2)
                nc.vector.tensor_scalar(hs[:, t:t + 1], ha[:, t:t + 1], 127.0, us[:, t:t + 1], ALU.mult, ALU.mult).then_inc(s_hs, 1)
                if t >= 2:
                    finish(dve, t - 2)
            finish(dve, TT - 2)
            finish(dve, TT - 1)

        @block.gpsimd
        def _(pool):
            for t in range(TT):
                pool.wait_ge(s_hs, 4 * (t + 1))
                wait(pool, s_hq, t - 1)
                nc.gpsimd.tensor_scalar(hr[t % 2][:, :], hh[t % 2][:, :], hs[:, t:t + 1], MAGIC, ALU.mult, ALU.add).then_inc(s_hr, 1)

        @block.sync
        def _(sp):
            for t in range(TT):
                sp.wait_ge(s_o, t + 1)
                sp.dma_start(out_v[t], y[t % 2][:, :]).then_inc(s_st[t % 2], 16)
            for i in range(2):
                sp.wait_ge(s_st[i], 16 * TT // 2)

        @block.tensor
        def _(pe):
            def gate_up(t):
                for n in range(2):
                    wait(pe, s_si, 2 * (t - 1) + n + 1)
                    for dk in range(DK):
                        mm = nc.tensor.matmul(pg[n][:, :], xqT[:, dk, t * P:(t + 1) * P], gq[:, dk, n * 512:(n + 1) * 512],
                                              start=(dk == 0), stop=(dk == DK - 1))
                    mm.then_inc(s_g, 1)
                    wait(pe, s_h, 2 * (t - 1) + n + 1)
                    for dk in range(DK):
                        mm = nc.tensor.matmul(pu[n][:, :], xqT[:, dk, t * P:(t + 1) * P], uq[:, dk, n * 512:(n + 1) * 512],
                                              start=(dk == 0), stop=(dk == DK - 1))
                    mm.then_inc(s_u, 1)

            def hidden_turned(t):
                i = t % 2
                pe.wait_ge(s_hq, t + 1)
                wait(pe, s_he, t - 1)
                for f in range(FB):
                    tr = nc.tensor.transpose(ptx[i][:, f * P:(f + 1) * P], hq[i][:, f * P:(f + 1) * P], identb[:, :])
                tr.then_inc(s_ht, 1)

            def down(t):
                i = t % 2
                pe.wait_ge(s_he, t + 1)
                wait(pe, s_o, t - 1)
                for f in range(FB):
                    mm = nc.tensor.matmul(py[i][:, 0:D], hqT[i][:, f * P:(f + 1) * P], dq[:, f, :],
                                          start=(f == 0), stop=(f == FB - 1))
                mm.then_inc(s_y, 1)

            gate_up(0)
            for t in range(TT + 2):
                if t + 1 < TT:
                    gate_up(t + 1)
                if t >= 2:
                    down(t - 2)
                if 1 <= t <= TT:
                    hidden_turned(t - 1)

        @block.scalar
        def _(act):
            def hidden_out(t):
                act.wait_ge(s_ht, t + 1)
                wait(act, s_y, t - 1)
                nc.scalar.copy(hqT[t % 2][:, :], ptx[t % 2][:, :]).then_inc(s_he, 1)

            def integers(t):
                act.wait_ge(s_hr, t + 1)
                wait(act, s_ht, t - 1)
                nc.scalar.activation(hq[t % 2][:, :], hr[t % 2][:, :], ACT.Identity, bias=minus_magic[:, :]).then_inc(s_hq, 1)

            act.wait_ge(s_mag, 1)
            for t in range(TT + 2):
                if t < TT:
                    wait(act, s_h, 2 * (t - 1))
                    for n in range(2):
                        act.wait_ge(s_g, 2 * t + n + 1)
                        nc.scalar.activation(g[t % 2][:, n * 512:(n + 1) * 512], pg[n][:, :], ACT.Silu,
                                             scale=gs[:, t:t + 1]).then_inc(s_si, 1)
                if t >= 2:
                    hidden_out(t - 2)
                if 1 <= t <= TT:
                    integers(t - 1)


def kernel(**inputs):
    import numpy as np
    import concourse.bacc as bacc
    from concourse.bass_utils import run_bass_kernel_spmd

    g = {n: np.asarray(v) for n, v in inputs.items()}
    t = lambda v: np.ascontiguousarray(np.swapaxes(v, -1, -2))
    cols = lambda v: np.ascontiguousarray(np.swapaxes(v.reshape(*v.shape[:-1], -1, P), -1, -2))
    by_partition = lambda v: np.ascontiguousarray(np.swapaxes(v.reshape(E, -1, P, v.shape[-1]), 1, 2).reshape(E, P, -1))
    arrays = {
        "x": g["x"],
        "ctxT": t(g["ctx_1024"].reshape(TOK, D)),
        "mask": g["mask_1x1xSxS2_ik0"], "maskT": t(g["mask_1x1xSxS2_ik0"]),
        "above": np.triu(np.ones((P, P), np.float32), 1),
        "ident": np.eye(P, dtype=np.float32),
        "iota": np.ascontiguousarray(np.broadcast_to(np.arange(E, dtype=np.float32), (P, E))),
        "L0_WqT": t(g["L0_xattn_Wq"]), "L0_WkT": t(g["L0_xattn_Wk"]), "L0_WvT": t(g["L0_xattn_Wv"]),
        "L0_bq": cols(g["L0_xattn_bq"]), "L0_bk": cols(g["L0_xattn_bk"]), "L0_bv": g["L0_xattn_bv"],
        "ErT": t(g["L0_xattn_Er"]),
        "routerT": t(g["L0_ffn_router_w"]),
        "w1p": np.ascontiguousarray(np.concatenate([by_partition(t(g["L0_ffn_w1"])), cols(g["L0_ffn_b1"])], axis=-1)),
        "w2p": by_partition(t(g["L0_ffn_w2"])), "b2": g["L0_ffn_b2"],
        "tile_no": np.ascontiguousarray(np.broadcast_to(np.arange(SLOT_TILES, dtype=np.float32), (P, SLOT_TILES))),
        "same": np.tile(np.eye(E, dtype=np.float32), (TT, 1)),
        "prior": np.ascontiguousarray(np.kron(np.triu(np.ones((TOPK * TT,) * 2, np.float32), 1), np.eye(E, dtype=np.float32))
                                      .reshape(TOPK, P, TOPK * P).swapaxes(0, 1)),
        "L1_WqT": t(g["L1_xattn_w_q"]), "L1_WkT": t(g["L1_xattn_w_k"]), "L1_WvT": t(g["L1_xattn_w_v"]),
        "L1_WoT": t(g["L1_xattn_w_o"]),
        "gateT": t(g["L1_ffn_w_gate"]), "upT": t(g["L1_ffn_w_up"]), "downT": t(g["L1_ffn_w_down"]),
    }
    nc = bacc.Bacc("TRN2", target_bir_lowering=False, num_devices=1)
    aps = {n: nc.dram_tensor(f"in_{n}", v.shape, mybir.dt.from_np(v.dtype), kind="ExternalInput").ap()
           for n, v in arrays.items()}
    out = nc.dram_tensor("out", (B, S, D), F32, kind="ExternalOutput").ap()
    build(nc, aps, out)
    r = run_bass_kernel_spmd(nc, [{f"in_{n}": v for n, v in arrays.items()}], core_ids=[0])
    return r.results[0]["out"]
```
